# Optimizing a Trainium2 kernel written in Bass

```python
import numpy as np
import jax
import jax.numpy as jnp

def _softmax(x, axis=-1):
    return jax.nn.softmax(x, axis=axis)

def _gelu(x):
    return jax.nn.gelu(x, approximate=True)

def _silu(x):
    return jax.nn.silu(x)

def _sigmoid(x):
    return jax.nn.sigmoid(x)

def _layernorm(x, axis=-1, eps=1e-05):
    m = jnp.mean(x, axis=axis, keepdims=True)
    v = jnp.var(x, axis=axis, keepdims=True)
    return (x - m) / jnp.sqrt(v + eps)

def _scatter_add(tgt, idx, src, axis=0):
    return tgt.at[idx].add(src)

def _segment_sum(src, seg, n):
    return jax.ops.segment_sum(src, seg, n)
kernel_name = 'mk_recurrent_d2_jaxref_r8_3bb092'

def setup_inputs(seed: int=0):
    np.random.seed(seed)
    _w = jnp.asarray

    def _L0_attn_setup():
        import jax, jax.numpy as jnp
        import numpy as np
        key = jax.random.key(seed)
        ks = jax.random.split(key, 4)
        B, S, D = (4, 512, 128)
        scale = 1.0 / np.sqrt(D)
        return {'inputs': jax.random.normal(ks[0], (B, S, D), dtype=jnp.float32), 'Wa': jax.random.normal(ks[1], (D, D), dtype=jnp.float32) * scale, 'ba': jnp.zeros((D,), dtype=jnp.float32), 'Wb': jax.random.normal(ks[2], (D, D), dtype=jnp.float32) * scale, 'bb': jnp.zeros((D,), dtype=jnp.float32), 'Wc': jax.random.normal(ks[3], (D, D), dtype=jnp.float32) * scale, 'bc': jnp.zeros((D,), dtype=jnp.float32)}
    _L0_attn_in = _L0_attn_setup()

    def _L0_ffn_setup():
        import jax, jax.numpy as jnp
        import numpy as np

        def _binarize(w):
            alpha = jax.lax.stop_gradient(jnp.mean(jnp.abs(w), axis=1, keepdims=True))
            bw = alpha * jnp.sign(w)
            return w + jax.lax.stop_gradient(bw - w)
        key = jax.random.key(seed)
        k1, k2, k3, k4, k5 = jax.random.split(key, 5)
        D, H = (128, 512)
        x = jax.random.normal(k1, (64, 196, D), dtype=jnp.float32)
        w1 = jax.random.normal(k2, (H, D), dtype=jnp.float32) * 0.02
        b1 = jax.random.normal(k3, (H,), dtype=jnp.float32) * 0.02
        w2 = jax.random.normal(k4, (D, H), dtype=jnp.float32) * 0.02
        b2 = jax.random.normal(k5, (D,), dtype=jnp.float32) * 0.02
        return {'x': x, 'w1': w1, 'b1': b1, 'w2': w2, 'b2': b2}
    _L0_ffn_in = _L0_ffn_setup()

    def _L1_attn_setup():
        import jax, jax.numpy as jnp
        import numpy as np
        DIM, HEADS, DH, CHUNK, DEPTH = (128, 8, 128, 64, 2)
        BATCH, SEQLEN = (2, 512)
        MAX_LR = 0.01
        EPS = 1e-06

        def _rmsnorm(x, g=None):
            y = x * jax.lax.rsqrt(jnp.mean(x * x, axis=-1, keepdims=True) + EPS)
            return y * g if g is not None else y

        def _mem_mlp(ws, x):
            x = x @ ws[0]
            for w in ws[1:]:
                x = jax.nn.silu(x) @ w
            return x

        def _assoc_scan(gates, x):
            g = jnp.broadcast_to(gates, x.shape)

            def op(a, b):
                ga, xa = a
                gb, xb = b
                return (ga * gb, gb * xa + xb)
            _, y = jax.lax.associative_scan(op, (g, x), axis=3)
            return y
        key = jax.random.key(seed)
        ks = jax.random.split(key, 12)
        b, n, d, h, dh = (BATCH, SEQLEN, DIM, HEADS, DH)
        di = h * dh
        lin = lambda k, i, o: jax.random.normal(k, (i, o), jnp.float32) * np.float32(1.0 / np.sqrt(i))
        return {'seq': jax.random.normal(ks[0], (b, n, d), jnp.float32), 'store_norm_g': jnp.ones((d,), jnp.float32), 'retrieve_norm_g': jnp.ones((d,), jnp.float32), 'w_kv': lin(ks[1], d, 2 * di), 'w_q': lin(ks[2], d, di), 'w_step': lin(ks[3], d, h), 'w_mom': lin(ks[4], d, h), 'w_decay': lin(ks[5], d, h), 'w_gate': lin(ks[6], d, h), 'w_combine': lin(ks[7], di, d), 'mh_gamma': jnp.zeros((h, 1, dh), jnp.float32), 'mem_w0': lin(ks[8], dh, dh), 'mem_w1': lin(ks[9], dh, dh)}
    _L1_attn_in = _L1_attn_setup()

    def _L1_ffn_setup():
        import jax, jax.numpy as jnp
        import numpy as np
        B, S, D, F, E = (8, 128, 128, 512, 8)
        EPS = 1e-05
        key = jax.random.key(seed)
        ks = jax.random.split(key, 4)
        s = 0.02
        return {'input_features': jax.random.normal(ks[0], (B, S, D), jnp.float32), 'centroids': jax.random.normal(ks[1], (E, D), jnp.float32) * 0.1, 'ln_g': jnp.ones((E, D), jnp.float32), 'ln_b': jnp.zeros((E, D), jnp.float32), 'w1': jax.random.normal(ks[2], (E, D, F), jnp.float32) * s, 'b1': jnp.zeros((E, F), jnp.float32), 'w2': jax.random.normal(ks[3], (E, F, D), jnp.float32) * s, 'b2': jnp.zeros((E, D), jnp.float32)}
    _L1_ffn_in = _L1_ffn_setup()
    _d = {'L0_attn_inputs': _L0_attn_in['inputs'], 'L0_attn_Wa': _L0_attn_in['Wa'], 'L0_attn_ba': _L0_attn_in['ba'], 'L0_attn_Wb': _L0_attn_in['Wb'], 'L0_attn_bb': _L0_attn_in['bb'], 'L0_attn_Wc': _L0_attn_in['Wc'], 'L0_attn_bc': _L0_attn_in['bc'], 'L0_ffn_w1': _L0_ffn_in['w1'], 'L0_ffn_b1': _L0_ffn_in['b1'], 'L0_ffn_w2': _L0_ffn_in['w2'], 'L0_ffn_b2': _L0_ffn_in['b2'], 'L1_attn_store_norm_g': _L1_attn_in['store_norm_g'], 'L1_attn_retrieve_norm_g': _L1_attn_in['retrieve_norm_g'], 'L1_attn_w_kv': _L1_attn_in['w_kv'], 'L1_attn_w_q': _L1_attn_in['w_q'], 'L1_attn_w_step': _L1_attn_in['w_step'], 'L1_attn_w_mom': _L1_attn_in['w_mom'], 'L1_attn_w_decay': _L1_attn_in['w_decay'], 'L1_attn_w_gate': _L1_attn_in['w_gate'], 'L1_attn_w_combine': _L1_attn_in['w_combine'], 'L1_attn_mh_gamma': _L1_attn_in['mh_gamma'], 'L1_attn_mem_w0': _L1_attn_in['mem_w0'], 'L1_attn_mem_w1': _L1_attn_in['mem_w1'], 'L1_ffn_centroids': _L1_ffn_in['centroids'], 'L1_ffn_ln_g': _L1_ffn_in['ln_g'], 'L1_ffn_ln_b': _L1_ffn_in['ln_b'], 'L1_ffn_w1': _L1_ffn_in['w1'], 'L1_ffn_b1': _L1_ffn_in['b1'], 'L1_ffn_w2': _L1_ffn_in['w2'], 'L1_ffn_b2': _L1_ffn_in['b2']}
    _x0 = _d['L0_attn_inputs']
    _d['L0_attn_inputs'] = jax.random.normal(jax.random.fold_in(jax.random.key(seed), 1), (8, 512, 128), dtype=_x0.dtype)
    del _x0
    return _d

def reference(L0_attn_inputs, L0_attn_Wa, L0_attn_ba, L0_attn_Wb, L0_attn_bb, L0_attn_Wc, L0_attn_bc, L0_ffn_w1, L0_ffn_b1, L0_ffn_w2, L0_ffn_b2, L1_attn_store_norm_g, L1_attn_retrieve_norm_g, L1_attn_w_kv, L1_attn_w_q, L1_attn_w_step, L1_attn_w_mom, L1_attn_w_decay, L1_attn_w_gate, L1_attn_w_combine, L1_attn_mh_gamma, L1_attn_mem_w0, L1_attn_mem_w1, L1_ffn_centroids, L1_ffn_ln_g, L1_ffn_ln_b, L1_ffn_w1, L1_ffn_b1, L1_ffn_w2, L1_ffn_b2):

    def _L0_attn_ref(inputs, Wa, ba, Wb, bb, Wc, bc):
        import jax, jax.numpy as jnp
        import numpy as np
        a = jax.nn.sigmoid(jnp.einsum('bsd,ed->bse', inputs, Wa) + ba)
        b = jnp.tanh(jnp.einsum('bsd,ed->bse', inputs, Wb) + bb)
        c = jax.nn.sigmoid(jnp.einsum('bsd,ed->bse', inputs, Wc) + bc)
        B, S, D = inputs.shape

        def step(state, abc):
            a_t, b_t, c_t = abc
            state = a_t * state + (1.0 - a_t) * b_t
            return (state, c_t * state)
        abc = (jnp.swapaxes(a, 0, 1), jnp.swapaxes(b, 0, 1), jnp.swapaxes(c, 0, 1))
        init = jnp.zeros((B, D), dtype=inputs.dtype)
        _, ys = jax.lax.scan(step, init, abc)
        return jnp.swapaxes(ys, 0, 1)

    def _L0_ffn_ref(x, w1, b1, w2, b2):
        import jax, jax.numpy as jnp
        import numpy as np

        def _binarize(w):
            alpha = jax.lax.stop_gradient(jnp.mean(jnp.abs(w), axis=1, keepdims=True))
            bw = alpha * jnp.sign(w)
            return w + jax.lax.stop_gradient(bw - w)
        bw1 = _binarize(w1)
        h = jnp.einsum('bsd,hd->bsh', x, bw1) + b1
        h = jax.nn.gelu(h, approximate=False)
        bw2 = _binarize(w2)
        out = jnp.einsum('bsh,dh->bsd', h, bw2) + b2
        return out

    def _L1_attn_ref(seq, store_norm_g, retrieve_norm_g, w_kv, w_q, w_step, w_mom, w_decay, w_gate, w_combine, mh_gamma, mem_w0, mem_w1):
        import jax, jax.numpy as jnp
        import numpy as np
        DIM, HEADS, DH, CHUNK, DEPTH = (128, 8, 128, 64, 2)
        BATCH, SEQLEN = (2, 512)
        MAX_LR = 0.01
        EPS = 1e-06

        def _rmsnorm(x, g=None):
            y = x * jax.lax.rsqrt(jnp.mean(x * x, axis=-1, keepdims=True) + EPS)
            return y * g if g is not None else y

        def _mem_mlp(ws, x):
            x = x @ ws[0]
            for w in ws[1:]:
                x = jax.nn.silu(x) @ w
            return x

        def _assoc_scan(gates, x):
            g = jnp.broadcast_to(gates, x.shape)

            def op(a, b):
                ga, xa = a
                gb, xb = b
                return (ga * gb, gb * xa + xb)
            _, y = jax.lax.associative_scan(op, (g, x), axis=3)
            return y
        b, n, d = seq.shape
        h, dh, c = (HEADS, DH, CHUNK)
        nc = n // c
        mem_ws = (mem_w0, mem_w1)
        ss = _rmsnorm(seq, store_norm_g)
        lr = jax.nn.sigmoid(jnp.einsum('bnd,dh->bhn', ss, w_step)) * MAX_LR
        lr = lr.reshape(b, h, nc, c)
        cmean = ss.reshape(b, nc, c, d).mean(axis=2)
        mom_gate = jax.nn.sigmoid(jnp.einsum('bnd,dh->bhn', cmean, w_mom))
        decay = jax.nn.sigmoid(jnp.einsum('bnd,dh->bhn', cmean, w_decay))
        kv = ss @ w_kv
        keys, values = jnp.split(kv, 2, axis=-1)
        split = lambda t: t.reshape(b, n, h, dh).transpose(0, 2, 1, 3).reshape(b, h, nc, c, dh)
        keys, values = (split(keys), split(values))

        def chunk_loss(ws, k, lrc, v):
            pred = _mem_mlp(ws, k)
            return jnp.sum(jnp.mean((pred - v) ** 2, axis=-1) * lrc)
        flat = lambda t: t.reshape(b * h * nc, c, dh)
        grads = jax.vmap(jax.grad(chunk_loss), in_axes=(None, 0, 0, 0))(mem_ws, flat(keys), lr.reshape(b * h * nc, c), flat(values))
        grads = jnp.stack([g.reshape(b, h, nc, dh, dh) for g in grads])
        surprise = -grads
        gm = mom_gate[None, :, :, :, None, None]
        gd = (1.0 - decay)[None, :, :, :, None, None]
        momentum = _assoc_scan(gm, surprise)
        updates = _assoc_scan(gd, momentum)
        sr = _rmsnorm(seq, retrieve_norm_g)
        sr = jnp.pad(sr[:, c - 1:], ((0, 0), (0, c - 1), (0, 0)))
        q = (sr @ w_q).reshape(b, n, h, dh).transpose(0, 2, 1, 3).reshape(b, h, nc, c, dh)
        w0 = mem_w0 + updates[0]
        w1 = mem_w1 + updates[1]
        x = jnp.einsum('bhncd,bhnde->bhnce', q, w0)
        vals = jnp.einsum('bhncd,bhnde->bhnce', jax.nn.silu(x), w1)
        vals = vals.reshape(b, h, n, dh)
        vals = _rmsnorm(vals) * (mh_gamma + 1.0)
        gate = jax.nn.sigmoid(jnp.einsum('bnd,dh->bhn', sr, w_gate))[..., None]
        vals = vals * gate
        vals = vals.transpose(0, 2, 1, 3).reshape(b, n, h * dh)
        out = vals @ w_combine
        out = jnp.pad(out, ((0, 0), (c - 1, 0), (0, 0)))[:, :n]
        return out

    def _L1_ffn_ref(input_features, centroids, ln_g, ln_b, w1, b1, w2, b2):
        import jax, jax.numpy as jnp
        import numpy as np
        B, S, D, F, E = (8, 128, 128, 512, 8)
        EPS = 1e-05
        x = input_features.reshape(-1, D)
        aff = jax.lax.stop_gradient(x @ centroids.T)
        eid = jnp.argmax(aff, axis=-1)
        alpha = jax.nn.sigmoid(jnp.sum(x * centroids[eid], axis=-1, keepdims=True))
        mu = jnp.mean(x, axis=-1, keepdims=True)
        var = jnp.mean((x - mu) ** 2, axis=-1, keepdims=True)
        xn = (x - mu) * jax.lax.rsqrt(var + EPS)
        xln = xn * ln_g[eid] + ln_b[eid]
        onehot = jax.nn.one_hot(eid, E, dtype=x.dtype)
        ffn = jnp.zeros_like(x)
        for e in range(E):
            h = jax.nn.relu(xln @ w1[e] + b1[e])
            ffn = ffn + onehot[:, e:e + 1] * (h @ w2[e] + b2[e])
        out = x + alpha * ffn
        return out.reshape(input_features.shape)
    x = L0_attn_inputs
    xn = _layernorm(x, axis=-1)
    s = _L0_attn_ref(xn, L0_attn_Wa, L0_attn_ba, L0_attn_Wb, L0_attn_bb, L0_attn_Wc, L0_attn_bc)
    g = _silu(_L0_ffn_ref(xn, L0_ffn_w1, L0_ffn_b1, L0_ffn_w2, L0_ffn_b2))
    x = x + s * g
    xn = _layernorm(x, axis=-1)
    s = _L1_attn_ref(xn, L1_attn_store_norm_g, L1_attn_retrieve_norm_g, L1_attn_w_kv, L1_attn_w_q, L1_attn_w_step, L1_attn_w_mom, L1_attn_w_decay, L1_attn_w_gate, L1_attn_w_combine, L1_attn_mh_gamma, L1_attn_mem_w0, L1_attn_mem_w1)
    g = _silu(_L1_ffn_ref(xn, L1_ffn_centroids, L1_ffn_ln_g, L1_ffn_ln_b, L1_ffn_w1, L1_ffn_b1, L1_ffn_w2, L1_ffn_b2))
    x = x + s * g
    return x

_drawn_inputs = setup_inputs


def setup_inputs(seed=0):
    import zlib

    import numpy as np

    out = dict(_drawn_inputs(seed))
    spreads = {'L0_attn_ba': (0.0, 0.8),
     'L0_attn_bb': (0.0, 0.8),
     'L0_attn_bc': (0.0, 0.8),
     'L1_attn_store_norm_g': (1.0, 0.6),
     'L1_attn_retrieve_norm_g': (1.0, 0.2),
     'L1_attn_mh_gamma': (0.0, 0.274),
     'L1_ffn_ln_g': (1.0, 0.6),
     'L1_ffn_ln_b': (0.0, 0.8),
     'L1_ffn_b1': (0.0, 0.8),
     'L1_ffn_b2': (0.0, 0.311)}
    factors = {'L0_attn_Wa': 8.0,
     'L0_attn_Wb': 8.0,
     'L0_attn_Wc': 8.0,
     'L0_ffn_w1': 8.0,
     'L0_ffn_b1': 8.0,
     'L0_ffn_w2': 8.0,
     'L0_ffn_b2': 8.0,
     'L1_attn_w_kv': 4.761,
     'L1_attn_w_step': 8.0,
     'L1_attn_w_mom': 8.0,
     'L1_attn_w_decay': 8.0,
     'L1_ffn_w1': 3.545,
     'L1_ffn_w2': 2.78}
    for name, (base, spread) in spreads.items():
        noise = np.random.default_rng([zlib.crc32(name.encode()), seed]).standard_normal(out[name].shape)
        drawn = base * np.exp(spread * noise) if base else spread * noise
        out[name] = jnp.asarray(drawn.astype(out[name].dtype))
    for name, factor in factors.items():
        out[name] = (out[name] * factor).astype(out[name].dtype)
    return out
```

```python
from contextlib import ExitStack

import concourse.bass as bass
from concourse import mybir

F32 = mybir.dt.float32
I32 = mybir.dt.int32
U32 = mybir.dt.uint32
ALU = mybir.AluOpType
ACT = mybir.ActivationFunctionType
AX = mybir.AxisListType

P = 128
B, S, D = 8, 512, 128
T = S // P
NT = B * T
HF = 512
FB = HF // P
H = 8
C = 64
NC = S // C
SHIFT = C - 1
E = 8
NB = NT + E
ROW = D + 2
LN_EPS, RMS_EPS, MAX_LR = 1e-5, 1e-6, 0.01

V_BA, V_BB, V_BC, V_B1, V_B2, V_GS, V_GR, V_GAM = 0, 1, 2, 3, 7, 8, 9, 10
V_CENT, V_LNG, V_LNB, V_EB1 = 18, 26, 34, 42
V_ROWS = V_EB1 + E * FB

SC_BANK = [4, 5, 6, 5]
SC_COL = [0, 0, 0, 384]
P_COL = [0, 512, 1024, 896]
SC_ORDER = [0, 1, 3, 2]
SC_BANKS = 3
P_COLS = sum(S - P * i for i in range(T))


class Chain:

    def __init__(self, eng, sem, base=0):
        self.eng, self.sem, self.base, self.n = eng, sem, base, 0

    def __call__(self, ins):
        self.n += 1
        ins.then_inc(self.sem, 1)
        self.eng.wait_ge(self.sem, self.base + self.n)


class At:

    def __init__(self, half, par):
        self.i, self.par, self.half = half * 2 + par, par, half


def less(n, k):
    return max(n - k, 0) if isinstance(n, int) else n - k


def pipelined(eng, step, count, depth):
    at = lambda i: At(i // 2, i % 2) if 0 <= i < count else None
    first, last = 4, count
    last -= last % 2
    for t in range(first):
        step(*[at(t - k) for k in range(depth)])
    with eng.Fori(0, (last - first) // 2) as j:
        for u in range(2):
            ats = []
            for k in range(depth):
                c = first + u - k
                ats.append(At(j + c // 2, c % 2))
            step(*ats)
    for t in range(last, count + depth - 1):
        step(*[at(t - k) for k in range(depth)])


class Mem:
    pass


def prepare(nc, m, a):
    with ExitStack() as ctx:
        sb = lambda n, s, d=F32: ctx.enter_context(nc.sbuf_tensor(n, s, d))
        sem = lambda n: ctx.enter_context(nc.semaphore(n))
        vec = sb("vec", [P, D])
        sq4 = sb("sq4", [P, 4, D])
        mem0 = sb("mem0", [P, D])
        l0w1 = sb("l0w1", [P, FB, D])
        l0w2 = sb("l0w2", [P, HF])
        wkv = sb("wkv", [P, 2 * H * D])
        wq = sb("wq", [P, H * D])
        wcomb = sb("wcomb", [P, H, D])
        small = sb("small", [P, 4, H])
        b2row = sb("b2row", [1, E * D])
        sg1 = sb("sg1", [P, FB, D])
        sg2 = sb("sg2", [P, HF])
        kt = sb("kt", [P, H, D])
        qt = sb("qt", [P, H, D])
        gam1 = sb("gam1", [P, H])
        junk = sb("junk", [P, HF])
        fill = sb("fill", [P, NB, ROW])
        names = ["vec", "sq4", "mem0", "l0w1", "l0w2", "wkv", "wq", "wcomb", "small", "b2row"]
        got = {n: sem(f"got_{n}") for n in names}
        filled = sem("filled")
        consts = sem("consts")
        pool_made = []
        fill_ok = sem("fill_ok")
        signs = sem("signs")
        pe_group = sem("pe_group")
        out_group = sem("out_group")
        scaled = sem("scaled")
        dve_c = sem("dve_c0")
        act_c = sem("act_c0")

        with nc.Block() as block:

            @block.sync
            def _(sp):
                rows = [
                    (V_BA, 1, a["L0_attn_ba"].rearrange("(a n) -> a n", a=1)),
                    (V_BB, 1, a["L0_attn_bb"].rearrange("(a n) -> a n", a=1)),
                    (V_BC, 1, a["L0_attn_bc"].rearrange("(a n) -> a n", a=1)),
                    (V_B1, FB, a["L0_ffn_b1"].rearrange("(a n) -> a n", a=FB)),
                    (V_B2, 1, a["L0_ffn_b2"].rearrange("(a n) -> a n", a=1)),
                    (V_GS, 1, a["L1_attn_store_norm_g"].rearrange("(a n) -> a n", a=1)),
                    (V_GR, 1, a["L1_attn_retrieve_norm_g"].rearrange("(a n) -> a n", a=1)),
                    (V_GAM, H, a["L1_attn_mh_gamma"].rearrange("h a d -> (h a) d")),
                    (V_CENT, E, a["L1_ffn_centroids"]),
                    (V_LNG, E, a["L1_ffn_ln_g"]),
                    (V_LNB, E, a["L1_ffn_ln_b"]),
                    (V_EB1, E * FB, a["L1_ffn_b1"].rearrange("e (k n) -> (e k) n", k=FB)),
                ]
                for r, n, src in rows:
                    sp.dma_start(vec[r:r + n, :], src).then_inc(got["vec"], 16)
                for k, n in enumerate(["L0_attn_Wa", "L0_attn_Wb", "L0_attn_Wc", "L1_attn_mem_w1"]):
                    sp.dma_start(sq4[:, k, :], a[n]).then_inc(got["sq4"], 16)
                sp.dma_start(l0w1[:], a["L0_ffn_w1"].rearrange("(k p) d -> p k d", p=P)).then_inc(got["l0w1"], 16)
                sp.dma_start(l0w2[:], a["L0_ffn_w2"]).then_inc(got["l0w2"], 16)
                sp.wait_ge(fill_ok, 1)
                sp.dma_start(m.sorted_rows.rearrange("(n p) r -> p n r", p=P), fill[:]).then_inc(filled, 16)
                sp.wait_ge(filled, 16)

            @block.scalar
            def _(act):
                act.dma_start(wkv[:], a["L1_attn_w_kv"]).then_inc(got["wkv"], 16)
                act.dma_start(wq[:], a["L1_attn_w_q"]).then_inc(got["wq"], 16)
                act.dma_start(mem0[:], a["L1_attn_mem_w0"]).then_inc(got["mem0"], 16)
                act.dma_start(m.w1n[:], a["L1_attn_mem_w1"]).then_inc(got["mem0"], 16)
                for k, n in enumerate(["step", "mom", "decay", "gate"]):
                    act.dma_start(small[:, k, :], a[f"L1_attn_w_{n}"]).then_inc(got["small"], 16)
                act.dma_start(wcomb[:], a["L1_attn_w_combine"].rearrange("(h e) d -> e h d", e=D)).then_inc(got["wcomb"], 16)
                act.dma_start(b2row[:], a["L1_ffn_b2"].rearrange("(a e) d -> a (e d)", a=1)).then_inc(got["b2row"], 16)
                act.wait_ge(got["l0w1"], 16)
                nc.scalar.activation(sg1[:], l0w1[:], ACT.Sign).then_inc(signs, 1)
                act.wait_ge(got["l0w2"], 16)
                nc.scalar.activation(sg2[:], l0w2[:], ACT.Sign).then_inc(signs, 1)
                chain = Chain(act, act_c)
                for k in range(FB):
                    chain(nc.scalar.activation(junk[:, 0:D], l0w1[:, k, :], ACT.Abs, accum_out=m.alpha1[:, k:k + 1]))
                chain(nc.scalar.activation(junk[:], l0w2[:], ACT.Abs, accum_out=m.alpha2[:]))
                chain(nc.scalar.mul(m.alpha1[:], m.alpha1[:], 1.0 / D))
                chain(nc.scalar.mul(m.alpha2[:], m.alpha2[:], 1.0 / HF))
                chain(nc.scalar.mul(m.alpha2h[:], m.alpha2[:], 0.5))

            @block.gpsimd
            def _(pool):
                chain = Chain(pool, consts)
                chain(nc.gpsimd.memset(m.ident[:], 0.0))
                chain(nc.gpsimd.affine_select(out=m.ident[:], in_=m.ident[:], compare_op=ALU.not_equal, fill=1.0,
                                              base=0, pattern=[[-1, P]], channel_multiplier=1))
                chain(nc.gpsimd.memset(m.ones[:], 1.0))
                chain(nc.gpsimd.memset(m.upper[:], 1.0))
                chain(nc.gpsimd.affine_select(out=m.upper[:], in_=m.upper[:], compare_op=ALU.is_gt, fill=0.0,
                                              base=0, pattern=[[1, P]], channel_multiplier=-1))
                chain(nc.gpsimd.memset(m.neg_half[:], -0.5))
                chain(nc.gpsimd.memset(m.starts[:], 0.0))
                for half in range(2):
                    part = m.starts[C * half:C * half + C]
                    chain(nc.gpsimd.affine_select(out=part, in_=part, compare_op=ALU.not_equal, fill=1.0, base=-half,
                                                  pattern=[[1, NC], [-2, T]], channel_multiplier=0))
                chain(nc.gpsimd.iota(m.rank_i[:], [[0, NT], [-1, E]], base=E, channel_multiplier=0))
                chain(nc.gpsimd.memset(m.restart[:], 1.0))
                chain(nc.gpsimd.memset(m.restart[:, :, 0:1], 0.0))
                chain(nc.gpsimd.iota(m.block_i[:], [[1, NB], [0, E]], base=0, channel_multiplier=0))
                chain(nc.gpsimd.iota(m.token_i[:], [[P, NT]], base=0, channel_multiplier=1))
                chain(nc.gpsimd.memset(fill[:], 0.0))
                chain(nc.gpsimd.iota(fill[:, :, D].bitcast(I32), [[P, NB]], base=B * S, channel_multiplier=1))
                pool.sem_inc(fill_ok, 1)
                for y in m.y_f:
                    chain(nc.gpsimd.memset(y[:, S:], 0.0))
                chain(nc.gpsimd.memset(m.zeros[:], 0.0))
                pool_made.append(chain.n)

            @block.tensor
            def _(pe):
                pe.wait_ge(consts, 3)
                group = 0

                def bank():
                    nonlocal group
                    if group >= 8:
                        pe.wait_ge(out_group, group - 7)
                    group += 1
                    return m.bank[(group - 1) % 8]

                o = bank()
                pe.wait_ge(got["vec"], 12 * 16)
                pe.transpose(o[:, 0:V_ROWS], vec[0:V_ROWS, :], m.ident[0:V_ROWS, 0:V_ROWS]).then_inc(pe_group, 1)
                o = bank()
                pe.wait_ge(got["sq4"], 64)
                for k in range(4):
                    last = pe.transpose(o[:, k * P:k * P + P], sq4[:, k, :], m.ident[:])
                last.then_inc(pe_group, 1)
                o = bank()
                pe.wait_ge(signs, 1)
                for k in range(FB):
                    last = pe.transpose(o[:, k * P:k * P + P], sg1[:, k, :], m.ident[:])
                last.then_inc(pe_group, 1)
                o = bank()
                pe.wait_ge(signs, 2)
                for k in range(FB):
                    last = pe.transpose(o[:, k * P:k * P + P], sg2[:, k * P:k * P + P], m.ident[:])
                last.then_inc(pe_group, 1)
                for which, src in ((1, wkv), (2, wq)):
                    pe.wait_ge(scaled, which)
                    for g in range(2):
                        o = bank()
                        for k in range(4):
                            h = 4 * g + k
                            last = pe.transpose(o[:, k * P:k * P + P], src[:, h * D:h * D + D], m.ident[:])
                        last.then_inc(pe_group, 1)
                pe.wait_ge(got["mem0"], 32)
                pe.wait_ge(out_group, 8)
                for left, right in ((kt, None), (qt, None), (qt, kt)):
                    for g in range(2):
                        o = bank()
                        for k in range(4):
                            h = 4 * g + k
                            rhs = mem0[:] if right is None else right[:, h, :]
                            last = pe.matmul(o[:, k * P:k * P + P], left[:, h, :], rhs, start=True, stop=True)
                        last.then_inc(pe_group, 1)
                pe.wait_ge(got["b2row"], 16)
                for g in range(2):
                    o = bank()
                    pe.matmul(o[:], m.ones[0:1, :], b2row[:, g * 512:g * 512 + 512], start=True, stop=True).then_inc(pe_group, 1)

            @block.vector
            def _(dve):
                group = 0
                chain = Chain(dve, dve_c)

                def out(dst):
                    nonlocal group
                    group += 1
                    dve.wait_ge(pe_group, group)
                    n = dst.free_size()
                    nc.vector.tensor_copy(dst, m.bank[(group - 1) % 8][:, 0:n] if len(dst.shape) == 2 else
                                          m.bank[(group - 1) % 8][:, 0:n].rearrange("p (a b) -> p a b", b=P)).then_inc(out_group, 1)

                def param(v, n=1):
                    return m.cols[:, v:v + n]

                out(m.cols[:, 0:V_ROWS])
                dve.wait_ge(out_group, 1)
                dve.wait_ge(got["wkv"], 16)
                nc.vector.tensor_scalar(wkv[:, 0:H * D], wkv[:, 0:H * D], param(V_GS), None, ALU.mult).then_inc(scaled, 1)
                dve.wait_ge(got["wq"], 16)
                nc.vector.tensor_scalar(wq[:], wq[:], param(V_GR), None, ALU.mult).then_inc(scaled, 1)
                out(m.w4t[:])
                out(m.s1t[:])
                out(m.s2t[:])
                for g in range(2):
                    out(kt[:, 4 * g:4 * g + 4, :])
                for g in range(2):
                    out(qt[:, 4 * g:4 * g + 4, :])
                nc.vector.tensor_scalar(m.w_v[:].rearrange("p h d -> p (h d)"), wkv[:, H * D:], param(V_GS), -1.0,
                                        ALU.mult, ALU.mult).then_inc(scaled, 1)
                chain(nc.vector.tensor_scalar(gam1[:], param(V_GAM, H), 1.0, None, ALU.add))
                dve.wait_ge(got["wcomb"], 16)
                for h in range(H):
                    nc.vector.tensor_scalar(m.w_out[:, h, :], wcomb[:, h, :], gam1[:, h:h + 1], None, ALU.mult).then_inc(scaled, 1)
                chain(nc.vector.tensor_scalar(m.half_b[:, 0:3], param(V_BA, 3), 0.5, None, ALU.mult))
                chain(nc.vector.tensor_scalar(m.half_b[:, 3:4], param(V_B2), 0.5, None, ALU.mult))
                nc.vector.tensor_copy(m.par_e[:, :, 0:1].rearrange("p e a -> p (e a)"), param(V_LNG, E))
                nc.vector.tensor_copy(m.par_e[:, :, 1:2].rearrange("p e a -> p (e a)"), param(V_LNB, E))
                nc.vector.tensor_copy(m.par_e[:, :, 2:], param(V_EB1, E * FB).rearrange("p (e k) -> p e k", k=FB)).then_inc(scaled, 1)
                dve.wait_ge(got["small"], 64)
                nc.vector.tensor_copy(m.w_sm[:, 0:E], param(V_CENT, E)).then_inc(scaled, 1)
                nc.vector.tensor_scalar(m.w_sm[:, E:E + H], small[:, 0, :], param(V_GS), None, ALU.mult).then_inc(scaled, 1)
                nc.vector.tensor_scalar(m.w_sm[:, E + H:E + 2 * H], small[:, 3, :], param(V_GR), None, ALU.mult).then_inc(scaled, 1)
                nc.vector.tensor_scalar(m.w_md[:], small[:, 1:3, :].rearrange("p a h -> p (a h)"), param(V_GS), None, ALU.mult).then_inc(scaled, 1)
                for g in range(2):
                    out(m.w_u[:, 4 * g:4 * g + 4, :])
                for g in range(2):
                    out(m.w_x[:, 4 * g:4 * g + 4, :])
                for g in range(2):
                    out(m.w_qk[:, 4 * g:4 * g + 4, :])
                for g in range(2):
                    out(m.b2_bc[:, 4 * g:4 * g + 4, :])
                dve.wait_ge(consts, pool_made[0])
                nc.vector.tensor_copy(m.rank_f[:], m.rank_i[:]).then_inc(scaled, 1)
                nc.vector.tensor_copy(m.block_f[:], m.block_i[:]).then_inc(scaled, 1)


def layer0(nc, m, a):
    with ExitStack() as ctx:
        sb = lambda n, s, d=F32: ctx.enter_context(nc.sbuf_tensor(n, s, d))
        sem = lambda n: ctx.enter_context(nc.semaphore(n))
        two = lambda n, s: [sb(f"{n}{k}", s) for k in range(2)]
        x0 = two("x0", [P, T, D])
        xn = two("xn", [P, T, D])
        xnf = two("xnf", [P, S])
        th = [sb(f"th{k}", [P, S]) for k in range(3)]
        ga = sb("ga", [P, S])
        nb = sb("nb", [P, S])
        st = sb("st", [P, S])
        hid = sb("hid", [P, FB, S])
        thg = sb("thg", [P, S])
        z = sb("z", [P, S])
        pr = sb("pr", [P, S])
        x1 = two("x1", [P, T, D])
        xn1 = two("xn1", [P, T, D])
        yt = sb("yt", [P, T, D])
        xl = two("xl", [P, T, D])
        bn = sb("bn", [P, T, 6])
        bn1 = sb("bn1", [P, T, 6])
        bn2 = sb("bn2", [P, T, 6])
        mv0, mv1, mv2 = (sb(f"mv{k}", [P, T, 2]) for k in range(3))
        ve0, ve1 = sb("ve0", [P, T]), sb("ve1", [P, T])
        ve2 = sb("ve2", [P, 2, T])
        r0, r1 = sb("r0", [P, T]), sb("r1", [P, T])
        r2 = sb("r2", [P, 2, T])
        cm = sb("cm", [P, NC])
        cmw = sb("cmw", [P, NC, 2 * H])

        s_x0 = [sem(f"s_x0_{k}") for k in range(2)]
        s_keep = [sem(f"s_keep_{k}") for k in range(2)]
        v_var0, v_var1, v_var2 = sem("v_var0"), sem("v_var1"), sem("v_var2")
        g_r0, g_r1, g_r2 = sem("g_r0"), sem("g_r1"), sem("g_r2")
        v_xn = sem("v_xn")
        p_xn, c_xnf = sem("p_xn"), sem("c_xnf")
        p_qkv, c_th = sem("p_qkv"), sem("c_th")
        p_h, c_h = sem("p_h"), sem("c_h")
        p_f, c_thg, v_z = sem("p_f"), sem("c_thg"), sem("v_z")
        v_rec, v_pr, p_pr = sem("v_rec"), sem("v_pr"), sem("p_pr")
        v_x1, v_xn1, v_y = sem("v_x1"), sem("v_xn1"), sem("v_y")
        v_ry = sem("v_ry")
        p_y, c_yf = sem("p_y"), sem("c_yf")
        v_cm, p_sm, p_gt, c_sm = sem("v_cm"), sem("p_sm"), sem("p_gt"), sem("c_sm")
        v_held = sem("v_held")
        c1, c2, c3a, c3b, c3c = sem("c1"), sem("c2"), sem("c3a"), sem("c3b"), sem("c3c")

        with nc.Block() as block:

            @block.sync
            def _(sp):
                def step(b1, b2, b3):
                    if b1 is not None:
                        sp.wait_ge(v_x1, less(b1.i, 1))
                        sp.dma_start(x0[b1.par][:], a["L0_attn_inputs"][b1.i].rearrange("(k p) d -> p k d", p=P)).then_inc(s_x0[b1.par], 16)
                    if b3 is not None:
                        q = b3.par
                        sp.wait_ge(v_y, b3.i + 1)
                        sp.dma_start(m.x1_all[:, bass.ts(b3.i, T), :], x1[q][:]).then_inc(s_keep[q], 16)
                        sp.dma_start(m.xn1_all[:, bass.ts(b3.i, T), :], xn1[q][:]).then_inc(s_keep[q], 16)
                        sp.dma_start(m.xl_all[:, bass.ts(b3.i, T), 0:D], xl[q][:]).then_inc(s_keep[q], 16)
                        sp.wait_ge(c_yf, b3.i + 1)
                        sp.dma_start(m.y_all[:, bass.ts(b3.i, 1), :], m.y_f[q][:]).then_inc(s_keep[q], 16)

                pipelined(sp, step, B, 3)
                for q in range(2):
                    sp.wait_ge(s_keep[q], 64 * B // 2)

            @block.gpsimd
            def _(pool):
                def power(dst, src, n):
                    return nc.gpsimd.tensor_tensor(dst, src, m.neg_half[:, 0:n], ALU.pow)

                def step(b1, b2, b3):
                    if b3 is not None:
                        pool.wait_ge(v_var1, b3.i + 1)
                        power(r1[:], ve1[:], T).then_inc(g_r1, 1)
                    if b1 is not None:
                        pool.wait_ge(v_var0, b1.i + 1)
                        power(r0[:], ve0[:], T).then_inc(g_r0, 1)
                    if b3 is not None:
                        pool.wait_ge(v_var2, b3.i + 1)
                        power(r2[:].rearrange("p a t -> p (a t)"), ve2[:].rearrange("p a t -> p (a t)"), 2 * T).then_inc(g_r2, 1)

                pipelined(pool, step, B, 3)

            @block.tensor
            def _(pe):
                def step(b1, b2, b3):
                    if b3 is not None:
                        pe.wait_ge(v_pr, b3.i + 1)
                        pe.wait_ge(c_sm, b3.i)
                        for k in range(T):
                            last = pe.transpose(m.bank[7][:, k * P:k * P + P], pr[:, k * P:k * P + P], m.ident[:])
                        last.then_inc(p_pr, 1)
                    if b2 is not None:
                        pe.wait_ge(c_xnf, b2.i + 1)
                        pe.wait_ge(c_th, 3 * b2.i)
                        for k in range(3):
                            pe.matmul(m.bank[1 + k][:], m.w4t[:, k, :], xnf[b2.par][:], start=True, stop=True).then_inc(p_qkv, 1)
                        for k in range(FB):
                            pe.wait_ge(c_h, FB * b2.i + (k - 1) if k else FB * b2.i)
                            pe.matmul(m.bank[4 + k % 2][:], m.s1t[:, k, :], xnf[b2.par][:], start=True, stop=True).then_inc(p_h, 1)
                    if b1 is not None:
                        pe.wait_ge(v_xn, b1.i + 1)
                        pe.wait_ge(c_xnf, b1.i)
                        for k in range(T):
                            last = pe.transpose(m.bank[0][:, k * P:k * P + P], xn[b1.par][:, k, :], m.ident[:])
                        last.then_inc(p_xn, 1)
                    if b2 is not None:
                        pe.wait_ge(v_z, b2.i)
                        for k in range(FB):
                            pe.wait_ge(c_h, FB * b2.i + k + 1)
                            last = pe.matmul(m.bank[6][:], m.s2t[:, k, :], hid[:, k, :], start=(k == 0), stop=(k == FB - 1))
                        last.then_inc(p_f, 1)
                    if b3 is not None:
                        pe.wait_ge(v_y, b3.i + 1)
                        for k in range(T):
                            last = pe.transpose(m.bank[7][:, k * P:k * P + P], yt[:, k, :], m.ident[:])
                        last.then_inc(p_y, 1)
                        y = m.y_f[b3.par]
                        pe.wait_ge(c_yf, b3.i + 1)
                        for k in range(T):
                            pe.matmul(m.bank[7][:, 24 * k:24 * k + 16], y[:, k * P:k * P + P], m.w_sm[:, 0:16], start=True, stop=True)
                            last = pe.matmul(m.bank[7][:, 24 * k + 16:24 * k + 24], y[:, SHIFT + k * P:SHIFT + k * P + P],
                                             m.w_sm[:, 16:24], start=True, stop=True)
                        pe.wait_ge(v_cm, b3.i + 1)
                        pe.matmul(m.bank[7][:, 128:256], m.ones[:], cmw[:].rearrange("p c h -> p (c h)"), start=True, stop=True).then_inc(p_gt, 1)

                pipelined(pe, step, B, 3)

            @block.scalar
            def _(act):
                def step(b1, b2, b3):
                    if b2 is not None:
                        act.wait_ge(v_pr, b2.i)
                        for k in range(3):
                            act.wait_ge(p_qkv, 3 * b2.i + k + 1)
                            if k == 1:
                                nc.scalar.activation(th[1][:], m.bank[2][:], ACT.Tanh, bias=m.cols[:, V_BB:V_BB + 1]).then_inc(c_th, 1)
                            else:
                                nc.scalar.activation(th[k][:], m.bank[1 + k][:], ACT.Tanh, bias=m.half_b[:, k:k + 1], scale=0.5).then_inc(c_th, 1)
                        act.wait_ge(p_f, b2.i)
                        for k in range(FB):
                            act.wait_ge(p_h, FB * b2.i + k + 1)
                            nc.scalar.activation(hid[:, k, :], m.bank[4 + k % 2][:], ACT.Gelu, bias=m.cols[:, V_B1 + k:V_B1 + k + 1],
                                                 scale=m.alpha1[:, k:k + 1]).then_inc(c_h, 1)
                    if b1 is not None:
                        act.wait_ge(p_xn, b1.i + 1)
                        nc.scalar.copy(xnf[b1.par][:], m.bank[0][:]).then_inc(c_xnf, 1)
                    if b2 is not None:
                        act.wait_ge(p_f, b2.i + 1)
                        act.wait_ge(v_z, b2.i)
                        nc.scalar.activation(thg[:], m.bank[6][:], ACT.Tanh, bias=m.half_b[:, 3:4], scale=m.alpha2h[:]).then_inc(c_thg, 1)
                    if b3 is not None:
                        y = m.y_f[b3.par]
                        act.wait_ge(p_y, b3.i + 1)
                        act.wait_ge(s_keep[b3.par], 64 * b3.half)
                        act.wait_ge(v_cm, b3.i)
                        nc.scalar.copy(y[:, 0:S], m.bank[7][:]).then_inc(c_yf, 1)
                        act.wait_ge(p_gt, b3.i + 1)
                        sm = m.bank[7][:, 0:96].rearrange("p (k j) -> p k j", j=24)
                        nc.scalar.copy(m.aff[:, bass.ts(b3.i, T), :], sm[:, :, 0:8])
                        nc.scalar.activation(m.lr_th[:, bass.ts(b3.i, T), :], sm[:, :, 8:16], ACT.Tanh, scale=0.5)
                        nc.scalar.activation(m.gate_th[:, bass.ts(b3.i, T), :], sm[:, :, 16:24], ACT.Tanh, scale=0.5)
                        nc.scalar.activation(m.md_th[:, bass.ts(b3.i, NC), :], m.bank[7][:, 128:256].rearrange("p (c h) -> p c h", h=2 * H),
                                             ACT.Tanh, scale=0.5).then_inc(c_sm, 1)

                pipelined(act, step, B, 3)

            @block.vector
            def _(dve):
                def stats(link, src, bn_, mv):
                    for k in range(T):
                        last = nc.vector.bn_stats(bn_[:, k, :], src[:, k, :])
                    link(last)
                    dve.sem_inc(v_held, 1)
                    for k in range(T):
                        last = nc.vector.bn_aggr(mv[:, k, :], bn_[:, k, :])
                    link(last)

                def step(b1, b2, b3):
                    if b3 is not None:
                        q = b3.par
                        link = Chain(dve, c3a, 3 * b3.i)
                        dve.wait_ge(p_pr, b3.i + 1)
                        dve.wait_ge(s_keep[q], 64 * b3.half)
                        link(nc.vector.scalar_tensor_tensor(x1[q][:].rearrange("p k d -> p (k d)"), m.bank[7][:], -0.125,
                                                            x0[q][:].rearrange("p k d -> p (k d)"), ALU.mult, ALU.add))
                        stats(link, x1[q], bn1, mv1)
                        nc.vector.tensor_scalar(ve1[:], mv1[:, :, 1], LN_EPS, None, ALU.add).then_inc(v_var1, 1)
                        nc.vector.nop().then_inc(v_x1, 1)
                    if b1 is not None:
                        q = b1.par
                        link = Chain(dve, c1, 2 * b1.i)
                        dve.wait_ge(s_x0[q], 16 * (b1.half + 1))
                        stats(link, x0[q], bn, mv0)
                        nc.vector.tensor_scalar(ve0[:], mv0[:, :, 1], LN_EPS, None, ALU.add).then_inc(v_var0, 1)
                    if b3 is not None:
                        q = b3.par
                        link = Chain(dve, c3b, 4 * b3.i)
                        dve.wait_ge(g_r1, b3.i + 1)
                        for k in range(T):
                            last = nc.vector.tensor_scalar(xn1[q][:, k, :], x1[q][:, k, :], mv1[:, k, 0:1], r1[:, k:k + 1], ALU.subtract, ALU.mult)
                        link(last)
                        stats(link, xn1[q], bn2, mv2)
                        link(nc.vector.tensor_tensor(ve2[:, 0, :], mv2[:, :, 0], mv2[:, :, 0], ALU.mult))
                        nc.vector.scalar_tensor_tensor(ve2[:, 0, :], ve2[:, 0, :], RMS_EPS, mv2[:, :, 1], ALU.add, ALU.add)
                        nc.vector.tensor_scalar(ve2[:, 1, :], mv2[:, :, 1], LN_EPS, None, ALU.add).then_inc(v_var2, 1)
                    if b1 is not None:
                        q = b1.par
                        dve.wait_ge(g_r0, b1.i + 1)
                        dve.wait_ge(p_xn, less(b1.i, 1))
                        for k in range(T):
                            last = nc.vector.tensor_scalar(xn[q][:, k, :], x0[q][:, k, :], mv0[:, k, 0:1], r0[:, k:k + 1], ALU.subtract, ALU.mult)
                        last.then_inc(v_xn, 1)
                    if b2 is not None:
                        link = Chain(dve, c2, b2.i)
                        dve.wait_ge(c_th, 3 * b2.i + 3)
                        nc.vector.tensor_scalar(ga[:], th[0][:], 0.5, 0.5, ALU.mult, ALU.add)
                        link(nc.vector.scalar_tensor_tensor(nb[:], th[0][:], -1.0, th[1][:], ALU.add, ALU.mult))
                        nc.vector.tensor_tensor_scan(st[:], ga[:], nb[:], 0.0, ALU.mult, ALU.add).then_inc(v_rec, 1)
                    if b3 is not None:
                        q = b3.par
                        dve.wait_ge(g_r2, b3.i + 1)
                        dve.wait_ge(p_y, b3.i)
                        nc.vector.tensor_copy(m.ry[:, bass.ts(b3.i, T)], r2[:, 0, :]).then_inc(v_ry, 1)
                        for k in range(T):
                            nc.vector.tensor_scalar(xl[q][:, k, :], xn1[q][:, k, :], mv2[:, k, 0:1], r2[:, 1, k:k + 1], ALU.subtract, ALU.mult)
                            last = nc.vector.tensor_scalar(yt[:, k, :], xn1[q][:, k, :], r2[:, 0, k:k + 1], None, ALU.mult)
                        last.then_inc(v_y, 1)
                    if b2 is not None:
                        link = Chain(dve, c3c, 3 * b2.i)
                        dve.wait_ge(c_thg, b2.i + 1)
                        link(nc.vector.tensor_scalar(z[:], m.bank[6][:], m.alpha2[:], m.cols[:, V_B2:V_B2 + 1], ALU.mult, ALU.add))
                        link(nc.vector.scalar_tensor_tensor(z[:], thg[:], 1.0, z[:], ALU.add, ALU.mult))
                        nc.vector.nop().then_inc(v_z, 1)
                        dve.wait_ge(v_rec, b2.i + 1)
                        link(nc.vector.scalar_tensor_tensor(st[:], th[2][:], 1.0, st[:], ALU.add, ALU.mult))
                        dve.wait_ge(p_pr, b2.i)
                        nc.vector.tensor_tensor(pr[:], st[:], z[:], ALU.mult).then_inc(v_pr, 1)
                    if b3 is not None:
                        y = m.y_f[b3.par]
                        dve.wait_ge(c_yf, b3.i + 1)
                        nc.vector.tensor_reduce(cm[:], y[:, 0:S].rearrange("p (c n) -> p c n", n=C), AX.X, ALU.add).then_inc(v_ry, 1)
                        dve.wait_ge(v_ry, 2 * b3.i + 2)
                        nc.vector.scalar_tensor_tensor(cmw[:], cm[:].unsqueeze(2).broadcast_to([P, NC, 2 * H]), 1.0 / C,
                                                       m.w_md[:].unsqueeze(1).broadcast_to([P, NC, 2 * H]), ALU.mult, ALU.mult).then_inc(v_cm, 1)

                pipelined(dve, step, B, 3)


def routing(nc, m):
    with ExitStack() as ctx:
        sb = lambda n, s, d=F32: ctx.enter_context(nc.sbuf_tensor(n, s, d))
        sem = lambda n: ctx.enter_context(nc.semaphore(n))
        mom = sb("mom", [P, B, H, T])
        upd = sb("upd", [P, B, H, T])
        gates = sb("gates", [P, B * NC, 2 * H])
        lr = sb("lr", [P, NT, H])
        top = sb("top", [P, NT])
        oh = sb("oh", [P, NT, E])
        t1 = sb("t1", [P, NT, E])
        best = sb("best", [P, NT])
        cnt = sb("cnt", [P, E, NT])
        run = sb("run", [P, E, NT])
        nblk = sb("nblk", [P, E])
        nblk_i = sb("nblk_i", [P, E], I32)
        endb = sb("endb", [P, E])
        cmp = sb("cmp", [P, NB, E])
        be = sb("be", [P, NB])
        pos = sb("pos", [P, NT])
        d_c, v_oh, p_cnt, v_z = sem("d_c"), sem("v_oh"), sem("p_cnt"), sem("v_zz")
        a_th = sem("a_th")

        with nc.Block() as block:

            @block.tensor
            def _(pe):
                pe.wait_ge(v_oh, 1)
                flat = oh[:].rearrange("p n e -> p (n e)")
                pe.matmul(m.bank[0][:, 0:NT * E], m.upper[:], flat, start=True, stop=True)
                pe.matmul(m.bank[1][:, 0:NT * E], m.ones[:], flat, start=True, stop=True).then_inc(p_cnt, 1)

            @block.scalar
            def _(act):
                act.wait_ge(v_z, 1)
                nc.scalar.activation(best[:], top[:], ACT.Tanh, scale=0.5).then_inc(a_th, 1)

            @block.vector
            def _(dve):
                link = Chain(dve, d_c)
                bc = lambda ap: ap.unsqueeze(2).broadcast_to([P, NT, E])
                link(nc.vector.tensor_reduce(top[:], m.aff[:], AX.X, ALU.max))
                link(nc.vector.tensor_tensor(oh[:], m.aff[:], bc(top[:]), ALU.is_equal))
                link(nc.vector.tensor_tensor(oh[:], oh[:], m.rank_f[:], ALU.mult))
                link(nc.vector.tensor_reduce(best[:], oh[:], AX.X, ALU.max))
                link(nc.vector.tensor_tensor(oh[:], m.rank_f[:], bc(best[:]), ALU.is_equal))
                nc.vector.nop().then_inc(v_oh, 1)
                link(nc.vector.reciprocal(pos[:], m.ry[:]))
                link(nc.vector.tensor_tensor(top[:], top[:], pos[:], ALU.mult))
                nc.vector.nop().then_inc(v_z, 1)
                dve.wait_ge(p_cnt, 1)
                link(nc.vector.tensor_copy(cnt[:], m.bank[1][:, 0:NT * E].rearrange("p (n e) -> p e n", e=E)))
                link(nc.vector.tensor_tensor_scan(run[:].rearrange("p e n -> p (e n)"), m.restart[:].rearrange("p e n -> p (e n)"),
                                                  cnt[:].rearrange("p e n -> p (e n)"), 0.0, ALU.mult, ALU.add))
                link(nc.vector.tensor_scalar(nblk_i[:], run[:, :, NT - 1], float(P - 1), None, ALU.add))
                link(nc.vector.tensor_scalar(nblk_i[:], nblk_i[:], 7, None, ALU.arith_shift_right))
                link(nc.vector.tensor_copy(nblk[:], nblk_i[:]))
                link(nc.vector.tensor_tensor_scan(endb[:], m.ones[:, 0:E], nblk[:], 0.0, ALU.mult, ALU.add))
                link(nc.vector.tensor_tensor(cmp[:], m.block_f[:], endb[:].unsqueeze(1).broadcast_to([P, NB, E]), ALU.is_ge))
                link(nc.vector.tensor_reduce(be[:], cmp[:], AX.X, ALU.add))
                link(nc.vector.tensor_scalar(m.blk_e[:], be[:], float(E - 1), None, ALU.min))
                link(nc.vector.tensor_tensor(nblk[:], endb[:], nblk[:], ALU.subtract))
                link(nc.vector.tensor_tensor(run[:], run[:], cnt[:], ALU.subtract))
                link(nc.vector.scalar_tensor_tensor(run[:], nblk[:].unsqueeze(2).broadcast_to([P, E, NT]), float(P), run[:], ALU.mult, ALU.add))
                link(nc.vector.tensor_tensor(t1[:], m.bank[0][:, 0:NT * E].rearrange("p (n e) -> p n e", e=E),
                                             run[:].rearrange("p e n -> p n e"), ALU.add))
                link(nc.vector.tensor_tensor(t1[:], t1[:], oh[:], ALU.mult))
                link(nc.vector.tensor_reduce(pos[:], t1[:], AX.X, ALU.add))
                link(nc.vector.tensor_copy(m.place[:], pos[:]))
                dve.wait_ge(a_th, 1)
                link(nc.vector.tensor_scalar(m.xl_all[:, :, D + 1], best[:], 0.5, 0.5, ALU.mult, ALU.add))
                link(nc.vector.tensor_copy(m.xl_all[:, :, D].bitcast(I32), m.token_i[:]))
                link(nc.vector.tensor_scalar(gates[:, :, 0:H], m.md_th[:, :, 0:H], 0.5, 0.5, ALU.mult, ALU.add))
                link(nc.vector.tensor_scalar(gates[:, :, H:], m.md_th[:, :, H:], -0.5, 0.5, ALU.mult, ALU.add))
                link(nc.vector.tensor_scalar(m.gate_th[:], m.gate_th[:], 0.5, 0.5, ALU.mult, ALU.add))
                k = -MAX_LR / D
                link(nc.vector.tensor_scalar(lr[:], m.lr_th[:], k, k, ALU.mult, ALU.add))
                link(nc.vector.memset(mom[:], 0.0))
                link(nc.vector.memset(upd[:], 0.0))
                g4 = gates[:].rearrange("p (b c) h -> p b c h", b=B)
                w4 = m.coef[:].rearrange("p b h (i c) -> p b h i c", i=T)
                for c in range(NC):
                    gm = g4[:, :, c, 0:H].unsqueeze(3).broadcast_to([P, B, H, T])
                    gd = g4[:, :, c, H:].unsqueeze(3).broadcast_to([P, B, H, T])
                    ind = m.starts[:, c, :].unsqueeze(1).broadcast_to([P, B * H, T])
                    m3 = mom[:].rearrange("p b h i -> p (b h) i")
                    link(nc.vector.tensor_tensor(mom[:], mom[:], gm, ALU.mult))
                    link(nc.vector.tensor_tensor(m3, m3, ind, ALU.add))
                    link(nc.vector.tensor_tensor(upd[:], upd[:], gd, ALU.mult))
                    link(nc.vector.tensor_tensor(upd[:], upd[:], mom[:], ALU.add))
                    link(nc.vector.tensor_copy(w4[:, :, :, :, c].rearrange("p b h i -> p (b h) i"), upd[:].rearrange("p b h i -> p (b h) i")))
                for b in range(B):
                    for i in range(T):
                        w = m.coef[:, b, :, i * NC:i * NC + NC]
                        link(nc.vector.tensor_tensor(w, w, lr[:, b * T + i, :].unsqueeze(2).broadcast_to([P, H, NC]), ALU.mult))


def memory_attention(nc, m):
    with ExitStack() as ctx:
        sb = lambda n, s, d=F32: ctx.enter_context(nc.sbuf_tensor(n, s, d))
        sem = lambda n: ctx.enter_context(nc.semaphore(n))
        yb = sb("yb", [P, S + SHIFT])
        cf = sb("cf", [P, H, T * NC])
        s_sb = [sb(f"s_sb{k}", [P, S]) for k in range(2)]
        th = sb("thu", [P, S])
        q_sb = sb("q_sb", [P, S])
        qa = sb("qa", [P, S])
        err = sb("err", [P, S])
        err_t = sb("err_t", [P, T, D])
        du = sb("du", [P, S])
        du_t = sb("du_t", [P, T, D])
        p_sb = sb("p_sb", [P, P_COLS])
        xs = sb("xs", [P, S])
        vals = sb("vals", [P, S])
        sq = sb("sq", [P, S])
        ms = sb("ms", [P, T])
        rs = sb("rs", [P, T])
        rg = sb("rg", [P, T])
        acc = sb("acc", [P, T, D])
        U, QA, EB, XB, VB = m.bank[0], m.bank[1], m.bank[2], m.bank[3], m.bank[7]

        p_u, p_qa, p_e, p_d, p_et, p_dt = (sem(f"p_{k}") for k in ("u", "qa", "e", "d", "et", "dt"))
        p_s0, p_x, p_s1, p_v, p_o = (sem(f"p_{k}") for k in ("s0", "x", "s1", "v", "o"))
        a_s, a_th, a_qa, a_err, a_et, a_xs, a_v, a_sq = (sem(f"a_{k}") for k in ("s", "tu", "qa", "err", "et", "xs", "v", "sq"))
        v_q, v_g, v_du, v_p0, v_dt, v_p1, v_ms, v_acc, v_y, v_cf = (
            sem(f"v_{k}") for k in ("q", "g", "du", "p0", "dt", "p1", "ms", "acc", "yb", "cf"))
        g_rs, g_rg = sem("g_rs"), sem("g_rg")
        s_out = sem("s_out")
        s_zero = sem("s_zero")

        def heads(eng, step):
            step((0, 0), None)
            for h in range(H):
                step((0, h + 1) if h + 1 < H else (1, 0), (0, h))
            with eng.Fori(1, B - 1) as b:
                for h in range(H):
                    step((b, h + 1) if h + 1 < H else (b + 1, 0), (b, h))
            for h in range(H):
                step((B - 1, h + 1) if h + 1 < H else None, (B - 1, h))

        n_of = lambda at: at[0] * H + at[1]

        with nc.Block() as block:

            @block.tensor
            def _(pe):
                def scores(first, left, right, done):
                    for i in SC_ORDER:
                        last = pe.matmul(m.bank[SC_BANK[i]][:, SC_COL[i]:SC_COL[i] + S - P * i],
                                         left[:, i * P:i * P + P], right[:, P * i:], start=True, stop=True)
                        if i != 1:
                            last.then_inc(done, 1)

                def apply(out, rows, made, n):
                    for i in SC_ORDER:
                        if i != 3:
                            pe.wait_ge(made, SC_BANKS * n + {0: 1, 1: 2, 2: 3}[i])
                        last = pe.matmul(out[:, P * i:], rows[:, i, :], p_sb[:, P_COL[i]:P_COL[i] + S - P * i],
                                         start=False, stop=True, skip_group_check=True)
                    return last

                def step(f, s):
                    if f is not None:
                        h, n = f[1], n_of(f)
                        yq = yb[:, SHIFT:]
                        if h == 0:
                            pe.wait_ge(v_y, f[0] + 1)
                        pe.wait_ge(v_du, n)
                        pe.matmul(U[:], m.w_u[:, h, :], yb[:, 0:S], start=True, stop=True).then_inc(p_u, 1)
                        if isinstance(n, int) and n < 2:
                            pass
                        else:
                            pe.wait_ge(v_acc, n - 1)
                        pe.matmul(QA[:], m.w_qk[:, h, :], yq, start=True, stop=True).then_inc(p_qa, 1)
                    if s is not None:
                        k = n_of(s)
                        pe.wait_ge(a_xs, k + 1)
                        pe.wait_ge(v_p0, SC_BANKS * (k + 1))
                        scores(s, s_sb[s[1] % 2], xs, p_s1)
                    if f is not None:
                        pe.wait_ge(v_dt, n)
                        pe.matmul(EB[:], m.w_v[:, h, :], yb[:, 0:S], start=True, stop=False)
                        pe.wait_ge(a_s, n + 1)
                        pe.matmul(EB[:], m.w1n[:], s_sb[h % 2][:], start=False, stop=True).then_inc(p_e, 1)
                    if s is not None:
                        pe.wait_ge(v_ms, k)
                        pe.wait_ge(a_et, k + 1)
                        pe.matmul(VB[:], m.w1n[:], xs[:], start=True, stop=True)
                        apply(VB, err_t, v_p1, k).then_inc(p_v, 1)
                    if f is not None:
                        pe.wait_ge(a_err, n + 1)
                        pe.wait_ge(v_q, n + 1)
                        pe.matmul(U[:], m.w4t[:, 3, :], err[:], start=True, stop=True).then_inc(p_d, 1)
                        pe.wait_ge(a_xs, n)
                        for t in range(T):
                            last = pe.transpose(XB[:, t * P:t * P + P], err[:, t * P:t * P + P], m.ident[:])
                        last.then_inc(p_et, 1)
                        pe.wait_ge(a_qa, n + 1)
                        pe.wait_ge(v_p1, SC_BANKS * n)
                        scores(f, yb, qa, p_s0)
                    if s is not None:
                        pe.wait_ge(a_v, k + 1)
                        for t in range(T):
                            pe.matmul(QA[:, t * P:t * P + P], vals[:, t * P:t * P + P], m.w_out[:, s[1], :], start=True, stop=True)
                        pe.wait_ge(a_sq, k + 1)
                        for t in range(T):
                            last = pe.matmul(VB[:, t:t + 1], sq[:, t * P:t * P + P], m.ones[:, 0:1], start=True, stop=True)
                        last.then_inc(p_o, 1)
                    if f is not None:
                        pe.wait_ge(v_du, n + 1)
                        for t in range(T):
                            last = pe.transpose(EB[:, t * P:t * P + P], du[:, t * P:t * P + P], m.ident[:])
                        last.then_inc(p_dt, 1)
                        pe.wait_ge(a_et, n + 1)
                        pe.matmul(XB[:], m.w_x[:, h, :], yq, start=True, stop=True)
                        pe.wait_ge(v_dt, n + 1)
                        apply(XB, du_t, v_p0, n).then_inc(p_x, 1)

                heads(pe, step)

            @block.scalar
            def _(act):
                def step(f, s):
                    if s is not None:
                        k = n_of(s)
                        act.wait_ge(p_x, k + 1)
                        nc.scalar.activation(xs[:], XB[:], ACT.Silu).then_inc(a_xs, 1)
                    if f is not None:
                        h, n = f[1], n_of(f)
                        act.wait_ge(p_u, n + 1)
                        nc.scalar.activation(s_sb[h % 2][:], U[:], ACT.Silu).then_inc(a_s, 1)
                        act.wait_ge(v_g, n)
                        nc.scalar.activation(th[:], U[:], ACT.Tanh, scale=0.5).then_inc(a_th, 1)
                        act.wait_ge(p_qa, n + 1)
                        nc.scalar.copy(qa[:], QA[:]).then_inc(a_qa, 1)
                        act.wait_ge(p_e, n + 1)
                        nc.scalar.copy(err[:], EB[:]).then_inc(a_err, 1)
                    if s is not None:
                        act.wait_ge(p_v, k + 1)
                        nc.scalar.copy(vals[:], VB[:]).then_inc(a_v, 1)
                        act.wait_ge(a_v, k + 1)
                        nc.scalar.activation(sq[:], vals[:], ACT.Square).then_inc(a_sq, 1)
                    if f is not None:
                        act.wait_ge(p_et, n + 1)
                        nc.scalar.copy(err_t[:].rearrange("p t d -> p (t d)"), XB[:]).then_inc(a_et, 1)

                heads(act, step)

            @block.vector
            def _(dve):
                def weigh(h, made):
                    for i in SC_ORDER:
                        ch = NC - 2 * i
                        src = m.bank[SC_BANK[i]][:, SC_COL[i]:SC_COL[i] + C * ch].rearrange("p (c n) -> p c n", n=C)
                        dst = p_sb[:, P_COL[i]:P_COL[i] + C * ch].rearrange("p (c n) -> p c n", n=C)
                        w = cf[:, h, i * NC + 2 * i:i * NC + NC].unsqueeze(2).broadcast_to([P, ch, C])
                        yield i, dst, src, w

                def step(f, s):
                    if f is not None and f[1] == 0:
                        dve.wait_ge(p_x, f[0] * H)
                        nc.vector.tensor_copy(yb[:], m.y_all[:, bass.ts(f[0], 1), :].rearrange("p a n -> p (a n)")).then_inc(v_y, 1)
                    if s is not None:
                        k = n_of(s)
                        for i, dst, src, w in weigh(s[1], v_p1):
                            if i != 3:
                                dve.wait_ge(p_s1, SC_BANKS * k + {0: 1, 1: 2, 2: 3}[i])
                            last = nc.vector.tensor_tensor(dst, src, w, ALU.mult)
                            if i != 1:
                                last.then_inc(v_p1, 1)
                    if f is not None:
                        h, n = f[1], n_of(f)
                        if h == 0:
                            if s is not None:
                                dve.wait_ge(v_p1, SC_BANKS * (k + 1))
                            nc.vector.tensor_copy(cf[:], m.coef[:, bass.ts(f[0], 1), :, :].rearrange("p a h c -> p (a h) c")).then_inc(v_cf, 1)
                        dve.wait_ge(a_th, n + 1)
                        dve.wait_ge(a_s, n + 1)
                        nc.vector.scalar_tensor_tensor(q_sb[:], U[:], 1.0, s_sb[h % 2][:], ALU.add, ALU.subtract).then_inc(v_q, 1)
                        dve.wait_ge(v_q, n + 1)
                        nc.vector.scalar_tensor_tensor(q_sb[:], th[:], 1.0, q_sb[:], ALU.add, ALU.mult).then_inc(v_g, 1)
                        dve.wait_ge(v_g, n + 1)
                        dve.wait_ge(p_d, n + 1)
                        nc.vector.scalar_tensor_tensor(du[:], q_sb[:], 0.5, U[:], ALU.mult, ALU.mult).then_inc(v_du, 1)
                        if h == 0:
                            dve.wait_ge(v_cf, f[0] + 1)
                        for i, dst, src, w in weigh(h, v_p0):
                            if i != 3:
                                dve.wait_ge(p_s0, SC_BANKS * n + {0: 1, 1: 2, 2: 3}[i])
                            last = nc.vector.tensor_tensor(dst, src, w, ALU.mult)
                            if i != 1:
                                last.then_inc(v_p0, 1)
                    if s is not None:
                        dve.wait_ge(p_o, k + 1)
                        dve.wait_ge(g_rs, k)
                        nc.vector.tensor_scalar(ms[:], VB[:, 0:T], 1.0 / D, RMS_EPS, ALU.mult, ALU.add).then_inc(v_ms, 1)
                    if f is not None:
                        dve.wait_ge(p_dt, n + 1)
                        nc.vector.tensor_copy(du_t[:].rearrange("p t d -> p (t d)"), EB[:]).then_inc(v_dt, 1)
                    if s is not None:
                        dve.wait_ge(g_rg, k + 1)
                        if s[1] == 0:
                            dve.wait_ge(s_out, 32 * s[0])
                        else:
                            dve.wait_ge(v_acc, k)
                        for t in range(T):
                            o, g = QA[:, t * P:t * P + P], rg[:, t:t + 1]
                            if s[1] == 0:
                                last = nc.vector.tensor_scalar(acc[:, t, :], o, g, None, ALU.mult)
                            else:
                                last = nc.vector.scalar_tensor_tensor(acc[:, t, :], o, g, acc[:, t, :], ALU.mult, ALU.add)
                        last.then_inc(v_acc, 1)

                heads(dve, step)

            @block.gpsimd
            def _(pool):
                def scatter(t):
                    nc.gpsimd.indirect_dma_start(m.sorted_rows, bass.IndirectOffsetOnAxis(m.place[:, t:t + 1], axis=0),
                                                 m.xl_all[:, t, :], None).then_inc(m.s_scatter, 16)

                def norm(s):
                    k = n_of(s)
                    pool.wait_ge(v_ms, k + 1)
                    nc.gpsimd.tensor_tensor(rs[:], ms[:], m.neg_half[:, 0:T], ALU.pow).then_inc(g_rs, 1)
                    pool.wait_ge(g_rs, k + 1)
                    pool.wait_ge(v_acc, k)
                    gate = m.gate_th[:, bass.ts(s[0], T), :][:, :, s[1]]
                    nc.gpsimd.tensor_tensor(rg[:], rs[:], gate, ALU.mult).then_inc(g_rg, 1)

                for h in range(H):
                    norm((0, h))
                    for t in range(T):
                        scatter(T * h + t)
                with pool.Fori(1, B) as b:
                    for h in range(H):
                        norm((b, h))
                pool.wait_ge(m.s_scatter, 16 * NT)

            @block.sync
            def _(sp):
                rows = m.attn_out.rearrange("(b s) d -> b s d", s=S)
                sp.dma_start(rows[:, 0:SHIFT, :].rearrange("b p d -> p b d"), m.zeros[0:SHIFT]).then_inc(s_zero, 16)
                rest = S - SHIFT - (T - 1) * P
                with sp.Fori(0, B) as b:
                    sp.wait_ge(v_acc, (b + 1) * H)
                    sp.dma_start(rows[b, SHIFT:SHIFT + (T - 1) * P, :].rearrange("(t p) d -> p t d", p=P), acc[:, 0:T - 1, :]).then_inc(s_out, 16)
                    sp.dma_start(rows[b, S - rest:S, :], acc[0:rest, T - 1, :]).then_inc(s_out, 16)
                sp.wait_ge(s_out, 32 * B)
                sp.wait_ge(s_zero, 16)


def experts(nc, m, a):
    with ExitStack() as ctx:
        sb = lambda n, s, d=F32: ctx.enter_context(nc.sbuf_tensor(n, s, d))
        sem = lambda n: ctx.enter_context(nc.semaphore(n))
        two = lambda n, s, d=F32: [sb(f"{n}{k}", s, d) for k in range(2)]
        w1 = sb("ew1", [P, E, HF])
        w2 = sb("ew2", [P, E, FB, D])
        rows = two("rows", [P, ROW])
        w1s = two("w1s", [P, HF])
        col = two("col", [P, 2 + FB])
        meta = two("meta", [P, 2])
        ids = two("ids", [P, 1], I32)
        xf = two("xf", [P, P])
        hid = two("hidx", [P, FB, P])
        ysum = sb("ysum", [P, D])
        y = two("yx", [P, D])
        s_w1, s_w2 = sem("s_w1"), sem("s_w2")
        s_rows = [sem(f"s_rows{k}") for k in range(2)]
        s_y = [sem(f"s_y{k}") for k in range(2)]
        p_t, p_h, p_y = sem("p_t"), sem("p_hh"), sem("p_yy")
        v_w, v_xf, v_y, v_c = sem("v_w"), sem("v_xf"), sem("v_yy"), sem("v_c")
        a_h = sem("a_h")
        g_held = sem("g_held")

        with nc.Block() as block:

            @block.sync
            def _(sp):
                sp.dma_start(w1[:], a["L1_ffn_w1"].rearrange("e d f -> d e f")).then_inc(s_w1, 16)
                src = m.sorted_rows.rearrange("(n p) r -> n p r", p=P)
                for q in range(2):
                    sp.dma_start(rows[q][:], src[q]).then_inc(s_rows[q], 16)
                with sp.Fori(1, NB // 2) as j:
                    for q in range(2):
                        sp.wait_ge(p_t, 2 * j + q - 1)
                        sp.wait_ge(v_w, 2 * j + q - 1)
                        sp.dma_start(rows[q][:], src[2 * j + q]).then_inc(s_rows[q], 16)

            @block.scalar
            def _(act):
                act.dma_start(w2[:], a["L1_ffn_w2"].rearrange("e (k f) d -> f e k d", f=P)).then_inc(s_w2, 16)

                def step(t1, t2, t3):
                    if t2 is not None:
                        q = t2.par
                        act.wait_ge(p_h, t2.i + 1)
                        act.wait_ge(p_y, less(t2.i, 1))
                        for k in range(FB):
                            last = nc.scalar.activation(hid[q][:, k, :], m.bank[2 + q][:, k * P:k * P + P], ACT.Relu,
                                                        bias=col[q][:, 2 + k:3 + k])
                        last.then_inc(a_h, 1)

                pipelined(act, step, NB, 3)

            @block.tensor
            def _(pe):
                pe.wait_ge(s_w2, 16)

                def step(t1, t2, t3):
                    if t2 is not None:
                        q = t2.par
                        pe.wait_ge(v_xf, t2.i + 1)
                        pe.wait_ge(a_h, less(t2.i, 1))
                        for k in range(FB):
                            last = pe.matmul(m.bank[2 + q][:, k * P:k * P + P], w1s[q][:, k * P:k * P + P], xf[q][:], start=True, stop=True)
                        last.then_inc(p_h, 1)
                    if t1 is not None:
                        q = t1.par
                        pe.wait_ge(s_rows[q], 16 * (t1.half + 1))
                        pe.wait_ge(v_xf, less(t1.i, 1))
                        pe.transpose(m.bank[q][:, 0:P], rows[q][:, 0:D], m.ident[:]).then_inc(p_t, 1)
                    if t3 is not None:
                        q = t3.par
                        pe.wait_ge(a_h, t3.i + 1)
                        pe.wait_ge(v_y, less(t3.i, 1))
                        e = pe.value_load(m.blk_e[0:1, bass.ds(t3.i, 1)], min_val=0, max_val=E - 1)
                        for k in range(FB):
                            last = pe.matmul(m.bank[4 + q][:, 0:D], hid[q][:, k, :], w2[:, bass.ds(e, 1), k, :].rearrange("p a d -> p (a d)"),
                                             start=(k == 0), stop=(k == FB - 1))
                        last.then_inc(p_y, 1)

                pipelined(pe, step, NB, 3)

            @block.vector
            def _(dve):
                dve.wait_ge(s_w1, 16)

                def step(t1, t2, t3):
                    if t3 is not None:
                        q = t3.par
                        link = Chain(dve, v_c, t3.i)
                        dve.wait_ge(p_y, t3.i + 1)
                        dve.wait_ge(s_y[q], 16 * t3.half)
                        dve.wait_ge(v_y, t3.i)
                        e = dve.value_load(m.blk_e[0:1, bass.ds(t3.i, 1)], min_val=0, max_val=E - 1)
                        link(nc.vector.tensor_tensor(ysum[:], m.bank[4 + q][:, 0:D], m.b2_bc[:, bass.ds(e, 1), :].rearrange("p a d -> p (a d)"), ALU.add))
                        nc.vector.tensor_copy(ids[q][:], meta[q][:, 0:1].bitcast(I32))
                        nc.vector.tensor_scalar(y[q][:], ysum[:], meta[q][:, 1:2], None, ALU.mult).then_inc(v_y, 1)
                    if t1 is not None:
                        q = t1.par
                        e = dve.value_load(m.blk_e[0:1, bass.ds(t1.i, 1)], min_val=0, max_val=E - 1)
                        dve.wait_ge(p_h, less(t1.i, 1))
                        dve.wait_ge(a_h, less(t1.i, 1))
                        dve.wait_ge(v_y, less(t1.i, 1))
                        nc.vector.tensor_copy(w1s[q][:], w1[:, bass.ds(e, 1), :].rearrange("p a d -> p (a d)"))
                        nc.vector.tensor_copy(col[q][:], m.par_e[:, bass.ds(e, 1), :].rearrange("p a d -> p (a d)"))
                        dve.wait_ge(s_rows[q], 16 * (t1.half + 1))
                        nc.vector.tensor_copy(meta[q][:], rows[q][:, D:ROW]).then_inc(v_w, 1)
                        dve.wait_ge(v_w, t1.i + 1)
                        dve.wait_ge(p_t, t1.i + 1)
                        nc.vector.tensor_scalar(xf[q][:], m.bank[q][:, 0:P], col[q][:, 0:1], col[q][:, 1:2], ALU.mult, ALU.add).then_inc(v_xf, 1)

                pipelined(dve, step, NB, 3)

            @block.gpsimd
            def _(pool):
                with pool.Fori(0, NB // 2) as j:
                    for q in range(2):
                        pool.wait_ge(v_y, 2 * j + q + 1)
                        pool.sem_inc(g_held, 1)
                        nc.gpsimd.indirect_dma_start(m.ffn_rows, bass.IndirectOffsetOnAxis(ids[q][:, 0:1], axis=0),
                                                     y[q][:], None).then_inc(s_y[q], 16)
                for q in range(2):
                    pool.wait_ge(s_y[q], 16 * (NB // 2))


def combine(nc, m, out):
    with ExitStack() as ctx:
        sb = lambda n, s, d=F32: ctx.enter_context(nc.sbuf_tensor(n, s, d))
        sem = lambda n: ctx.enter_context(nc.semaphore(n))
        two = lambda n, s: [sb(f"{n}{k}", s) for k in range(2)]
        f = two("fin_f", [P, T * D])
        at = two("fin_a", [P, T * D])
        g = two("fin_g", [P, T * D])
        o = two("fin_o", [P, T * D])
        s_in = [sem(f"fin_in{k}") for k in range(2)]
        s_o = [sem(f"fin_out{k}") for k in range(2)]
        v_f, a_g, v_o, v_c = sem("fin_vf"), sem("fin_ag"), sem("fin_vo"), sem("fin_vc")

        with nc.Block() as block:

            @block.sync
            def _(sp):
                view = lambda rows: rows.rearrange("(b t p) d -> b p t d", t=T, p=P)

                def load(b, q):
                    sp.dma_start(f[q][:].rearrange("p (t d) -> p t d", d=D), view(m.ffn_rows[0:B * S])[b]).then_inc(s_in[q], 16)
                    sp.dma_start(at[q][:].rearrange("p (t d) -> p t d", d=D), view(m.attn_out)[b]).then_inc(s_in[q], 16)

                for q in range(2):
                    load(q, q)
                with sp.Fori(1, B // 2) as j:
                    for q in range(2):
                        sp.wait_ge(v_o, 2 * j + q - 1)
                        load(2 * j + q, q)

            @block.scalar
            def _(act):
                dst = out.rearrange("b (t p) d -> b p t d", p=P)

                def step(b1, b2):
                    if b1 is not None:
                        act.wait_ge(v_f, b1.i + 1)
                        act.wait_ge(v_o, less(b1.i, 1))
                        nc.scalar.activation(g[b1.par][:], f[b1.par][:], ACT.Silu).then_inc(a_g, 1)
                    if b2 is not None:
                        act.wait_ge(v_o, b2.i + 1)
                        act.dma_start(dst[b2.i], o[b2.par][:].rearrange("p (t d) -> p t d", d=D)).then_inc(s_o[b2.par], 16)

                pipelined(act, step, B, 2)
                for q in range(2):
                    act.wait_ge(s_o[q], 16 * B // 2)

            @block.vector
            def _(dve):
                flat = lambda t, b: t[:, bass.ts(b, T), :].rearrange("p t d -> p (t d)")

                def step(b1, b2):
                    if b1 is not None:
                        q = b1.par
                        dve.wait_ge(s_in[q], 32 * (b1.half + 1))
                        nc.vector.tensor_tensor(f[q][:], f[q][:], flat(m.xn1_all, b1.i), ALU.add).then_inc(v_f, 1)
                    if b2 is not None:
                        q = b2.par
                        link = Chain(dve, v_c, b2.i)
                        dve.wait_ge(a_g, b2.i + 1)
                        link(nc.vector.tensor_tensor(at[q][:], at[q][:], g[q][:], ALU.mult))
                        dve.wait_ge(s_o[q], 16 * b2.half)
                        nc.vector.tensor_tensor(o[q][:], at[q][:], flat(m.x1_all, b2.i), ALU.add).then_inc(v_o, 1)

                pipelined(dve, step, B, 2)


def program(nc, a, out):
    with ExitStack() as ctx:
        sb = lambda n, s, d=F32: ctx.enter_context(nc.sbuf_tensor(n, s, d))
        m = Mem()
        m.bank = [ctx.enter_context(nc.psum_tensor(f"bank{k}", [P, 512], F32)) for k in range(8)]
        m.sorted_rows = nc.dram_tensor("sorted_rows", (NB * P, ROW), F32, kind="Internal").ap()
        m.attn_out = nc.dram_tensor("attn_out", (B * S, D), F32, kind="Internal").ap()
        m.ffn_rows = nc.dram_tensor("ffn_rows", (B * S + NB * P, D), F32, kind="Internal").ap()
        m.s_scatter = ctx.enter_context(nc.semaphore("s_scatter"))
        m.ident, m.ones, m.upper = sb("ident", [P, P]), sb("ones", [P, P]), sb("upper", [P, P])
        m.neg_half = sb("neg_half", [P, 2 * T])
        m.starts = sb("starts", [P, NC, T])
        m.rank_i, m.rank_f = sb("rank_i", [P, NT, E], I32), sb("rank_f", [P, NT, E])
        m.block_i, m.block_f = sb("block_i", [P, NB, E], I32), sb("block_f", [P, NB, E])
        m.token_i = sb("token_i", [P, NT], I32)
        m.restart = sb("restart", [P, E, NT])
        m.zeros = sb("zeros", [P, B, D])
        m.cols = sb("cols", [P, V_ROWS])
        m.half_b = sb("half_b", [P, 4])
        m.alpha1, m.alpha2, m.alpha2h = sb("alpha1", [P, FB]), sb("alpha2", [P, 1]), sb("alpha2h", [P, 1])
        m.w4t, m.s1t, m.s2t = sb("w4t", [P, 4, D]), sb("s1t", [P, FB, P]), sb("s2t", [P, FB, P])
        m.w1n = sb("w1n", [P, D])
        m.w_u, m.w_v, m.w_qk, m.w_x, m.w_out = (sb(n, [P, H, D]) for n in ("w_u", "w_v", "w_qk", "w_x", "w_out"))
        m.w_sm, m.w_md = sb("w_sm", [P, E + 2 * H]), sb("w_md", [P, 2 * H])
        m.b2_bc = sb("b2_bc", [P, E, D])
        m.par_e = sb("par_e", [P, E, 2 + FB])
        m.x1_all, m.xn1_all = sb("x1_all", [P, NT, D]), sb("xn1_all", [P, NT, D])
        m.xl_all = sb("xl_all", [P, NT, ROW])
        m.y_all = sb("y_all", [P, B, S + SHIFT])
        m.y_f = [sb(f"y_f{k}", [P, S + SHIFT]) for k in range(2)]
        m.aff, m.lr_th, m.gate_th = (sb(n, [P, NT, E]) for n in ("aff", "lr_th", "gate_th"))
        m.md_th = sb("md_th", [P, B * NC, 2 * H])
        m.ry = sb("ry", [P, NT])
        m.coef = sb("coef", [P, B, H, T * NC])
        m.place = sb("place", [P, NT], U32)
        m.blk_e = sb("blk_e", [P, NB], I32)
        prepare(nc, m, a)
        layer0(nc, m, a)
        routing(nc, m)
        memory_attention(nc, m)
        experts(nc, m, a)
        combine(nc, m, out)


_INS = ["L0_attn_inputs", "L0_attn_Wa", "L0_attn_ba", "L0_attn_Wb", "L0_attn_bb", "L0_attn_Wc", "L0_attn_bc",
        "L0_ffn_w1", "L0_ffn_b1", "L0_ffn_w2", "L0_ffn_b2", "L1_attn_store_norm_g", "L1_attn_retrieve_norm_g",
        "L1_attn_w_kv", "L1_attn_w_q", "L1_attn_w_step", "L1_attn_w_mom", "L1_attn_w_decay", "L1_attn_w_gate",
        "L1_attn_w_combine", "L1_attn_mh_gamma", "L1_attn_mem_w0", "L1_attn_mem_w1", "L1_ffn_centroids",
        "L1_ffn_ln_g", "L1_ffn_ln_b", "L1_ffn_w1", "L1_ffn_b1", "L1_ffn_w2", "L1_ffn_b2"]


def kernel(**inputs):
    import numpy as np
    import concourse.bacc as bacc
    from concourse.bass_utils import run_bass_kernel_spmd

    nc = bacc.Bacc("TRN2", target_bir_lowering=False, num_devices=1)
    arrays, args = {}, {}
    for name in _INS:
        x = np.ascontiguousarray(inputs[name])
        arrays[f"in_{name}"] = x
        args[name] = nc.dram_tensor(f"in_{name}", x.shape, mybir.dt.from_np(x.dtype), kind="ExternalInput").ap()
    out = nc.dram_tensor("out", (B, S, D), F32, kind="ExternalOutput").ap()
    program(nc, args, out)
    r = run_bass_kernel_spmd(nc, [arrays], core_ids=[0])
    return r.results[0]["out"]
```

```python
from contextlib import ExitStack

import concourse.bass as bass
from concourse import mybir

F32 = mybir.dt.float32
F32R = mybir.dt.float32r
I32 = mybir.dt.int32
U32 = mybir.dt.uint32
BF16 = mybir.dt.bfloat16
ALU = mybir.AluOpType
ACT = mybir.ActivationFunctionType
AX = mybir.AxisListType

P = 128
B, S, D = 8, 512, 128
T = S // P
NT = B * T
HF = 512
FB = HF // P
H = 8
C = 64
NC = S // C
SHIFT = C - 1
QW = S - SHIFT + 1
Q_LAST = QW - (T - 1) * P
E = 8
NB = NT + E
ROW = D + 1
RING = 4
LN_EPS, RMS_EPS, MAX_LR = 1e-5, 1e-6, 0.01

V_BA, V_BB, V_BC, V_B1, V_B2, V_GS, V_GR, V_GAM = 0, 1, 2, 3, 7, 8, 9, 10
V_CENT, V_LNG, V_LNB, V_EB1 = 18, 26, 34, 42
V_ROWS = V_EB1 + E * FB

SC_BANK = [4, 5, 6, 5]
SC_COL = [0, 0, 0, 384]
P_COL = [0, 512, 1024, 896]
SC_ORDER = [0, 1, 3, 2]
SC_BANKS = 3
P_COLS = sum(S - P * i for i in range(T))


PAR, B2 = HF, HF + 2 + FB


class Chain:

    def __init__(self, eng, sem, base=0):
        self.eng, self.sem, self.base, self.n = eng, sem, base, 0

    def __call__(self, ins):
        self.n += 1
        ins.then_inc(self.sem, 1)
        self.eng.wait_ge(self.sem, self.base + self.n)


class At:

    def __init__(self, half, par, ring=2):
        self.i, self.par, self.half = half * ring + par, par, half


def less(n, k):
    return max(n - k, 0) if isinstance(n, int) else n - k


def pipelined(eng, step, count, depth, ring=2):
    at = lambda i: At(i // ring, i % ring, ring) if 0 <= i < count else None
    first, last = 4, count
    last -= last % ring
    for t in range(first):
        step(*[at(t - k) for k in range(depth)])
    with eng.Fori(0, (last - first) // ring) as j:
        for u in range(ring):
            ats = []
            for k in range(depth):
                c = first + u - k
                ats.append(At(j + c // ring, c % ring, ring))
            step(*ats)
    for t in range(last, count + depth - 1):
        step(*[at(t - k) for k in range(depth)])


class Mem:
    pass


def prepare(nc, m, a):
    with ExitStack() as ctx:
        sb = lambda n, s, d=F32: ctx.enter_context(nc.sbuf_tensor(n, s, d))
        sem = lambda n: ctx.enter_context(nc.semaphore(n))
        vec = sb("vec", [P, D])
        sq4 = sb("sq4", [P, 4, D])
        mem0 = sb("mem0", [P, D])
        l0w1 = sb("l0w1", [P, FB, D])
        l0w2 = sb("l0w2", [P, HF])
        wkv = sb("wkv", [P, 2 * H * D])
        wq = sb("wq", [P, H * D])
        wcomb = sb("wcomb", [P, H, D])
        small = sb("small", [P, 4, H])
        b2row = sb("b2row", [1, E * D])
        sg1 = sb("sg1", [P, FB, D])
        sg2 = sb("sg2", [P, HF])
        kt = sb("kt", [P, H, D])
        qt = sb("qt", [P, H, D])
        gam1 = sb("gam1", [P, H])
        junk = sb("junk", [P, HF])
        fill = sb("fill", [P, NB - NT, ROW])
        rank_i, block_i = sb("rank_i", [P, NT, E], I32), sb("block_i", [P, NB, E], I32)
        names = ["vec", "sq4", "mem0", "l0w1", "l0w2", "wkv", "wq", "wcomb", "small", "b2row"]
        got = {n: sem(f"got_{n}") for n in names}
        filled = sem("filled")
        consts = sem("consts")
        pool_made = []
        fill_ok = sem("fill_ok")
        signs = sem("signs")
        pe_group = sem("pe_group")
        out_group = sem("out_group")
        scaled = sem("scaled")
        dve_c = sem("dve_c0")
        act_c = sem("act_c0")
        a_high = sem("a_high")
        SPLIT = 8

        with nc.Block() as block:

            @block.sync
            def _(sp):
                rows = [
                    (V_BA, 1, a["L0_attn_ba"].rearrange("(a n) -> a n", a=1)),
                    (V_BB, 1, a["L0_attn_bb"].rearrange("(a n) -> a n", a=1)),
                    (V_BC, 1, a["L0_attn_bc"].rearrange("(a n) -> a n", a=1)),
                    (V_B1, FB, a["L0_ffn_b1"].rearrange("(a n) -> a n", a=FB)),
                    (V_B2, 1, a["L0_ffn_b2"].rearrange("(a n) -> a n", a=1)),
                    (V_GS, 1, a["L1_attn_store_norm_g"].rearrange("(a n) -> a n", a=1)),
                    (V_GR, 1, a["L1_attn_retrieve_norm_g"].rearrange("(a n) -> a n", a=1)),
                    (V_GAM, H, a["L1_attn_mh_gamma"].rearrange("h a d -> (h a) d")),
                    (V_CENT, E, a["L1_ffn_centroids"]),
                    (V_LNG, E, a["L1_ffn_ln_g"]),
                    (V_LNB, E, a["L1_ffn_ln_b"]),
                    (V_EB1, E * FB, a["L1_ffn_b1"].rearrange("e (k n) -> (e k) n", k=FB)),
                ]
                for r, n, src in rows:
                    sp.dma_start(vec[r:r + n, :], src).then_inc(got["vec"], 16)
                for k, n in enumerate(["L0_attn_Wa", "L0_attn_Wb", "L0_attn_Wc", "L1_attn_mem_w1"]):
                    sp.dma_start(sq4[:, k, :], a[n]).then_inc(got["sq4"], 16)
                sp.dma_start(l0w1[:], a["L0_ffn_w1"].rearrange("(k p) d -> p k d", p=P)).then_inc(got["l0w1"], 16)
                sp.dma_start(l0w2[:], a["L0_ffn_w2"]).then_inc(got["l0w2"], 16)
                sp.wait_ge(fill_ok, 1)
                blocks = m.sorted_rows.rearrange("(n p) r -> p n r", p=P)
                sp.dma_start(blocks[:, 0:NT, :], m.xl_all[:]).then_inc(filled, 16)
                sp.dma_start(blocks[:, NT:, :], fill[:]).then_inc(filled, 16)
                sp.wait_ge(filled, 32)

            @block.scalar
            def _(act):
                act.dma_start(wkv[:], a["L1_attn_w_kv"]).then_inc(got["wkv"], 16)
                act.dma_start(wq[:], a["L1_attn_w_q"]).then_inc(got["wq"], 16)
                act.dma_start(mem0[:], a["L1_attn_mem_w0"]).then_inc(got["mem0"], 16)
                act.dma_start(m.w1n[:], a["L1_attn_mem_w1"]).then_inc(got["mem0"], 16)
                for k, n in enumerate(["step", "mom", "decay", "gate"]):
                    act.dma_start(small[:, k, :], a[f"L1_attn_w_{n}"]).then_inc(got["small"], 16)
                act.dma_start(wcomb[:], a["L1_attn_w_combine"].rearrange("(h e) d -> e h d", e=D)).then_inc(got["wcomb"], 16)
                act.dma_start(b2row[:], a["L1_ffn_b2"].rearrange("(a e) d -> a (e d)", a=1)).then_inc(got["b2row"], 16)
                act.wait_ge(got["l0w1"], 16)
                nc.scalar.activation(sg1[:], l0w1[:], ACT.Sign).then_inc(signs, 1)
                act.wait_ge(got["l0w2"], 16)
                nc.scalar.activation(sg2[:], l0w2[:], ACT.Sign).then_inc(signs, 1)
                chain = Chain(act, act_c)
                for k in range(FB):
                    chain(nc.scalar.activation(junk[:, 0:D], l0w1[:, k, :], ACT.Abs, accum_out=m.alpha1[:, k:k + 1]))
                chain(nc.scalar.activation(junk[:], l0w2[:], ACT.Abs, accum_out=m.alpha2[:]))
                chain(nc.scalar.mul(m.alpha1[:], m.alpha1[:], 1.0 / D))
                chain(nc.scalar.mul(m.alpha2[:], m.alpha2[:], 1.0 / HF))
                chain(nc.scalar.mul(m.alpha2h[:], m.alpha2[:], 0.5))
                group = SPLIT
                for w in (m.w_u, m.w_x, m.w_qk):
                    for g in range(2):
                        group += 1
                        act.wait_ge(pe_group, group)
                        nc.scalar.copy(w[0][:, 4 * g:4 * g + 4, :], m.bank[(group - 1) % 8][:].rearrange("p (a b) -> p a b", b=P)).then_inc(a_high, 1)

            @block.gpsimd
            def _(pool):
                chain = Chain(pool, consts)
                chain(nc.gpsimd.memset(m.ident[:], 0.0))
                chain(nc.gpsimd.affine_select(out=m.ident[:], in_=m.ident[:], compare_op=ALU.not_equal, fill=1.0,
                                              base=0, pattern=[[-1, P]], channel_multiplier=1))
                chain(nc.gpsimd.memset(m.ones[:], 1.0))
                chain(nc.gpsimd.memset(m.upper[:], 1.0))
                chain(nc.gpsimd.affine_select(out=m.upper[:], in_=m.upper[:], compare_op=ALU.is_gt, fill=0.0,
                                              base=0, pattern=[[1, P]], channel_multiplier=-1))
                chain(nc.gpsimd.memset(m.neg_half[:], -0.5))
                chain(nc.gpsimd.memset(m.starts[:], 0.0))
                for half in range(2):
                    part = m.starts[C * half:C * half + C]
                    chain(nc.gpsimd.affine_select(out=part, in_=part, compare_op=ALU.not_equal, fill=1.0, base=-half,
                                                  pattern=[[1, NC], [-2, T]], channel_multiplier=0))
                chain(nc.gpsimd.iota(rank_i[:], [[0, NT], [-1, E]], base=E, channel_multiplier=0))
                chain(nc.gpsimd.memset(m.restart[:], 1.0))
                chain(nc.gpsimd.memset(m.restart[:, :, 0:1], 0.0))
                chain(nc.gpsimd.iota(block_i[:], [[1, NB], [0, E]], base=0, channel_multiplier=0))
                chain(nc.gpsimd.iota(m.token_i[:], [[P, NT]], base=0, channel_multiplier=1))
                for rows, n, first in ((m.xl_all, NT, 0), (fill, NB - NT, NT)):
                    chain(nc.gpsimd.memset(rows[:], 0.0))
                    chain(nc.gpsimd.iota(rows[:, :, D].bitcast(I32), [[P, n]], base=B * S + first * P, channel_multiplier=1))
                pool.sem_inc(fill_ok, 1)
                for y in m.y_f:
                    chain(nc.gpsimd.memset(y[:, S:], 0.0))
                chain(nc.gpsimd.memset(m.zeros[:], 0.0))
                pool_made.append(chain.n)

            @block.tensor
            def _(pe):
                pe.wait_ge(consts, 3)
                group = 0

                def bank():
                    nonlocal group
                    if group >= 8:
                        pe.wait_ge(out_group, group - 7)
                    group += 1
                    return m.bank[(group - 1) % 8]

                o = bank()
                pe.wait_ge(got["vec"], 12 * 16)
                pe.transpose(o[:, 0:V_ROWS], vec[0:V_ROWS, :], m.ident[0:V_ROWS, 0:V_ROWS]).then_inc(pe_group, 1)
                o = bank()
                pe.wait_ge(got["sq4"], 64)
                for k in range(4):
                    last = pe.transpose(o[:, k * P:k * P + P], sq4[:, k, :], m.ident[:])
                last.then_inc(pe_group, 1)
                o = bank()
                pe.wait_ge(signs, 1)
                for k in range(FB):
                    last = pe.transpose(o[:, k * P:k * P + P], sg1[:, k, :], m.ident[:])
                last.then_inc(pe_group, 1)
                o = bank()
                pe.wait_ge(signs, 2)
                for k in range(FB):
                    last = pe.transpose(o[:, k * P:k * P + P], sg2[:, k * P:k * P + P], m.ident[:])
                last.then_inc(pe_group, 1)
                for which, src in ((1, wkv), (2, wq)):
                    pe.wait_ge(scaled, which)
                    for g in range(2):
                        o = bank()
                        for k in range(4):
                            h = 4 * g + k
                            last = pe.transpose(o[:, k * P:k * P + P], src[:, h * D:h * D + D], m.ident[:])
                        last.then_inc(pe_group, 1)
                pe.wait_ge(got["mem0"], 32)
                pe.wait_ge(out_group, 8)
                for left, right in ((kt, None), (qt, None), (qt, kt)):
                    for g in range(2):
                        o = bank()
                        for k in range(4):
                            h = 4 * g + k
                            rhs = mem0[:] if right is None else right[:, h, :]
                            last = pe.matmul(o[:, k * P:k * P + P], left[:, h, :], rhs, start=True, stop=True)
                        last.then_inc(pe_group, 1)
                pe.wait_ge(got["b2row"], 16)
                for g in range(2):
                    o = bank()
                    pe.matmul(o[:], m.ones[0:1, :], b2row[:, g * 512:g * 512 + 512], start=True, stop=True).then_inc(pe_group, 1)

            @block.vector
            def _(dve):
                group = 0
                chain = Chain(dve, dve_c)

                def out(dst):
                    nonlocal group
                    group += 1
                    dve.wait_ge(pe_group, group)
                    n = dst.free_size()
                    nc.vector.tensor_copy(dst, m.bank[(group - 1) % 8][:, 0:n] if len(dst.shape) == 2 else
                                          m.bank[(group - 1) % 8][:, 0:n].rearrange("p (a b) -> p a b", b=P)).then_inc(out_group, 1)

                def out_split(w, h):
                    nonlocal group
                    group += 1
                    src = m.bank[(group - 1) % 8][:].rearrange("p (a b) -> p a b", b=P)
                    dve.wait_ge(a_high, group - SPLIT)
                    nc.vector.tensor_tensor(w[1][:, h:h + 4, :], src, w[0][:, h:h + 4, :], ALU.subtract).then_inc(out_group, 1)

                def param(v, n=1):
                    return m.cols[:, v:v + n]

                out(m.cols[:, 0:V_ROWS])
                dve.wait_ge(out_group, 1)
                dve.wait_ge(got["wkv"], 16)
                nc.vector.tensor_scalar(wkv[:, 0:H * D], wkv[:, 0:H * D], param(V_GS), None, ALU.mult).then_inc(scaled, 1)
                dve.wait_ge(got["wq"], 16)
                nc.vector.tensor_scalar(wq[:], wq[:], param(V_GR), None, ALU.mult).then_inc(scaled, 1)
                out(m.w4t[:])
                out(m.s1t[:])
                out(m.s2t[:])
                for g in range(2):
                    out(kt[:, 4 * g:4 * g + 4, :])
                for g in range(2):
                    out(qt[:, 4 * g:4 * g + 4, :])
                for part in range(2):
                    g = slice(4 * part * D, 4 * part * D + 4 * D)
                    v = wkv[:, H * D:][:, g]
                    flat = lambda w: w[:].rearrange("p h d -> p (h d)")[:, g]
                    chain(nc.vector.tensor_scalar(v, v, param(V_GS), -1.0, ALU.mult, ALU.mult))
                    chain(nc.vector.tensor_copy(flat(m.w_v[0]), v))
                    nc.vector.tensor_tensor(flat(m.w_v[1]), v, flat(m.w_v[0]), ALU.subtract).then_inc(scaled, 1)
                chain(nc.vector.tensor_scalar(gam1[:], param(V_GAM, H), 1.0, None, ALU.add))
                dve.wait_ge(got["wcomb"], 16)
                for h in range(H):
                    nc.vector.tensor_scalar(m.w_out[:, h, :], wcomb[:, h, :], gam1[:, h:h + 1], None, ALU.mult).then_inc(scaled, 1)
                chain(nc.vector.tensor_scalar(m.half_b[:, 0:3], param(V_BA, 3), 0.5, None, ALU.mult))
                chain(nc.vector.tensor_scalar(m.half_b[:, 3:4], param(V_B2), 0.5, None, ALU.mult))
                nc.vector.tensor_copy(m.ew1[:, :, PAR:PAR + 1].rearrange("p e a -> p (e a)"), param(V_LNG, E))
                nc.vector.tensor_copy(m.ew1[:, :, PAR + 1:PAR + 2].rearrange("p e a -> p (e a)"), param(V_LNB, E))
                nc.vector.tensor_copy(m.ew1[:, :, PAR + 2:B2], param(V_EB1, E * FB).rearrange("p (e k) -> p e k", k=FB)).then_inc(scaled, 1)
                dve.wait_ge(got["small"], 64)
                nc.vector.tensor_copy(m.w_sm[:, 0:E], param(V_CENT, E)).then_inc(scaled, 1)
                nc.vector.tensor_scalar(m.w_sm[:, E:E + H], small[:, 0, :], param(V_GS), None, ALU.mult).then_inc(scaled, 1)
                nc.vector.tensor_scalar(m.w_sm[:, E + H:E + 2 * H], small[:, 3, :], param(V_GR), None, ALU.mult).then_inc(scaled, 1)
                nc.vector.tensor_scalar(m.w_md[:], small[:, 1:3, :].rearrange("p a h -> p (a h)"), param(V_GS), None, ALU.mult).then_inc(scaled, 1)
                for w in (m.w_u, m.w_x, m.w_qk):
                    for g in range(2):
                        out_split(w, 4 * g)
                for g in range(2):
                    out(m.ew1[:, 4 * g:4 * g + 4, B2:])
                dve.wait_ge(consts, pool_made[0])
                nc.vector.tensor_copy(m.rank_f[:], rank_i[:]).then_inc(scaled, 1)
                nc.vector.tensor_copy(m.block_f[:], block_i[:]).then_inc(scaled, 1)


def layer0(nc, m, a):
    with ExitStack() as ctx:
        sb = lambda n, s, d=F32: ctx.enter_context(nc.sbuf_tensor(n, s, d))
        sem = lambda n: ctx.enter_context(nc.semaphore(n))
        two = lambda n, s: [sb(f"{n}{k}", s) for k in range(2)]
        x0 = two("x0", [P, T, D])
        xn = two("xn", [P, T, D])
        xnf = two("xnf", [P, S])
        th = [sb(f"th{k}", [P, S]) for k in range(3)]
        ga = sb("ga", [P, S])
        nb = sb("nb", [P, S])
        st = sb("st", [P, S])
        hid = sb("hid", [P, FB, S])
        thg = sb("thg", [P, S])
        z = sb("z", [P, S])
        pr = sb("pr", [P, S])
        x1 = two("x1", [P, T, D])
        xn1 = two("xn1", [P, T, D])
        yt = sb("yt", [P, T, D])
        xl = two("xl", [P, T, D])
        bn = sb("bn", [P, T, 6])
        bn1 = sb("bn1", [P, T, 6])
        bn2 = sb("bn2", [P, T, 6])
        mv0, mv1, mv2 = (sb(f"mv{k}", [P, T, 2]) for k in range(3))
        ve0, ve1 = sb("ve0", [P, T]), sb("ve1", [P, T])
        ve2 = sb("ve2", [P, 2, T])
        r0, r1 = sb("r0", [P, T]), sb("r1", [P, T])
        r2 = sb("r2", [P, 2, T])
        cm = sb("cm", [P, NC])
        cmw = sb("cmw", [P, NC, 2 * H])

        s_x0 = [sem(f"s_x0_{k}") for k in range(2)]
        s_keep = [sem(f"s_keep_{k}") for k in range(2)]
        v_var0, v_var1, v_var2 = sem("v_var0"), sem("v_var1"), sem("v_var2")
        g_r0, g_r1, g_r2 = sem("g_r0"), sem("g_r1"), sem("g_r2")
        v_xn = sem("v_xn")
        p_xn, c_xnf = sem("p_xn"), sem("c_xnf")
        p_qkv, c_th = sem("p_qkv"), sem("c_th")
        p_h, c_h = sem("p_h"), sem("c_h")
        p_f, c_thg, v_z = sem("p_f"), sem("c_thg"), sem("v_z")
        v_rec, v_pr, p_pr = sem("v_rec"), sem("v_pr"), sem("p_pr")
        v_x1, v_xn1, v_y = sem("v_x1"), sem("v_xn1"), sem("v_y")
        v_ry = sem("v_ry")
        p_y, c_yf = sem("p_y"), sem("c_yf")
        v_cm, p_sm, p_gt, c_sm = sem("v_cm"), sem("p_sm"), sem("p_gt"), sem("c_sm")
        v_held = sem("v_held")
        g_high, g_split = sem("g_high"), sem("g_split")
        c1, c2, c3a, c3b, c3c = sem("c1"), sem("c2"), sem("c3a"), sem("c3b"), sem("c3c")

        with nc.Block() as block:

            @block.sync
            def _(sp):
                def step(b1, b2, b3):
                    if b1 is not None:
                        sp.wait_ge(v_x1, less(b1.i, 1))
                        sp.dma_start(x0[b1.par][:], a["L0_attn_inputs"][b1.i].rearrange("(k p) d -> p k d", p=P)).then_inc(s_x0[b1.par], 16)
                    if b3 is not None:
                        q = b3.par
                        sp.wait_ge(v_y, b3.i + 1)
                        sp.dma_start(m.x1_rows.rearrange("(b t p) d -> b p t d", t=T, p=P)[b3.i], x1[q][:]).then_inc(s_keep[q], 16)
                        sp.dma_start(m.xn1_rows.rearrange("(b t p) d -> b p t d", t=T, p=P)[b3.i], xn1[q][:]).then_inc(s_keep[q], 16)
                        sp.dma_start(m.xl_all[:, bass.ts(b3.i, T), 0:D], xl[q][:]).then_inc(s_keep[q], 16)

                pipelined(sp, step, B, 3)
                for q in range(2):
                    sp.wait_ge(s_keep[q], 48 * B // 2)

            @block.gpsimd
            def _(pool):
                def power(dst, src, n):
                    return nc.gpsimd.tensor_tensor(dst, src, m.neg_half[:, 0:n], ALU.pow)

                def step(b1, b2, b3):
                    if b3 is not None:
                        pool.wait_ge(v_var1, b3.i + 1)
                        power(r1[:], ve1[:], T).then_inc(g_r1, 1)
                    if b1 is not None:
                        pool.wait_ge(v_var0, b1.i + 1)
                        power(r0[:], ve0[:], T).then_inc(g_r0, 1)
                    if b3 is not None:
                        pool.wait_ge(v_var2, b3.i + 1)
                        power(r2[:].rearrange("p a t -> p (a t)"), ve2[:].rearrange("p a t -> p (a t)"), 2 * T).then_inc(g_r2, 1)
                        y = m.y_f[b3.par][:, 0:SHIFT + QW]
                        high, low = (part[:, bass.ds(b3.i, 1), :].rearrange("p a n -> p (a n)") for part in m.y_all)
                        pool.wait_ge(c_yf, b3.i + 1)
                        nc.gpsimd.tensor_copy(high, y).then_inc(g_high, 1)
                        pool.wait_ge(g_high, b3.i + 1)
                        nc.gpsimd.tensor_tensor(low, y, high, ALU.subtract).then_inc(g_split, 1)

                pipelined(pool, step, B, 3)

            @block.tensor
            def _(pe):
                def step(b1, b2, b3):
                    if b3 is not None:
                        pe.wait_ge(v_pr, b3.i + 1)
                        pe.wait_ge(c_sm, b3.i)
                        for k in range(T):
                            last = pe.transpose(m.bank[7][:, k * P:k * P + P], pr[:, k * P:k * P + P], m.ident[:])
                        last.then_inc(p_pr, 1)
                    if b2 is not None:
                        pe.wait_ge(c_xnf, b2.i + 1)
                        pe.wait_ge(c_th, 3 * b2.i)
                        for k in range(3):
                            pe.matmul(m.bank[1 + k][:], m.w4t[:, k, :], xnf[b2.par][:], start=True, stop=True).then_inc(p_qkv, 1)
                        for k in range(FB):
                            pe.wait_ge(c_h, FB * b2.i + (k - 1) if k else FB * b2.i)
                            pe.matmul(m.bank[4 + k % 2][:], m.s1t[:, k, :], xnf[b2.par][:], start=True, stop=True).then_inc(p_h, 1)
                    if b1 is not None:
                        pe.wait_ge(v_xn, b1.i + 1)
                        pe.wait_ge(c_xnf, b1.i)
                        for k in range(T):
                            last = pe.transpose(m.bank[0][:, k * P:k * P + P], xn[b1.par][:, k, :], m.ident[:])
                        last.then_inc(p_xn, 1)
                    if b2 is not None:
                        pe.wait_ge(v_z, b2.i)
                        for k in range(FB):
                            pe.wait_ge(c_h, FB * b2.i + k + 1)
                            last = pe.matmul(m.bank[6][:], m.s2t[:, k, :], hid[:, k, :], start=(k == 0), stop=(k == FB - 1))
                        last.then_inc(p_f, 1)
                    if b3 is not None:
                        pe.wait_ge(v_y, b3.i + 1)
                        for k in range(T):
                            last = pe.transpose(m.bank[7][:, k * P:k * P + P], yt[:, k, :], m.ident[:])
                        last.then_inc(p_y, 1)
                        y = m.y_f[b3.par]
                        pe.wait_ge(c_yf, b3.i + 1)
                        for k in range(T):
                            pe.matmul(m.bank[7][:, 24 * k:24 * k + 16], y[:, k * P:k * P + P], m.w_sm[:, 0:16], start=True, stop=True)
                            last = pe.matmul(m.bank[7][:, 24 * k + 16:24 * k + 24], y[:, SHIFT + k * P:SHIFT + k * P + P],
                                             m.w_sm[:, 16:24], start=True, stop=True)
                        pe.wait_ge(v_cm, b3.i + 1)
                        pe.matmul(m.bank[7][:, 128:256], m.ones[:], cmw[:].rearrange("p c h -> p (c h)"), start=True, stop=True).then_inc(p_gt, 1)

                pipelined(pe, step, B, 3)

            @block.scalar
            def _(act):
                def step(b1, b2, b3):
                    if b2 is not None:
                        act.wait_ge(v_pr, b2.i)
                        for k in range(3):
                            act.wait_ge(p_qkv, 3 * b2.i + k + 1)
                            if k == 1:
                                nc.scalar.activation(th[1][:], m.bank[2][:], ACT.Tanh, bias=m.cols[:, V_BB:V_BB + 1]).then_inc(c_th, 1)
                            else:
                                nc.scalar.activation(th[k][:], m.bank[1 + k][:], ACT.Tanh, bias=m.half_b[:, k:k + 1], scale=0.5).then_inc(c_th, 1)
                        act.wait_ge(p_f, b2.i)
                        for k in range(FB):
                            act.wait_ge(p_h, FB * b2.i + k + 1)
                            nc.scalar.activation(hid[:, k, :], m.bank[4 + k % 2][:], ACT.Gelu, bias=m.cols[:, V_B1 + k:V_B1 + k + 1],
                                                 scale=m.alpha1[:, k:k + 1]).then_inc(c_h, 1)
                    if b1 is not None:
                        act.wait_ge(p_xn, b1.i + 1)
                        nc.scalar.copy(xnf[b1.par][:], m.bank[0][:]).then_inc(c_xnf, 1)
                    if b2 is not None:
                        act.wait_ge(p_f, b2.i + 1)
                        act.wait_ge(v_z, b2.i)
                        nc.scalar.activation(thg[:], m.bank[6][:], ACT.Tanh, bias=m.half_b[:, 3:4], scale=m.alpha2h[:]).then_inc(c_thg, 1)
                    if b3 is not None:
                        y = m.y_f[b3.par]
                        act.wait_ge(p_y, b3.i + 1)
                        act.wait_ge(g_split, less(b3.i, 1))
                        act.wait_ge(v_cm, b3.i)
                        nc.scalar.copy(y[:, 0:S], m.bank[7][:]).then_inc(c_yf, 1)
                        act.wait_ge(p_gt, b3.i + 1)
                        sm = m.bank[7][:, 0:96].rearrange("p (k j) -> p k j", j=24)
                        nc.scalar.copy(m.aff[:, bass.ts(b3.i, T), :], sm[:, :, 0:8])
                        nc.scalar.activation(m.lr_th[:, bass.ts(b3.i, T), :], sm[:, :, 8:16], ACT.Tanh, scale=0.5)
                        nc.scalar.activation(m.gate_th[:, bass.ts(b3.i, T), :], sm[:, :, 16:24], ACT.Tanh, scale=0.5)
                        nc.scalar.activation(m.md_th[:, bass.ts(b3.i, NC), :], m.bank[7][:, 128:256].rearrange("p (c h) -> p c h", h=2 * H),
                                             ACT.Tanh, scale=0.5).then_inc(c_sm, 1)

                pipelined(act, step, B, 3)

            @block.vector
            def _(dve):
                def stats(link, src, bn_, mv):
                    for k in range(T):
                        last = nc.vector.bn_stats(bn_[:, k, :], src[:, k, :])
                    link(last)
                    dve.sem_inc(v_held, 1)
                    for k in range(T):
                        last = nc.vector.bn_aggr(mv[:, k, :], bn_[:, k, :])
                    link(last)

                def step(b1, b2, b3):
                    if b3 is not None:
                        q = b3.par
                        link = Chain(dve, c3a, 3 * b3.i)
                        dve.wait_ge(p_pr, b3.i + 1)
                        dve.wait_ge(s_keep[q], 48 * b3.half)
                        link(nc.vector.scalar_tensor_tensor(x1[q][:].rearrange("p k d -> p (k d)"), m.bank[7][:], -0.125,
                                                            x0[q][:].rearrange("p k d -> p (k d)"), ALU.mult, ALU.add))
                        stats(link, x1[q], bn1, mv1)
                        nc.vector.tensor_scalar(ve1[:], mv1[:, :, 1], LN_EPS, None, ALU.add).then_inc(v_var1, 1)
                        nc.vector.nop().then_inc(v_x1, 1)
                    if b1 is not None:
                        q = b1.par
                        link = Chain(dve, c1, 2 * b1.i)
                        dve.wait_ge(s_x0[q], 16 * (b1.half + 1))
                        stats(link, x0[q], bn, mv0)
                        nc.vector.tensor_scalar(ve0[:], mv0[:, :, 1], LN_EPS, None, ALU.add).then_inc(v_var0, 1)
                    if b3 is not None:
                        q = b3.par
                        link = Chain(dve, c3b, 4 * b3.i)
                        dve.wait_ge(g_r1, b3.i + 1)
                        for k in range(T):
                            last = nc.vector.tensor_scalar(xn1[q][:, k, :], x1[q][:, k, :], mv1[:, k, 0:1], r1[:, k:k + 1], ALU.subtract, ALU.mult)
                        link(last)
                        stats(link, xn1[q], bn2, mv2)
                        link(nc.vector.tensor_tensor(ve2[:, 0, :], mv2[:, :, 0], mv2[:, :, 0], ALU.mult))
                        nc.vector.scalar_tensor_tensor(ve2[:, 0, :], ve2[:, 0, :], RMS_EPS, mv2[:, :, 1], ALU.add, ALU.add)
                        nc.vector.tensor_scalar(ve2[:, 1, :], mv2[:, :, 1], LN_EPS, None, ALU.add).then_inc(v_var2, 1)
                    if b1 is not None:
                        q = b1.par
                        dve.wait_ge(g_r0, b1.i + 1)
                        dve.wait_ge(p_xn, less(b1.i, 1))
                        for k in range(T):
                            last = nc.vector.tensor_scalar(xn[q][:, k, :], x0[q][:, k, :], mv0[:, k, 0:1], r0[:, k:k + 1], ALU.subtract, ALU.mult)
                        last.then_inc(v_xn, 1)
                    if b2 is not None:
                        link = Chain(dve, c2, b2.i)
                        dve.wait_ge(c_th, 3 * b2.i + 3)
                        nc.vector.tensor_scalar(ga[:], th[0][:], 0.5, 0.5, ALU.mult, ALU.add)
                        link(nc.vector.scalar_tensor_tensor(nb[:], th[0][:], -1.0, th[1][:], ALU.add, ALU.mult))
                        nc.vector.tensor_tensor_scan(st[:], ga[:], nb[:], 0.0, ALU.mult, ALU.add).then_inc(v_rec, 1)
                    if b3 is not None:
                        q = b3.par
                        dve.wait_ge(g_r2, b3.i + 1)
                        dve.wait_ge(p_y, b3.i)
                        nc.vector.tensor_copy(m.ry[:, bass.ts(b3.i, T)], r2[:, 0, :]).then_inc(v_ry, 1)
                        for k in range(T):
                            nc.vector.tensor_scalar(xl[q][:, k, :], xn1[q][:, k, :], mv2[:, k, 0:1], r2[:, 1, k:k + 1], ALU.subtract, ALU.mult)
                            last = nc.vector.tensor_scalar(yt[:, k, :], xn1[q][:, k, :], r2[:, 0, k:k + 1], None, ALU.mult)
                        last.then_inc(v_y, 1)
                    if b2 is not None:
                        link = Chain(dve, c3c, 3 * b2.i)
                        dve.wait_ge(c_thg, b2.i + 1)
                        link(nc.vector.tensor_scalar(z[:], m.bank[6][:], m.alpha2[:], m.cols[:, V_B2:V_B2 + 1], ALU.mult, ALU.add))
                        link(nc.vector.scalar_tensor_tensor(z[:], thg[:], 1.0, z[:], ALU.add, ALU.mult))
                        nc.vector.nop().then_inc(v_z, 1)
                        dve.wait_ge(v_rec, b2.i + 1)
                        link(nc.vector.scalar_tensor_tensor(st[:], th[2][:], 1.0, st[:], ALU.add, ALU.mult))
                        dve.wait_ge(p_pr, b2.i)
                        nc.vector.tensor_tensor(pr[:], st[:], z[:], ALU.mult).then_inc(v_pr, 1)
                    if b3 is not None:
                        y = m.y_f[b3.par]
                        dve.wait_ge(c_yf, b3.i + 1)
                        nc.vector.tensor_reduce(cm[:], y[:, 0:S].rearrange("p (c n) -> p c n", n=C), AX.X, ALU.add).then_inc(v_ry, 1)
                        dve.wait_ge(v_ry, 2 * b3.i + 2)
                        nc.vector.scalar_tensor_tensor(cmw[:], cm[:].unsqueeze(2).broadcast_to([P, NC, 2 * H]), 1.0 / C,
                                                       m.w_md[:].unsqueeze(1).broadcast_to([P, NC, 2 * H]), ALU.mult, ALU.mult).then_inc(v_cm, 1)

                pipelined(dve, step, B, 3)


def routing(nc, m):
    with ExitStack() as ctx:
        sb = lambda n, s, d=F32: ctx.enter_context(nc.sbuf_tensor(n, s, d))
        sem = lambda n: ctx.enter_context(nc.semaphore(n))
        mom = sb("mom", [P, B, H, T])
        upd = sb("upd", [P, B, H, T])
        gates = sb("gates", [P, B * NC, 2 * H])
        lr = sb("lr", [P, NT, H])
        top = sb("top", [P, NT])
        oh = sb("oh", [P, NT, E])
        t1 = sb("t1", [P, NT, E])
        best = sb("best", [P, NT])
        cnt = sb("cnt", [P, E, NT])
        run = sb("run", [P, E, NT])
        nblk = sb("nblk", [P, E])
        nblk_i = sb("nblk_i", [P, E], I32)
        endb = sb("endb", [P, E])
        cmp = sb("cmp", [P, NB, E])
        be = sb("be", [P, NB])
        pos = sb("pos", [P, NT])
        d_c, v_oh, p_cnt, v_z = sem("d_c"), sem("v_oh"), sem("p_cnt"), sem("v_zz")
        a_th = sem("a_th")

        with nc.Block() as block:

            @block.tensor
            def _(pe):
                pe.wait_ge(v_oh, 1)
                flat = oh[:].rearrange("p n e -> p (n e)")
                pe.matmul(m.bank[0][:, 0:NT * E], m.upper[:], flat, start=True, stop=True)
                pe.matmul(m.bank[1][:, 0:NT * E], m.ones[:], flat, start=True, stop=True).then_inc(p_cnt, 1)

            @block.scalar
            def _(act):
                act.wait_ge(v_z, 1)
                nc.scalar.activation(best[:], top[:], ACT.Tanh, scale=0.5).then_inc(a_th, 1)

            @block.vector
            def _(dve):
                link = Chain(dve, d_c)
                bc = lambda ap: ap.unsqueeze(2).broadcast_to([P, NT, E])
                link(nc.vector.tensor_reduce(top[:], m.aff[:], AX.X, ALU.max))
                link(nc.vector.tensor_tensor(oh[:], m.aff[:], bc(top[:]), ALU.is_equal))
                link(nc.vector.tensor_tensor(oh[:], oh[:], m.rank_f[:], ALU.mult))
                link(nc.vector.tensor_reduce(best[:], oh[:], AX.X, ALU.max))
                link(nc.vector.tensor_tensor(oh[:], m.rank_f[:], bc(best[:]), ALU.is_equal))
                nc.vector.nop().then_inc(v_oh, 1)
                link(nc.vector.reciprocal(pos[:], m.ry[:]))
                link(nc.vector.tensor_tensor(top[:], top[:], pos[:], ALU.mult))
                nc.vector.nop().then_inc(v_z, 1)
                dve.wait_ge(p_cnt, 1)
                link(nc.vector.tensor_copy(cnt[:], m.bank[1][:, 0:NT * E].rearrange("p (n e) -> p e n", e=E)))
                link(nc.vector.tensor_tensor_scan(run[:].rearrange("p e n -> p (e n)"), m.restart[:].rearrange("p e n -> p (e n)"),
                                                  cnt[:].rearrange("p e n -> p (e n)"), 0.0, ALU.mult, ALU.add))
                link(nc.vector.tensor_scalar(nblk_i[:], run[:, :, NT - 1], float(P - 1), None, ALU.add))
                link(nc.vector.tensor_scalar(nblk_i[:], nblk_i[:], 7, None, ALU.arith_shift_right))
                link(nc.vector.tensor_copy(nblk[:], nblk_i[:]))
                link(nc.vector.tensor_tensor_scan(endb[:], m.ones[:, 0:E], nblk[:], 0.0, ALU.mult, ALU.add))
                link(nc.vector.tensor_tensor(cmp[:], m.block_f[:], endb[:].unsqueeze(1).broadcast_to([P, NB, E]), ALU.is_ge))
                link(nc.vector.tensor_reduce(be[:], cmp[:], AX.X, ALU.add))
                link(nc.vector.tensor_scalar(m.blk_e[:], be[:], float(E - 1), None, ALU.min))
                link(nc.vector.tensor_tensor(nblk[:], endb[:], nblk[:], ALU.subtract))
                link(nc.vector.tensor_tensor(run[:], run[:], cnt[:], ALU.subtract))
                link(nc.vector.scalar_tensor_tensor(run[:], nblk[:].unsqueeze(2).broadcast_to([P, E, NT]), float(P), run[:], ALU.mult, ALU.add))
                link(nc.vector.tensor_tensor(t1[:], m.bank[0][:, 0:NT * E].rearrange("p (n e) -> p n e", e=E),
                                             run[:].rearrange("p e n -> p n e"), ALU.add))
                link(nc.vector.tensor_tensor(t1[:], t1[:], oh[:], ALU.mult))
                link(nc.vector.tensor_reduce(pos[:], t1[:], AX.X, ALU.add))
                link(nc.vector.tensor_copy(m.place[:], pos[:]))
                dve.wait_ge(a_th, 1)
                link(nc.vector.tensor_scalar(m.alpha_e[:], best[:], 0.5, 0.5, ALU.mult, ALU.add))
                link(nc.vector.tensor_copy(m.xl_all[:, :, D].bitcast(I32), m.token_i[:]))
                link(nc.vector.tensor_scalar(gates[:, :, 0:H], m.md_th[:, :, 0:H], 0.5, 0.5, ALU.mult, ALU.add))
                link(nc.vector.tensor_scalar(gates[:, :, H:], m.md_th[:, :, H:], -0.5, 0.5, ALU.mult, ALU.add))
                link(nc.vector.tensor_scalar(m.gate_th[:], m.gate_th[:], 0.5, 0.5, ALU.mult, ALU.add))
                k = -MAX_LR / D
                link(nc.vector.tensor_scalar(lr[:], m.lr_th[:], k, k, ALU.mult, ALU.add))
                link(nc.vector.memset(mom[:], 0.0))
                link(nc.vector.memset(upd[:], 0.0))
                g4 = gates[:].rearrange("p (b c) h -> p b c h", b=B)
                w4 = m.coef[:].rearrange("p b h (i c) -> p b h i c", i=T)
                for c in range(NC):
                    gm = g4[:, :, c, 0:H].unsqueeze(3).broadcast_to([P, B, H, T])
                    gd = g4[:, :, c, H:].unsqueeze(3).broadcast_to([P, B, H, T])
                    ind = m.starts[:, c, :].unsqueeze(1).broadcast_to([P, B * H, T])
                    m3 = mom[:].rearrange("p b h i -> p (b h) i")
                    link(nc.vector.tensor_tensor(mom[:], mom[:], gm, ALU.mult))
                    link(nc.vector.tensor_tensor(m3, m3, ind, ALU.add))
                    link(nc.vector.tensor_tensor(upd[:], upd[:], gd, ALU.mult))
                    link(nc.vector.tensor_tensor(upd[:], upd[:], mom[:], ALU.add))
                    link(nc.vector.tensor_copy(w4[:, :, :, :, c].rearrange("p b h i -> p (b h) i"), upd[:].rearrange("p b h i -> p (b h) i")))
                for b in range(B):
                    for i in range(T):
                        w = m.coef[:, b, :, i * NC:i * NC + NC]
                        link(nc.vector.tensor_tensor(w, w, lr[:, b * T + i, :].unsqueeze(2).broadcast_to([P, H, NC]), ALU.mult))


def memory_attention(nc, m, a):
    with ExitStack() as ctx:
        sb = lambda n, s, d=F32: ctx.enter_context(nc.sbuf_tensor(n, s, d))
        sem = lambda n: ctx.enter_context(nc.semaphore(n))
        pair = lambda n, s: [sb(f"{n}_{k}", s, F32R) for k in ("high", "low")]
        w1 = pair("w1n", [P, D])
        w1t = pair("w1t", [P, D])
        yb = sb("yb", [P, S - 2 * P])
        yk = pair("yk", [P, 2 * P])
        cf = sb("cf", [P, H, T * NC])
        s_sb = [sb(f"s_sb{k}", [P, S]) for k in range(2)]
        s_2 = [pair(f"s{k}", [P, S]) for k in range(2)]
        th = sb("thu", [P, S])
        q_sb = sb("q_sb", [P, S])
        qa, qa_2 = sb("qa", [P, QW]), pair("qa2", [P, QW])
        err, err_2 = sb("err", [P, S]), pair("err2", [P, S])
        err_t = sb("err_t", [P, T, D])
        du = sb("du", [P, S])
        du_t = sb("du_t", [P, T, D])
        p_sb = sb("p_sb", [P, P_COLS])
        xs, xs_2 = sb("xs", [P, QW]), pair("xs2", [P, QW])
        vals = sb("vals", [P, QW])
        sq = sb("sq", [P, QW])
        sq_rest = sb("sq_rest", [P, QW])
        sq_3 = [sb(f"sq_{k}", [P, QW], BF16) for k in ("high", "mid", "low")]
        ones = sb("ones16", [P, 1], BF16)
        ms = sb("ms", [P, T])
        rs = sb("rs", [P, T])
        rg = sb("rg", [P, T])
        acc = sb("acc", [P, T, D])
        U, QA, EB, XB, VB = m.bank[0], m.bank[1], m.bank[2], m.bank[3], m.bank[7]

        p_u, p_qa, p_e, p_d, p_et, p_dt = (sem(f"p_{k}") for k in ("u", "qa", "e", "d", "et", "dt"))
        p_s0, p_x, p_s1, p_v, p_o = (sem(f"p_{k}") for k in ("s0", "x", "s1", "v", "o"))
        a_s, a_th, a_qa, a_err, a_et, a_xs, a_v, a_sq, a_dt = (sem(f"a_{k}") for k in ("s", "tu", "qa", "err", "et", "xs", "v", "sq", "dt"))
        a_sh, a_qh, a_eh, a_xh, a_hi, a_mid = (sem(f"a_{k}") for k in ("sh", "qh", "eh", "xh", "hi", "mid"))
        v_q, v_g, v_du, v_p0, v_p1, v_ms, v_acc, v_y, v_cf, v_xl, v_el = (
            sem(f"v_{k}") for k in ("q", "g", "du", "p0", "p1", "ms", "acc", "yb", "cf", "xl", "el"))
        g_rs, g_rg, g_sl, g_ql, g_rest, g_lo = (sem(f"g_{k}") for k in ("rs", "rg", "sl", "ql", "rest", "lo"))
        s_out, s_zero, s_ew = sem("s_out"), sem("s_zero"), sem("s_ew")
        a_made, v_made = sem("a_made"), sem("v_made")

        def heads(eng, step):
            step((0, 0), None, None)
            for h in range(H):
                step((0, h + 1) if h + 1 < H else (1, 0), (0, h), (0, h - 1) if h else None)
            with eng.Fori(1, B - 1) as b:
                for h in range(H):
                    step((b, h + 1) if h + 1 < H else (b + 1, 0), (b, h), (b, h - 1) if h else (b - 1, H - 1))
            for h in range(H):
                step((B - 1, h + 1) if h + 1 < H else None, (B - 1, h), (B - 1, h - 1) if h else (B - 2, H - 1))
            step(None, None, (B - 1, H - 1))

        n_of = lambda at: at[0] * H + at[1]
        Q_ROWS = [P] * (T - 1) + [Q_LAST]

        with nc.Block() as block:

            @block.tensor
            def _(pe):
                def product(out, left, right, start=True, stop=True):
                    for j, (u, v) in enumerate(((0, 0), (0, 1), (1, 0))):
                        last = pe.matmul(out, left[u], right[v], start=start and j == 0, stop=stop and j == 2)
                    return last

                def project(out, w, at, first, stop=True):
                    width = S if first == 0 else QW
                    y = [part[:, bass.ds(at[0], 1), first:first + width].rearrange("p a n -> p (a n)") for part in m.y_all]
                    return product(out[:, 0:width], [part[:, at[1], :] for part in w], y, stop=stop)

                def scores(left_2, right_2, left, right, done, tiles=SC_ORDER):
                    for i in tiles:
                        out = m.bank[SC_BANK[i]][:, SC_COL[i]:SC_COL[i] + QW - P * i]
                        if i < 2:
                            last = product(out, [part[:, i * P:i * P + P] for part in left_2], [part[:, P * i:] for part in right_2])
                        else:
                            last = pe.matmul(out, left[:, (i - 2) * P:(i - 1) * P], right[:, P * i:], start=True, stop=True)
                        if i != 1:
                            last.then_inc(done, 1)

                def apply(out, rows, made, n):
                    for i in SC_ORDER:
                        if i != 3:
                            pe.wait_ge(made, SC_BANKS * n + {0: 1, 1: 2, 2: 3}[i])
                        last = pe.matmul(out[:, P * i:QW], rows[:, i, :], p_sb[:, P_COL[i]:P_COL[i] + QW - P * i],
                                         start=False, stop=True, skip_group_check=True)
                    return last

                def step(f, s, z):
                    if f is not None:
                        h, n = f[1], n_of(f)
                        pe.wait_ge(v_du, n)
                        project(U, m.w_u, f, 0).then_inc(p_u, 1)
                        pe.wait_ge(a_dt, n)
                        project(EB, m.w_v, f, 0, stop=False)
                    if s is not None:
                        k = n_of(s)
                        pe.wait_ge(v_xl, k + 1)
                        pe.wait_ge(v_p0, SC_BANKS * (k + 1))
                        scores(s_2[s[1] % 2], xs_2, s_sb[s[1] % 2][:, 2 * P:], xs, p_s1)
                    if f is not None:
                        if isinstance(n, int) and n < 2:
                            pass
                        else:
                            pe.wait_ge(v_acc, n - 1)
                        project(QA, m.w_qk, f, SHIFT).then_inc(p_qa, 1)
                        pe.wait_ge(g_sl, n + 1)
                        product(EB[:], [w[:] for w in w1], [part[:] for part in s_2[h % 2]], start=False).then_inc(p_e, 1)
                    if s is not None:
                        pe.wait_ge(v_ms, k)
                        pe.wait_ge(a_et, k + 1)
                        product(VB[:, 0:QW], [w[:] for w in w1], [part[:] for part in xs_2])
                        apply(VB, err_t, v_p1, k).then_inc(p_v, 1)
                    if f is not None:
                        pe.wait_ge(a_err, n + 1)
                        pe.wait_ge(a_xs, n)
                        for t in range(T):
                            last = pe.transpose(XB[:, t * P:t * P + P], err[:, t * P:t * P + P], m.ident[:])
                        last.then_inc(p_et, 1)
                        pe.wait_ge(v_el, n + 1)
                        pe.wait_ge(v_q, n + 1)
                        product(U[:], [w[:] for w in w1t], [part[:] for part in err_2]).then_inc(p_d, 1)
                        if h == 0:
                            pe.wait_ge(v_y, 3 * (f[0] + 1))
                        pe.wait_ge(g_ql, n + 1)
                        pe.wait_ge(v_p1, SC_BANKS * n)
                        scores(yk, qa_2, yb, qa, p_s0, SC_ORDER[:-1])
                        pe.wait_ge(v_du, n + 1)
                        for t in range(T):
                            last = pe.transpose(EB[:, t * P:t * P + P], du[:, t * P:t * P + P], m.ident[:])
                        last.then_inc(p_dt, 1)
                        scores(yk, qa_2, yb, qa, p_s0, SC_ORDER[-1:])
                        pe.wait_ge(a_et, n + 1)
                        project(XB, m.w_x, f, SHIFT)
                        pe.wait_ge(a_dt, n + 1)
                        apply(XB, du_t, v_p0, n).then_inc(p_x, 1)
                    if s is not None:
                        pe.wait_ge(a_v, k + 1)
                        for t, r in enumerate(Q_ROWS):
                            pe.matmul(QA[0:r, t * P:t * P + P], vals[:, t * P:t * P + r], m.w_out[:, s[1], :], start=True, stop=True)
                        pe.wait_ge(g_lo, k + 1)
                        for t, r in enumerate(Q_ROWS):
                            for j, part in enumerate(sq_3):
                                last = pe.matmul(VB[0:r, t:t + 1], part[:, t * P:t * P + r], ones[:], start=(j == 0), stop=(j == 2))
                        last.then_inc(p_o, 1)

                pe.wait_ge(v_made, 4)
                heads(pe, step)

            @block.scalar
            def _(act):
                def step(f, s, z):
                    if s is not None:
                        k = n_of(s)
                        act.wait_ge(p_x, k + 1)
                        nc.scalar.activation(xs[:], XB[:, 0:QW], ACT.Silu).then_inc(a_xs, 1)
                        act.wait_ge(a_xs, k + 1)
                        nc.scalar.copy(xs_2[0][:], xs[:]).then_inc(a_xh, 1)
                    if f is not None:
                        h, n = f[1], n_of(f)
                        act.wait_ge(p_u, n + 1)
                        nc.scalar.activation(s_sb[h % 2][:], U[:], ACT.Silu).then_inc(a_s, 1)
                        act.wait_ge(a_s, n + 1)
                        nc.scalar.copy(s_2[h % 2][0][:], s_sb[h % 2][:]).then_inc(a_sh, 1)
                        act.wait_ge(v_g, n)
                        nc.scalar.activation(th[:], U[:], ACT.Tanh, scale=0.5).then_inc(a_th, 1)
                        act.wait_ge(p_qa, n + 1)
                        act.wait_ge(p_s0, SC_BANKS * n)
                        nc.scalar.copy(qa[:], QA[:, 0:QW]).then_inc(a_qa, 1)
                        act.wait_ge(a_qa, n + 1)
                        nc.scalar.copy(qa_2[0][:], qa[:]).then_inc(a_qh, 1)
                        act.wait_ge(p_e, n + 1)
                        act.wait_ge(p_d, n)
                        nc.scalar.copy(err[:], EB[:]).then_inc(a_err, 1)
                        act.wait_ge(a_err, n + 1)
                        nc.scalar.copy(err_2[0][:], err[:]).then_inc(a_eh, 1)
                    if s is not None:
                        act.wait_ge(p_v, k + 1)
                        act.wait_ge(p_o, k)
                        nc.scalar.copy(vals[:], VB[:, 0:QW]).then_inc(a_v, 1)
                        act.wait_ge(a_v, k + 1)
                        nc.scalar.activation(sq[:], vals[:], ACT.Square).then_inc(a_sq, 1)
                        act.wait_ge(a_sq, k + 1)
                        nc.scalar.copy(sq_3[0][:], sq[:]).then_inc(a_hi, 1)
                    if f is not None:
                        act.wait_ge(p_et, n + 1)
                        nc.scalar.copy(err_t[:].rearrange("p t d -> p (t d)"), XB[:]).then_inc(a_et, 1)
                        act.wait_ge(p_dt, n + 1)
                        nc.scalar.copy(du_t[:].rearrange("p t d -> p (t d)"), EB[:]).then_inc(a_dt, 1)
                    if s is not None:
                        act.wait_ge(g_rest, k + 1)
                        nc.scalar.copy(sq_3[1][:], sq_rest[:]).then_inc(a_mid, 1)

                nc.scalar.copy(w1[0][:], m.w1n[:]).then_inc(a_made, 1)
                nc.scalar.copy(w1t[0][:], m.w4t[:, 3, :]).then_inc(a_made, 1)
                heads(act, step)

            @block.vector
            def _(dve):
                def weigh(h, made, done, n):
                    for i in SC_ORDER:
                        ch = NC - 2 * i
                        src = m.bank[SC_BANK[i]][:, SC_COL[i]:SC_COL[i] + C * ch].rearrange("p (c n) -> p c n", n=C)
                        dst = p_sb[:, P_COL[i]:P_COL[i] + C * ch].rearrange("p (c n) -> p c n", n=C)
                        w = cf[:, h, i * NC + 2 * i:i * NC + NC].unsqueeze(2).broadcast_to([P, ch, C])
                        if i != 3:
                            dve.wait_ge(made, SC_BANKS * n + {0: 1, 1: 2, 2: 3}[i])
                        last = nc.vector.tensor_tensor(dst, src, w, ALU.mult)
                        if i != 1:
                            last.then_inc(done, 1)

                def step(f, s, z):
                    if z is not None:
                        l = n_of(z)
                        dve.wait_ge(p_o, l + 1)
                        dve.wait_ge(g_rs, l)
                        nc.vector.tensor_scalar(ms[:, 0:T - 1], VB[:, 0:T - 1], 1.0 / D, RMS_EPS, ALU.mult, ALU.add)
                        nc.vector.tensor_scalar(ms[0:Q_LAST, T - 1:T], VB[0:Q_LAST, T - 1:T], 1.0 / D, RMS_EPS, ALU.mult, ALU.add).then_inc(v_ms, 1)
                    if f is not None:
                        h, n = f[1], n_of(f)
                        if h == 0:
                            dve.wait_ge(p_s0, SC_BANKS * H * f[0])
                            high, low = (part[:, bass.ds(f[0], 1), 0:S].rearrange("p a n -> p (a n)") for part in m.y_all)
                            nc.vector.tensor_copy(yk[0][:], high[:, 0:2 * P]).then_inc(v_y, 1)
                            nc.vector.tensor_copy(yk[1][:], low[:, 0:2 * P]).then_inc(v_y, 1)
                            nc.vector.tensor_tensor(yb[:], high[:, 2 * P:], low[:, 2 * P:], ALU.add).then_inc(v_y, 1)
                    if s is not None:
                        k = n_of(s)
                        dve.wait_ge(a_xh, k + 1)
                        nc.vector.tensor_tensor(xs_2[1][:], xs[:], xs_2[0][:], ALU.subtract).then_inc(v_xl, 1)
                    if z is not None:
                        dve.wait_ge(g_rg, l + 1)
                        if z[1] == 0:
                            dve.wait_ge(s_out, 32 * z[0])
                        else:
                            dve.wait_ge(v_acc, l)
                        for t, r in enumerate(Q_ROWS):
                            o, g, sums = QA[0:r, t * P:t * P + P], rg[0:r, t:t + 1], acc[0:r, t, :]
                            if z[1] == 0:
                                last = nc.vector.tensor_scalar(sums, o, g, None, ALU.mult)
                            else:
                                last = nc.vector.scalar_tensor_tensor(sums, o, g, sums, ALU.mult, ALU.add)
                        last.then_inc(v_acc, 1)
                    if s is not None:
                        dve.wait_ge(p_x, k + 1)
                        weigh(s[1], p_s1, v_p1, k)
                    if f is not None:
                        if h == 0:
                            if s is not None:
                                dve.wait_ge(v_p1, SC_BANKS * (k + 1))
                            nc.vector.tensor_copy(cf[:], m.coef[:, bass.ts(f[0], 1), :, :].rearrange("p a h c -> p (a h) c")).then_inc(v_cf, 1)
                        dve.wait_ge(a_th, n + 1)
                        dve.wait_ge(a_s, n + 1)
                        nc.vector.scalar_tensor_tensor(q_sb[:], U[:], 1.0, s_sb[h % 2][:], ALU.add, ALU.subtract).then_inc(v_q, 1)
                        dve.wait_ge(v_q, n + 1)
                        nc.vector.scalar_tensor_tensor(q_sb[:], th[:], 1.0, q_sb[:], ALU.add, ALU.mult).then_inc(v_g, 1)
                        dve.wait_ge(a_eh, n + 1)
                        nc.vector.tensor_tensor(err_2[1][:], err[:], err_2[0][:], ALU.subtract).then_inc(v_el, 1)
                        dve.wait_ge(v_g, n + 1)
                        dve.wait_ge(p_d, n + 1)
                        nc.vector.scalar_tensor_tensor(du[:], q_sb[:], 0.5, U[:], ALU.mult, ALU.mult).then_inc(v_du, 1)
                        if h == 0:
                            dve.wait_ge(v_cf, f[0] + 1)
                        if s is not None:
                            dve.wait_ge(p_v, k + 1)
                        weigh(h, p_s0, v_p0, n)

                nc.vector.memset(ms[:], 1.0).then_inc(v_made, 1)
                nc.vector.memset(ones[:], 1.0).then_inc(v_made, 1)
                dve.wait_ge(a_made, 2)
                nc.vector.tensor_tensor(w1[1][:], m.w1n[:], w1[0][:], ALU.subtract).then_inc(v_made, 1)
                nc.vector.tensor_tensor(w1t[1][:], m.w4t[:, 3, :], w1t[0][:], ALU.subtract).then_inc(v_made, 1)
                dve.wait_ge(v_made, 4)
                heads(dve, step)

            @block.gpsimd
            def _(pool):
                def scatter(t):
                    nc.gpsimd.indirect_dma_start(m.sorted_rows, bass.IndirectOffsetOnAxis(m.place[:, t:t + 1], axis=0),
                                                 m.xl_all[:, t, :], None).then_inc(m.s_scatter, 16)

                def lacks(whole, parts, done):
                    nc.gpsimd.tensor_tensor(parts[1][:], whole[:], parts[0][:], ALU.subtract).then_inc(done, 1)

                def step(f, s, z):
                    if s is not None:
                        k = n_of(s)
                    if z is not None:
                        l = n_of(z)
                        pool.wait_ge(v_ms, l + 1)
                        nc.gpsimd.tensor_tensor(rs[:], ms[:], m.neg_half[:, 0:T], ALU.pow).then_inc(g_rs, 1)
                        pool.wait_ge(g_rs, l + 1)
                        pool.wait_ge(v_acc, l)
                        gate = m.gate_th[:, bass.ts(z[0], T), :][:, :, z[1]]
                        nc.gpsimd.tensor_tensor(rg[:], rs[:], gate, ALU.mult).then_inc(g_rg, 1)
                    if f is not None:
                        h, n = f[1], n_of(f)
                        pool.wait_ge(a_sh, n + 1)
                        lacks(s_sb[h % 2], s_2[h % 2], g_sl)
                        pool.wait_ge(a_qh, n + 1)
                        lacks(qa, qa_2, g_ql)
                    if s is not None:
                        pool.wait_ge(a_hi, k + 1)
                        pool.wait_ge(p_o, k)
                        nc.gpsimd.tensor_tensor(sq_rest[:], sq[:], sq_3[0][:], ALU.subtract).then_inc(g_rest, 1)
                        pool.wait_ge(a_mid, k + 1)
                        pool.wait_ge(g_rest, k + 1)
                        nc.gpsimd.tensor_tensor(sq_3[2][:], sq_rest[:], sq_3[1][:], ALU.subtract).then_inc(g_lo, 1)
                        if isinstance(s[0], int) and s[0] == 0:
                            for t in range(T):
                                scatter(T * s[1] + t)

                heads(pool, step)
                pool.wait_ge(m.s_scatter, 16 * NT)

            @block.sync
            def _(sp):
                rows = m.attn_out.rearrange("(b s) d -> b s d", s=S)
                sp.dma_start(rows[:, 0:SHIFT, :].rearrange("b p d -> p b d"), m.zeros[0:SHIFT].unsqueeze(1).broadcast_to([SHIFT, B, D])).then_inc(s_zero, 16)
                rest = S - SHIFT - (T - 1) * P
                for e in range(E):
                    sp.dma_start(m.ew1[:, e, 0:HF], a["L1_ffn_w1"][e]).then_inc(s_ew, 16)
                sp.dma_start(m.ew2[:], a["L1_ffn_w2"].rearrange("e (k f) d -> f e k d", f=P)).then_inc(s_ew, 16)
                with sp.Fori(0, B) as b:
                    sp.wait_ge(v_acc, (b + 1) * H)
                    sp.dma_start(rows[b, SHIFT:SHIFT + (T - 1) * P, :].rearrange("(t p) d -> p t d", p=P), acc[:, 0:T - 1, :]).then_inc(s_out, 16)
                    sp.dma_start(rows[b, S - rest:S, :], acc[0:rest, T - 1, :]).then_inc(s_out, 16)
                sp.wait_ge(s_out, 32 * B)
                sp.wait_ge(s_zero, 16)
                sp.wait_ge(s_ew, 16 * (E + 1))


def experts(nc, m):
    with ExitStack() as ctx:
        sb = lambda n, s, d=F32: ctx.enter_context(nc.sbuf_tensor(n, s, d))
        sem = lambda n: ctx.enter_context(nc.semaphore(n))
        some = lambda k, n, s, d=F32: [sb(f"{n}{i}", s, d) for i in range(k)]
        w1, w2 = m.ew1, m.ew2
        rows = some(RING, "rows", [P, ROW])
        numbers = sb("numbers", [P, NB], I32)
        w1s = some(RING, "w1s", [P, B2 + D])
        ids = some(RING, "ids", [P, 1], I32)
        xf = some(2, "xf", [P, P])
        hid = some(2, "hidx", [P, FB, P])
        y = some(RING, "yx", [P, D])
        s_rows = [sem(f"s_rows{k}") for k in range(RING)]
        s_y = [sem(f"s_y{k}") for k in range(RING)]
        p_t, p_h, p_y = sem("p_t"), sem("p_hh"), sem("p_yy")
        v_w, v_xf, v_y = sem("v_w"), sem("v_xf"), sem("v_yy")
        a_h = sem("a_h")
        g_held, v_held = sem("g_held"), sem("v_held_x")
        s_last = sem("s_last")

        with nc.Block() as block:

            @block.sync
            def _(sp):
                src = m.sorted_rows.rearrange("(n p) r -> n p r", p=P)
                for r in range(RING):
                    sp.dma_start(rows[r][:], src[r]).then_inc(s_rows[r], 16)
                for kept, rows_of in ((m.xn1_all, m.xn1_rows), (m.at_all, m.attn_out), (m.x1_all, m.x1_rows)):
                    sp.dma_start(kept[:], rows_of.rearrange("(n p) d -> p n d", p=P)).then_inc(s_last, 16)
                with sp.Fori(1, NB // RING) as j:
                    for r in range(RING):
                        sp.wait_ge(p_t, RING * j + r - (RING - 1))
                        sp.wait_ge(v_xf, RING * j + r - (RING - 1))
                        sp.dma_start(rows[r][:], src[RING * j + r]).then_inc(s_rows[r], 16)
                sp.wait_ge(s_last, 48)

            @block.scalar
            def _(act):
                def step(t1, t2, t3, t4):
                    if t2 is not None:
                        r = t2.par
                        act.wait_ge(p_h, t2.i + 1)
                        act.wait_ge(p_y, less(t2.i, 1))
                        for k in range(FB):
                            last = nc.scalar.activation(hid[r % 2][:, k, :], m.bank[2 + r % 2][:, k * P:k * P + P], ACT.Relu,
                                                        bias=w1s[r][:, PAR + 2 + k:PAR + 3 + k])
                        last.then_inc(a_h, 1)

                pipelined(act, step, NB, 4, RING)

            @block.tensor
            def _(pe):
                def step(t1, t2, t3, t4):
                    if t3 is not None:
                        e = pe.value_load(m.blk_e[0:1, bass.ds(t3.i, 1)], min_val=0, max_val=E - 1)
                    if t1 is not None:
                        r = t1.par
                        pe.wait_ge(s_rows[r], 16 * (t1.half + 1))
                        pe.wait_ge(v_xf, less(t1.i, 1))
                        pe.transpose(m.bank[r % 2][:, 0:P], rows[r][:, 0:D], m.ident[:]).then_inc(p_t, 1)
                    if t2 is not None:
                        r = t2.par
                        pe.wait_ge(v_xf, t2.i + 1)
                        pe.wait_ge(a_h, less(t2.i, 1))
                        for k in range(FB):
                            last = pe.matmul(m.bank[2 + r % 2][:, k * P:k * P + P], w1s[r][:, k * P:k * P + P], xf[r % 2][:], start=True, stop=True)
                        last.then_inc(p_h, 1)
                    if t3 is not None:
                        r = t3.par % 2
                        pe.wait_ge(a_h, t3.i + 1)
                        pe.wait_ge(v_y, less(t3.i, 1))
                        for k in range(FB):
                            last = pe.matmul(m.bank[4 + r][:, 0:D], hid[r][:, k, :], w2[:, bass.ds(e, 1), k, :].rearrange("p a d -> p (a d)"),
                                             start=(k == 0), stop=(k == FB - 1))
                        last.then_inc(p_y, 1)

                pipelined(pe, step, NB, 4, RING)

            @block.vector
            def _(dve):
                def step(t1, t2, t3, t4):
                    if t1 is not None:
                        r = t1.par
                        e = dve.value_load(m.blk_e[0:1, bass.ds(t1.i, 1)], min_val=0, max_val=E - 1)
                        dve.wait_ge(v_y, less(t1.i, 3))
                        dve.wait_ge(p_h, less(t1.i, 1))
                        dve.sem_inc(v_held, 1)
                        nc.vector.tensor_copy(w1s[r][:], w1[:, bass.ds(e, 1), :].rearrange("p a d -> p (a d)")).then_inc(v_w, 1)
                        dve.wait_ge(s_rows[r], 16 * (t1.half + 1))
                        dve.sem_inc(v_held, 1)
                        nc.vector.tensor_copy(numbers[:, bass.ds(t1.i, 1)], rows[r][:, D:ROW].bitcast(I32))
                        dve.wait_ge(v_w, t1.i + 1)
                        dve.wait_ge(p_t, t1.i + 1)
                        nc.vector.tensor_scalar(xf[r % 2][:], m.bank[r % 2][:, 0:P], w1s[r][:, PAR:PAR + 1], w1s[r][:, PAR + 1:PAR + 2],
                                                ALU.mult, ALU.add).then_inc(v_xf, 1)
                    if t4 is not None:
                        r = t4.par
                        dve.wait_ge(p_y, t4.i + 1)
                        dve.wait_ge(s_y[r], 16 * t4.half)
                        dve.sem_inc(v_held, 1)
                        nc.vector.tensor_copy(ids[r][:], numbers[:, bass.ds(t4.i, 1)])
                        nc.vector.tensor_tensor(y[r][:], m.bank[4 + r % 2][:, 0:D], w1s[r][:, B2:], ALU.add).then_inc(v_y, 1)

                pipelined(dve, step, NB, 4, RING)

            @block.gpsimd
            def _(pool):
                with pool.Fori(0, NB // RING) as j:
                    for r in range(RING):
                        pool.wait_ge(v_y, RING * j + r + 1)
                        pool.sem_inc(g_held, 1)
                        nc.gpsimd.indirect_dma_start(m.ffn_rows, bass.IndirectOffsetOnAxis(ids[r][:, 0:1], axis=0),
                                                     y[r][:], None).then_inc(s_y[r], 16)
                for r in range(RING):
                    pool.wait_ge(s_y[r], 16 * (NB // RING))


def combine(nc, m, out):
    with ExitStack() as ctx:
        sb = lambda n, s, d=F32: ctx.enter_context(nc.sbuf_tensor(n, s, d))
        sem = lambda n: ctx.enter_context(nc.semaphore(n))
        f = [sb(f"fin_f{k}", [P, T * D]) for k in range(RING)]
        g = [sb(f"fin_g{k}", [P, T * D]) for k in range(2)]
        o = [sb(f"fin_o{k}", [P, T * D]) for k in range(2)]
        s_in = [sem(f"fin_in{k}") for k in range(RING)]
        s_o = [sem(f"fin_out{k}") for k in range(2)]
        v_f, a_g, v_o, v_c = sem("fin_vf"), sem("fin_ag"), sem("fin_vo"), sem("fin_vc")

        with nc.Block() as block:

            @block.sync
            def _(sp):
                rows = m.ffn_rows[0:B * S].rearrange("(b t p) d -> b p t d", t=T, p=P)
                for b in range(B):
                    r = b % RING
                    if b >= RING:
                        sp.wait_ge(a_g, b - RING + 1)
                    sp.dma_start(f[r][:].rearrange("p (t d) -> p t d", d=D), rows[b]).then_inc(s_in[r], 16)

            @block.scalar
            def _(act):
                dst = out.rearrange("b (t p) d -> b p t d", p=P)
                for b in range(B + 1):
                    if b < B:
                        act.wait_ge(v_f, b + 1)
                        if b >= 2:
                            act.wait_ge(v_o, b - 1)
                        nc.scalar.activation(g[b % 2][:], f[b % RING][:], ACT.Silu).then_inc(a_g, 1)
                    if b >= 1:
                        act.wait_ge(v_o, b)
                        act.dma_start(dst[b - 1], o[(b - 1) % 2][:].rearrange("p (t d) -> p t d", d=D)).then_inc(s_o[(b - 1) % 2], 16)
                for q in range(2):
                    act.wait_ge(s_o[q], 16 * B // 2)

            @block.vector
            def _(dve):
                link = Chain(dve, v_c)
                flat = lambda t, b: t[:, b * T:b * T + T, :].rearrange("p t d -> p (t d)")
                for b in range(B + 1):
                    if b < B:
                        r = b % RING
                        dve.wait_ge(s_in[r], 16 * (b // RING + 1))
                        for t in range(T):
                            part = f[r][:, t * D:t * D + D]
                            last = nc.vector.scalar_tensor_tensor(part, part, m.alpha_e[:, b * T + t:b * T + t + 1],
                                                                  m.xn1_all[:, b * T + t, :], ALU.mult, ALU.add)
                        last.then_inc(v_f, 1)
                    if b >= 1:
                        q = (b - 1) % 2
                        dve.wait_ge(a_g, b)
                        if b > 2:
                            dve.wait_ge(s_o[q], 16 * ((b - 1) // 2))
                        link(nc.vector.tensor_tensor(o[q][:], flat(m.at_all, b - 1), g[q][:], ALU.mult))
                        nc.vector.tensor_tensor(o[q][:], o[q][:], flat(m.x1_all, b - 1), ALU.add).then_inc(v_o, 1)


def program(nc, a, out):
    with ExitStack() as ctx:
        sb = lambda n, s, d=F32: ctx.enter_context(nc.sbuf_tensor(n, s, d))
        m = Mem()
        m.bank = [ctx.enter_context(nc.psum_tensor(f"bank{k}", [P, 512], F32)) for k in range(8)]
        m.sorted_rows = nc.dram_tensor("sorted_rows", (NB * P, ROW), F32, kind="Internal").ap()
        m.attn_out = nc.dram_tensor("attn_out", (B * S, D), F32, kind="Internal").ap()
        m.xn1_rows = nc.dram_tensor("xn1_rows", (B * S, D), F32, kind="Internal").ap()
        m.x1_rows = nc.dram_tensor("x1_rows", (B * S, D), F32, kind="Internal").ap()
        m.ffn_rows = nc.dram_tensor("ffn_rows", (B * S + NB * P, D), F32, kind="Internal").ap()
        m.s_scatter = ctx.enter_context(nc.semaphore("s_scatter"))
        m.ident, m.ones, m.upper = sb("ident", [P, P]), sb("ones", [P, P]), sb("upper", [P, P])
        m.neg_half = sb("neg_half", [P, 2 * T])
        m.starts = sb("starts", [P, NC, T])
        m.rank_f = sb("rank_f", [P, NT, E])
        m.block_f = sb("block_f", [P, NB, E])
        m.token_i = sb("token_i", [P, NT], I32)
        m.restart = sb("restart", [P, E, NT])
        m.zeros = sb("zeros", [P, D])
        m.cols = sb("cols", [P, V_ROWS])
        m.w4t = sb("w4t", [P, 4, D])
        m.w1n = sb("w1n", [P, D])
        m.ew1, m.ew2 = sb("ew1", [P, E, B2 + D]), sb("ew2", [P, E, FB, D])
        m.aff, m.lr_th, m.gate_th = (sb(n, [P, NT, E]) for n in ("aff", "lr_th", "gate_th"))
        m.md_th = sb("md_th", [P, B * NC, 2 * H])
        m.ry = sb("ry", [P, NT])
        m.coef = sb("coef", [P, B, H, T * NC])
        m.place = sb("place", [P, NT], U32)
        m.alpha_e = sb("alpha_e", [P, NT])
        m.blk_e = sb("blk_e", [P, NB], I32)
        with ExitStack() as front:
            sb1 = lambda n, s, d=F32: front.enter_context(nc.sbuf_tensor(n, s, d))
            m.w_u, m.w_v, m.w_qk, m.w_x = ([sb1(f"{n}_{k}", [P, H, D], F32R) for k in ("high", "low")]
                                           for n in ("w_u", "w_v", "w_qk", "w_x"))
            m.w_out = sb1("w_out", [P, H, D])
            m.y_all = [sb1(f"y_{k}", [P, B, SHIFT + QW], F32R) for k in ("high", "low")]
            m.xl_all = sb1("xl_all", [P, NT, ROW])
            with ExitStack() as first:
                sb0 = lambda n, s: first.enter_context(nc.sbuf_tensor(n, s, F32))
                m.s1t, m.s2t = sb0("s1t", [P, FB, P]), sb0("s2t", [P, FB, P])
                m.alpha1, m.alpha2, m.alpha2h = sb0("alpha1", [P, FB]), sb0("alpha2", [P, 1]), sb0("alpha2h", [P, 1])
                m.half_b = sb0("half_b", [P, 4])
                m.w_sm, m.w_md = sb0("w_sm", [P, E + 2 * H]), sb0("w_md", [P, 2 * H])
                m.y_f = [sb0(f"y_f{k}", [P, S + SHIFT]) for k in range(2)]
                prepare(nc, m, a)
                layer0(nc, m, a)
            routing(nc, m)
            memory_attention(nc, m, a)
        m.xn1_all, m.at_all, m.x1_all = (sb(n, [P, NT, D]) for n in ("xn1_all", "at_all", "x1_all"))
        experts(nc, m)
        combine(nc, m, out)


_INS = ["L0_attn_inputs", "L0_attn_Wa", "L0_attn_ba", "L0_attn_Wb", "L0_attn_bb", "L0_attn_Wc", "L0_attn_bc",
        "L0_ffn_w1", "L0_ffn_b1", "L0_ffn_w2", "L0_ffn_b2", "L1_attn_store_norm_g", "L1_attn_retrieve_norm_g",
        "L1_attn_w_kv", "L1_attn_w_q", "L1_attn_w_step", "L1_attn_w_mom", "L1_attn_w_decay", "L1_attn_w_gate",
        "L1_attn_w_combine", "L1_attn_mh_gamma", "L1_attn_mem_w0", "L1_attn_mem_w1", "L1_ffn_centroids",
        "L1_ffn_ln_g", "L1_ffn_ln_b", "L1_ffn_w1", "L1_ffn_b1", "L1_ffn_w2", "L1_ffn_b2"]


def kernel(**inputs):
    import numpy as np
    import concourse.bacc as bacc
    from concourse.bass_utils import run_bass_kernel_spmd

    nc = bacc.Bacc("TRN2", target_bir_lowering=False, num_devices=1)
    arrays, args = {}, {}
    for name in _INS:
        x = np.ascontiguousarray(inputs[name])
        arrays[f"in_{name}"] = x
        args[name] = nc.dram_tensor(f"in_{name}", x.shape, mybir.dt.from_np(x.dtype), kind="ExternalInput").ap()
    out = nc.dram_tensor("out", (B, S, D), F32, kind="ExternalOutput").ap()
    program(nc, args, out)
    r = run_bass_kernel_spmd(nc, [arrays], core_ids=[0])
    return r.results[0]["out"]
```

```python
from contextlib import ExitStack

import concourse.bass as bass
from concourse import mybir

F32 = mybir.dt.float32
F32R = mybir.dt.float32r
I32 = mybir.dt.int32
U32 = mybir.dt.uint32
BF16 = mybir.dt.bfloat16
ALU = mybir.AluOpType
ACT = mybir.ActivationFunctionType
AX = mybir.AxisListType

P = 128
B, S, D = 8, 512, 128
T = S // P
NT = B * T
HF = 512
FB = HF // P
H = 8
C = 64
NC = S // C
SHIFT = C - 1
QW = S - SHIFT + 1
Q_LAST = QW - (T - 1) * P
E = 8
NB = NT + E
ROW = D + 1
RING = 4
LN_EPS, RMS_EPS, MAX_LR = 1e-5, 1e-6, 0.01

V_BA, V_BB, V_BC, V_B1, V_B2, V_GS, V_GR, V_GAM = 0, 1, 2, 3, 7, 8, 9, 10
V_CENT, V_LNG, V_LNB, V_EB1 = 18, 26, 34, 42
V_ROWS = V_EB1 + E * FB

SC_BANK = [4, 5, 6, 5]
SC_COL = [0, 0, 0, 384]
P_COL = [0, 512, 1024, 896]
SC_ORDER = [0, 1, 3, 2]
SC_BANKS = 3
P_COLS = sum(S - P * i for i in range(T))


PAR, B2 = HF, HF + 2 + FB


class Chain:

    def __init__(self, eng, sem, base=0):
        self.eng, self.sem, self.base, self.n = eng, sem, base, 0

    def __call__(self, ins):
        self.n += 1
        ins.then_inc(self.sem, 1)
        self.eng.wait_ge(self.sem, self.base + self.n)


class At:

    def __init__(self, half, par, ring=2):
        self.i, self.par, self.half = half * ring + par, par, half


def less(n, k):
    return max(n - k, 0) if isinstance(n, int) else n - k


def pipelined(eng, step, count, depth, ring=2):
    at = lambda i: At(i // ring, i % ring, ring) if 0 <= i < count else None
    first, last = depth + depth % 2, count
    last -= last % ring
    for t in range(first):
        step(*[at(t - k) for k in range(depth)])
    with eng.Fori(0, (last - first) // ring) as j:
        for u in range(ring):
            ats = []
            for k in range(depth):
                c = first + u - k
                ats.append(At(j + c // ring, c % ring, ring))
            step(*ats)
    for t in range(last, count + depth - 1):
        step(*[at(t - k) for k in range(depth)])


class Mem:
    pass


def prepare(nc, m, a):
    with ExitStack() as ctx:
        sb = lambda n, s, d=F32: ctx.enter_context(nc.sbuf_tensor(n, s, d))
        used = []

        def sem(name):
            used.append(nc.alloc_semaphore(name))
            return used[-1]

        vec = sb("vec", [P, D])
        sq4 = sb("sq4", [P, 4, D])
        mem0 = sb("mem0", [P, D])
        l0w1 = sb("l0w1", [P, FB, D])
        l0w2 = sb("l0w2", [P, HF])
        wkv = sb("wkv", [P, 2 * H * D])
        wq = sb("wq", [P, H * D])
        wcomb = sb("wcomb", [P, H, D])
        small = sb("small", [P, 4, H])
        b2row = sb("b2row", [1, E * D])
        sg1 = sb("sg1", [P, FB, D])
        sg2 = sb("sg2", [P, HF])
        kt = sb("kt", [P, H, D])
        qt = sb("qt", [P, H, D])
        gam1 = sb("gam1", [P, H])
        neg_gs = sb("neg_gs", [P, 1])
        fill = sb("fill", [P, NB - NT, ROW])
        rank_i, block_i = sb("rank_i", [P, NT, E], I32), sb("block_i", [P, NB, E], I32)
        names = ["vec", "sq4", "mem0", "l0w1", "l0w2", "wkv", "wq", "wcomb", "small", "b2row"]
        got = {n: sem(f"got_{n}") for n in names}
        filled = sem("filled")
        consts = sem("consts")
        pool_made = []
        fill_ok = sem("fill_ok")
        signs = sem("signs")
        pe_group = sem("pe_group")
        out_group = sem("out_group")
        scaled = sem("scaled")
        dve_c = sem("dve_c0")
        act_c = sem("act_c0")
        a_high, kq_out, a_v = sem("a_high"), sem("kq_out"), sem("a_v0")
        KQ = 4
        SPLIT = 8

        with nc.Block() as block:

            @block.sync
            def _(sp):
                rows = [
                    (V_BA, 1, a["L0_attn_ba"].rearrange("(a n) -> a n", a=1)),
                    (V_BB, 1, a["L0_attn_bb"].rearrange("(a n) -> a n", a=1)),
                    (V_BC, 1, a["L0_attn_bc"].rearrange("(a n) -> a n", a=1)),
                    (V_B1, FB, a["L0_ffn_b1"].rearrange("(a n) -> a n", a=FB)),
                    (V_B2, 1, a["L0_ffn_b2"].rearrange("(a n) -> a n", a=1)),
                    (V_GS, 1, a["L1_attn_store_norm_g"].rearrange("(a n) -> a n", a=1)),
                    (V_GR, 1, a["L1_attn_retrieve_norm_g"].rearrange("(a n) -> a n", a=1)),
                    (V_GAM, H, a["L1_attn_mh_gamma"].rearrange("h a d -> (h a) d")),
                    (V_CENT, E, a["L1_ffn_centroids"]),
                    (V_LNG, E, a["L1_ffn_ln_g"]),
                    (V_LNB, E, a["L1_ffn_ln_b"]),
                    (V_EB1, E * FB, a["L1_ffn_b1"].rearrange("e (k n) -> (e k) n", k=FB)),
                ]
                for r, n, src in rows:
                    sp.dma_start(vec[r:r + n, :], src).then_inc(got["vec"], 16)
                for k, n in enumerate(["L0_attn_Wa", "L0_attn_Wb", "L0_attn_Wc", "L1_attn_mem_w1"]):
                    sp.dma_start(sq4[:, k, :], a[n]).then_inc(got["sq4"], 16)
                for k, n in enumerate(["step", "mom", "decay", "gate"]):
                    sp.dma_start(small[:, k, :], a[f"L1_attn_w_{n}"]).then_inc(got["small"], 16)
                sp.dma_start(wcomb[:], a["L1_attn_w_combine"].rearrange("(h e) d -> e h d", e=D)).then_inc(got["wcomb"], 16)
                sp.dma_start(b2row[:], a["L1_ffn_b2"].rearrange("(a e) d -> a (e d)", a=1)).then_inc(got["b2row"], 16)
                sp.wait_ge(fill_ok, 1)
                blocks = m.sorted_rows.rearrange("(n p) r -> p n r", p=P)
                sp.dma_start(blocks[:, 0:NT, :], m.xl_all[:]).then_inc(filled, 16)
                sp.dma_start(blocks[:, NT:, :], fill[:]).then_inc(filled, 16)
                for b in range(2):
                    sp.dma_start(m.x0[b][:], a["L0_attn_inputs"][b].rearrange("(k p) d -> p k d", p=P)).then_inc(m.s_x0[b], 16)
                sp.wait_ge(filled, 32)

            @block.scalar
            def _(act):
                act.dma_start(l0w1[:], a["L0_ffn_w1"].rearrange("(k p) d -> p k d", p=P)).then_inc(got["l0w1"], 16)
                act.dma_start(l0w2[:], a["L0_ffn_w2"]).then_inc(got["l0w2"], 16)
                act.dma_start(wkv[:], a["L1_attn_w_kv"]).then_inc(got["wkv"], 16)
                act.dma_start(wq[:], a["L1_attn_w_q"]).then_inc(got["wq"], 16)
                act.dma_start(mem0[:], a["L1_attn_mem_w0"]).then_inc(got["mem0"], 16)
                act.dma_start(m.w1n[:], a["L1_attn_mem_w1"]).then_inc(got["mem0"], 16)
                act.wait_ge(got["l0w1"], 16)
                nc.scalar.activation(sg1[:], l0w1[:], ACT.Sign).then_inc(signs, 1)
                act.wait_ge(got["l0w2"], 16)
                nc.scalar.activation(sg2[:], l0w2[:], ACT.Sign).then_inc(signs, 1)
                act.wait_ge(pe_group, 2)
                nc.scalar.copy(m.w4t[0][:], m.bank[1][:].rearrange("p (a b) -> p a b", b=P)).then_inc(a_high, 1)
                for g in range(4):
                    act.wait_ge(pe_group, KQ + g + 1)
                    nc.scalar.copy((kt, qt)[g // 2][:, g % 2 * 4:g % 2 * 4 + 4, :],
                                   m.bank[(KQ + g) % 8][:].rearrange("p (a b) -> p a b", b=P)).then_inc(kq_out, 1)
                flat = lambda w: w[:].rearrange("p h d -> p (h d)")
                act.wait_ge(scaled, 3)
                nc.scalar.mul(wkv[:, H * D:], wkv[:, H * D:], neg_gs[:]).then_inc(a_v, 1)
                act.wait_ge(a_v, 1)
                nc.scalar.copy(flat(m.w_v[0]), wkv[:, H * D:]).then_inc(a_v, 1)
                group = SPLIT
                for w in (m.w_u, m.w_x, m.w_qk):
                    for g in range(2):
                        group += 1
                        act.wait_ge(pe_group, group)
                        nc.scalar.copy(w[0][:, 4 * g:4 * g + 4, :], m.bank[(group - 1) % 8][:].rearrange("p (a b) -> p a b", b=P)).then_inc(a_high, 1)
                chain = Chain(act, act_c)
                for k in range(FB):
                    chain(nc.scalar.activation(l0w1[:, k, :], l0w1[:, k, :], ACT.Abs, accum_out=m.alpha1[:, k:k + 1]))
                chain(nc.scalar.activation(l0w2[:], l0w2[:], ACT.Abs, accum_out=m.alpha2[:]))
                chain(nc.scalar.mul(m.alpha1[:], m.alpha1[:], 1.0 / D))
                chain(nc.scalar.mul(m.alpha2[:], m.alpha2[:], 1.0 / HF))
                chain(nc.scalar.mul(m.alpha2h[:], m.alpha2[:], 0.5))

            @block.gpsimd
            def _(pool):
                chain = Chain(pool, consts)
                chain(nc.gpsimd.memset(m.ident[:], 0.0))
                chain(nc.gpsimd.affine_select(out=m.ident[:], in_=m.ident[:], compare_op=ALU.not_equal, fill=1.0,
                                              base=0, pattern=[[-1, P]], channel_multiplier=1))
                chain(nc.gpsimd.memset(m.ones[:], 1.0))
                chain(nc.gpsimd.memset(m.upper[:], 1.0))
                chain(nc.gpsimd.affine_select(out=m.upper[:], in_=m.upper[:], compare_op=ALU.is_gt, fill=0.0,
                                              base=0, pattern=[[1, P]], channel_multiplier=-1))
                chain(nc.gpsimd.memset(m.neg_half[:], -0.5))
                chain(nc.gpsimd.memset(m.starts[:], 0.0))
                for half in range(2):
                    part = m.starts[C * half:C * half + C]
                    chain(nc.gpsimd.affine_select(out=part, in_=part, compare_op=ALU.not_equal, fill=1.0, base=-half,
                                                  pattern=[[1, NC], [-2, T]], channel_multiplier=0))
                chain(nc.gpsimd.iota(rank_i[:], [[0, NT], [-1, E]], base=E, channel_multiplier=0))
                chain(nc.gpsimd.memset(m.restart[:], 1.0))
                chain(nc.gpsimd.memset(m.restart[:, :, 0:1], 0.0))
                chain(nc.gpsimd.iota(block_i[:], [[1, NB], [0, E]], base=0, channel_multiplier=0))
                chain(nc.gpsimd.iota(m.token_i[:], [[P, NT]], base=0, channel_multiplier=1))
                for rows, n, first in ((m.xl_all, NT, 0), (fill, NB - NT, NT)):
                    chain(nc.gpsimd.memset(rows[:], 0.0))
                    chain(nc.gpsimd.iota(rows[:, :, D].bitcast(I32), [[P, n]], base=B * S + first * P, channel_multiplier=1))
                pool.sem_inc(fill_ok, 1)
                for y in m.y_f:
                    chain(nc.gpsimd.memset(y[:, S:], 0.0))
                pool_made.append(chain.n)

            @block.tensor
            def _(pe):
                pe.wait_ge(consts, 3)
                group = 0

                def bank():
                    nonlocal group
                    if 8 <= group < 8 + KQ:
                        pe.wait_ge(out_group, group - 7)
                    group += 1
                    return m.bank[(group - 1) % 8]

                o = bank()
                pe.wait_ge(got["vec"], 12 * 16)
                pe.transpose(o[:, 0:V_ROWS], vec[0:V_ROWS, :], m.ident[0:V_ROWS, 0:V_ROWS]).then_inc(pe_group, 1)
                o = bank()
                pe.wait_ge(got["sq4"], 64)
                for k in range(4):
                    last = pe.transpose(o[:, k * P:k * P + P], sq4[:, k, :], m.ident[:])
                last.then_inc(pe_group, 1)
                o = bank()
                pe.wait_ge(signs, 1)
                for k in range(FB):
                    last = pe.transpose(o[:, k * P:k * P + P], sg1[:, k, :], m.ident[:])
                last.then_inc(pe_group, 1)
                o = bank()
                pe.wait_ge(signs, 2)
                for k in range(FB):
                    last = pe.transpose(o[:, k * P:k * P + P], sg2[:, k * P:k * P + P], m.ident[:])
                last.then_inc(pe_group, 1)
                for which, src in ((1, wkv), (2, wq)):
                    pe.wait_ge(scaled, which)
                    for g in range(2):
                        o = bank()
                        for k in range(4):
                            h = 4 * g + k
                            last = pe.transpose(o[:, k * P:k * P + P], src[:, h * D:h * D + D], m.ident[:])
                        last.then_inc(pe_group, 1)
                pe.wait_ge(got["mem0"], 32)
                pe.wait_ge(kq_out, 4)
                for left, right in ((kt, None), (qt, None), (qt, kt)):
                    for g in range(2):
                        o = bank()
                        for k in range(4):
                            h = 4 * g + k
                            rhs = mem0[:] if right is None else right[:, h, :]
                            last = pe.matmul(o[:, k * P:k * P + P], left[:, h, :], rhs, start=True, stop=True)
                        last.then_inc(pe_group, 1)
                pe.wait_ge(got["b2row"], 16)
                for g in range(2):
                    o = bank()
                    pe.matmul(o[:], m.ones[0:1, :], b2row[:, g * 512:g * 512 + 512], start=True, stop=True).then_inc(pe_group, 1)

            @block.vector
            def _(dve):
                group = 0
                chain = Chain(dve, dve_c)

                def out(dst):
                    nonlocal group
                    group += 1
                    dve.wait_ge(pe_group, group)
                    n = dst.free_size()
                    nc.vector.tensor_copy(dst, m.bank[(group - 1) % 8][:, 0:n] if len(dst.shape) == 2 else
                                          m.bank[(group - 1) % 8][:, 0:n].rearrange("p (a b) -> p a b", b=P)).then_inc(out_group, 1)

                def out_split(w, n):
                    nonlocal group
                    group += 1
                    src = m.bank[(group - 1) % 8][:].rearrange("p (a b) -> p a b", b=P)
                    dve.wait_ge(a_high, n)
                    nc.vector.tensor_tensor(w[1], src, w[0], ALU.subtract).then_inc(out_group, 1)

                def param(v, n=1):
                    return m.cols[:, v:v + n]

                out(m.cols[:, 0:V_ROWS])
                dve.wait_ge(out_group, 1)
                dve.wait_ge(got["wkv"], 16)
                nc.vector.tensor_scalar(wkv[:, 0:H * D], wkv[:, 0:H * D], param(V_GS), None, ALU.mult).then_inc(scaled, 1)
                dve.wait_ge(got["wq"], 16)
                nc.vector.tensor_scalar(wq[:], wq[:], param(V_GR), None, ALU.mult).then_inc(scaled, 1)
                nc.vector.tensor_scalar(gam1[:], param(V_GAM, H), 1.0, None, ALU.add)
                nc.vector.tensor_scalar(neg_gs[:], param(V_GS), -1.0, None, ALU.mult).then_inc(scaled, 1)
                out_split([w[:] for w in m.w4t], 1)
                out(m.s1t[:])
                out(m.s2t[:])
                group += 4
                chain(nc.vector.tensor_scalar(m.half_b[:, 0:3], param(V_BA, 3), 0.5, None, ALU.mult))
                chain(nc.vector.tensor_scalar(m.half_b[:, 3:4], param(V_B2), 0.5, None, ALU.mult))
                nc.vector.tensor_copy(m.ew1[:, :, PAR:PAR + 1].rearrange("p e a -> p (e a)"), param(V_LNG, E))
                nc.vector.tensor_copy(m.ew1[:, :, PAR + 1:PAR + 2].rearrange("p e a -> p (e a)"), param(V_LNB, E))
                nc.vector.tensor_copy(m.ew1[:, :, PAR + 2:B2], param(V_EB1, E * FB).rearrange("p (e k) -> p e k", k=FB)).then_inc(scaled, 1)
                dve.wait_ge(got["small"], 64)
                nc.vector.tensor_copy(m.w_sm[:, 0:E], param(V_CENT, E)).then_inc(scaled, 1)
                nc.vector.tensor_scalar(m.w_sm[:, E:E + H], small[:, 0, :], param(V_GS), None, ALU.mult).then_inc(scaled, 1)
                nc.vector.tensor_scalar(m.w_sm[:, E + H:E + 2 * H], small[:, 3, :], param(V_GR), None, ALU.mult).then_inc(scaled, 1)
                nc.vector.tensor_scalar(m.w_md[:], small[:, 1:3, :].rearrange("p a h -> p (a h)"), param(V_GS), None, ALU.mult).then_inc(scaled, 1)
                dve.wait_ge(got["wcomb"], 16)
                for h in range(H):
                    nc.vector.tensor_scalar(m.w_out[:, h, :], wcomb[:, h, :], gam1[:, h:h + 1], None, ALU.mult).then_inc(scaled, 1)
                dve.wait_ge(a_v, 2)
                nc.vector.tensor_tensor(m.w_v[1][:].rearrange("p h d -> p (h d)"), wkv[:, H * D:],
                                        m.w_v[0][:].rearrange("p h d -> p (h d)"), ALU.subtract).then_inc(scaled, 1)
                for k, w in enumerate((m.w_u, m.w_x, m.w_qk)):
                    for g in range(2):
                        out_split([part[:, 4 * g:4 * g + 4, :] for part in w], 2 + 2 * k + g)
                for g in range(2):
                    out(m.ew1[:, 4 * g:4 * g + 4, B2:])
                dve.wait_ge(consts, pool_made[0])
                nc.vector.tensor_copy(m.rank_f[:], rank_i[:]).then_inc(scaled, 1)
                nc.vector.tensor_copy(m.block_f[:], block_i[:]).then_inc(scaled, 1)

        nc.clear_and_free_semaphores(used)
        nc.all_engine_barrier()


def layer0(nc, m, a):
    with ExitStack() as ctx:
        sb = lambda n, s, d=F32: ctx.enter_context(nc.sbuf_tensor(n, s, d))
        sem = lambda n: ctx.enter_context(nc.semaphore(n))
        two = lambda n, s, d=F32: [sb(f"{n}{k}", s, d) for k in range(2)]
        xn = sb("xn", [P, T, D])
        xnf = [two(f"xnf{k}_", [P, S], F32R) for k in range(2)]
        th = [sb(f"th{k}", [P, S]) for k in range(3)]
        st = sb("st", [P, S])
        hid = sb("hid", [P, FB, S])
        thg = sb("thg", [P, S])
        z = sb("z", [P, S])
        pr = sb("pr", [P, S])
        x1 = two("x1", [P, T, D])
        xn1 = two("xn1", [P, T, D])
        yt = sb("yt", [P, T, D])
        xl = two("xl", [P, T, D])
        bn = sb("bn", [P, T, 6])
        mv0, mv1, mv2 = (sb(f"mv{k}", [P, T, 2]) for k in range(3))
        nm = sb("nm", [P, T])
        ve0, ve1 = sb("ve0", [P, T]), sb("ve1", [P, T])
        ve2 = sb("ve2", [P, 2, T])
        r0, r1 = sb("r0", [P, T]), sb("r1", [P, T])
        r2 = sb("r2", [P, 2, T])
        cm = sb("cm", [P, NC])
        cmw = sb("cmw", [P, NC, 2 * H])

        x0, s_x0 = m.x0, m.s_x0
        s_x1, s_x1o, s_xn1o, s_xlo = ([sem(f"s_{n}_{k}") for k in range(2)] for n in ("x1", "x1o", "xn1o", "xlo"))
        v_var0, v_var1, v_var2 = sem("v_var0"), sem("v_var1"), sem("v_var2")
        g_r0, g_r1, g_r2, g_xl, g_high, g_split = (sem(f"g_{k}") for k in ("r0", "r1", "r2", "xl", "high", "split"))
        v_nm, c_xn, p_xn, c_xnf, v_xnf = sem("v_nm"), sem("c_xn"), sem("p_xn"), sem("c_xnf"), sem("v_xnf")
        p_qkv, c_th = sem("p_qkv"), sem("c_th")
        p_h, c_h = sem("p_h"), sem("c_h")
        p_f, c_z, c_thg, v_z = sem("p_f"), sem("c_z"), sem("c_thg"), sem("v_z")
        v_th, v_rec, v_pr, p_pr = sem("v_th"), sem("v_rec"), sem("v_pr"), sem("p_pr")
        v_x1, v_xn1 = sem("v_x1"), sem("v_xn1")
        c_yt, p_y, c_yf = sem("c_yt"), sem("p_y"), sem("c_yf")
        v_cm, p_gt, c_sm = sem("v_cm"), sem("p_gt"), sem("c_sm")
        v_held, held, held_sp = sem("v_held"), sem("held"), sem("held_sp")
        c1, c2, c3, c4, c5 = (sem(f"c{k}") for k in range(1, 6))

        with nc.Block() as block:

            @block.sync
            def _(sp):
                rows_of = lambda rows, b: rows.rearrange("(b t p) d -> b p t d", t=T, p=P)[b]
                x0_of = lambda b: a["L0_attn_inputs"][b].rearrange("(k p) d -> p k d", p=P)

                def step(b1, b2, b3, b4, b5):
                    if b1 is not None and not (isinstance(b1.i, int) and b1.i < 2):
                        sp.wait_ge(c_xn, less(b1.i, 1))
                        sp.sem_inc(held_sp, 1)
                        sp.dma_start(x0[b1.par][:], x0_of(b1.i)).then_inc(s_x0[b1.par], 16)
                    if b4 is not None:
                        q = b4.par
                        sp.wait_ge(v_xn1, b4.i + 1)
                        sp.sem_inc(held_sp, 1)
                        sp.dma_start(rows_of(m.xn1_rows, b4.i), xn1[q][:]).then_inc(s_xn1o[q], 16)
                    if b2 is not None:
                        q = b2.par
                        sp.wait_ge(s_x1o[q], 16 * b2.half)
                        sp.sem_inc(held_sp, 1)
                        sp.wait_ge(v_xn1, less(b2.i, 1))
                        sp.sem_inc(held_sp, 1)
                        sp.dma_start(x1[q][:], x0_of(b2.i)).then_inc(s_x1[q], 16)
                    if b5 is not None:
                        q = b5.par
                        sp.wait_ge(g_xl, b5.i + 1)
                        sp.sem_inc(held_sp, 1)
                        sp.dma_start(m.xl_all[:, bass.ts(b5.i, T), 0:D], xl[q][:]).then_inc(s_xlo[q], 16)
                    if b3 is not None:
                        q = b3.par
                        sp.wait_ge(v_x1, b3.i + 1)
                        sp.sem_inc(held_sp, 1)
                        sp.dma_start(rows_of(m.x1_rows, b3.i), x1[q][:]).then_inc(s_x1o[q], 16)

                pipelined(sp, step, B, 5)
                for q in range(2):
                    for kept in (s_x1o, s_xn1o, s_xlo):
                        sp.wait_ge(kept[q], 16 * B // 2)

            @block.gpsimd
            def _(pool):
                def power(dst, src, n):
                    return nc.gpsimd.tensor_tensor(dst, src, m.neg_half[:, 0:n], ALU.pow)

                def step(b1, b2, b3, b4, b5):
                    if b1 is not None:
                        pool.wait_ge(v_var0, b1.i + 1)
                        power(r0[:], ve0[:], T).then_inc(g_r0, 1)
                    if b4 is not None:
                        q = b4.par
                        pool.wait_ge(v_var2, b4.i + 1)
                        pool.wait_ge(c_yt, b4.i)
                        power(r2[:].rearrange("p a t -> p (a t)"), ve2[:].rearrange("p a t -> p (a t)"), 2 * T).then_inc(g_r2, 1)
                        pool.wait_ge(g_r2, b4.i + 1)
                        pool.wait_ge(s_xlo[q], 16 * b4.half)
                        pool.sem_inc(held, 1)
                        for k in range(T):
                            last = nc.gpsimd.tensor_scalar(xl[q][:, k, :], xn1[q][:, k, :], mv2[:, k, 0:1], r2[:, 1, k:k + 1], ALU.subtract, ALU.mult)
                        last.then_inc(g_xl, 1)
                    if b3 is not None:
                        pool.wait_ge(v_var1, b3.i + 1)
                        pool.wait_ge(v_xn1, b3.i)
                        power(r1[:], ve1[:], T).then_inc(g_r1, 1)
                    if b5 is not None:
                        y = m.y_f[b5.par][:, 0:SHIFT + QW]
                        high, low = (part[:, bass.ds(b5.i, 1), :].rearrange("p a n -> p (a n)") for part in m.y_all)
                        pool.wait_ge(c_yf, b5.i + 1)
                        nc.gpsimd.tensor_copy(high, y).then_inc(g_high, 1)
                        pool.wait_ge(g_high, b5.i + 1)
                        nc.gpsimd.tensor_tensor(low, y, high, ALU.subtract).then_inc(g_split, 1)

                pipelined(pool, step, B, 5)

            @block.tensor
            def _(pe):
                def first_product(b, blocks):
                    for k in blocks:
                        pe.wait_ge(c_h, FB * b.i + (k - 1) if k else FB * b.i)
                        for v in range(2):
                            last = pe.matmul(m.bank[4 + k % 2][:], m.s1t[:, k, :], xnf[v][b.par][:], start=(v == 0), stop=(v == 1))
                        last.then_inc(p_h, 1)

                def step(b1, b2, b3, b4, b5):
                    if b3 is not None:
                        pe.wait_ge(c_thg, b3.i)
                        pe.wait_ge(c_h, FB * (b3.i + 1))
                        for k in range(FB):
                            last = pe.matmul(m.bank[6][:], m.s2t[:, k, :], hid[:, k, :], start=(k == 0), stop=(k == FB - 1))
                        last.then_inc(p_f, 1)
                    if b2 is not None:
                        q = b2.par
                        pe.wait_ge(v_xnf, b2.i + 1)
                        pe.wait_ge(c_th, 3 * b2.i)
                        for k in range(3):
                            for j, (u, v) in enumerate(((0, 0), (0, 1), (1, 0))):
                                last = pe.matmul(m.bank[1 + k][:], m.w4t[u][:, k, :], xnf[v][q][:], start=(j == 0), stop=(j == 2))
                            last.then_inc(p_qkv, 1)
                    if b5 is not None:
                        pe.wait_ge(c_yt, b5.i + 1)
                        pe.wait_ge(c_sm, b5.i)
                        for k in range(T):
                            last = pe.transpose(m.bank[7][:, k * P:k * P + P], yt[:, k, :], m.ident[:])
                        last.then_inc(p_y, 1)
                    if b2 is not None:
                        first_product(b2, (0, 1))
                    if b3 is not None:
                        pe.wait_ge(v_pr, b3.i + 1)
                        for k in range(T):
                            last = pe.transpose(m.bank[0][:, k * P:k * P + P], pr[:, k * P:k * P + P], m.ident[:])
                        last.then_inc(p_pr, 1)
                    if b5 is not None:
                        y = m.y_f[b5.par]
                        pe.wait_ge(c_yf, b5.i + 1)
                        for k in range(T):
                            pe.matmul(m.bank[7][:, 24 * k:24 * k + 16], y[:, k * P:k * P + P], m.w_sm[:, 0:16], start=True, stop=True)
                            pe.matmul(m.bank[7][:, 24 * k + 16:24 * k + 24], y[:, SHIFT + k * P:SHIFT + k * P + P],
                                      m.w_sm[:, 16:24], start=True, stop=True)
                    if b2 is not None:
                        first_product(b2, (2, 3))
                    if b1 is not None:
                        pe.wait_ge(c_xn, b1.i + 1)
                        if b3 is not None:
                            pe.wait_ge(v_x1, b3.i + 1)
                        else:
                            pe.wait_ge(v_xnf, b1.i)
                        for k in range(T):
                            last = pe.transpose(m.bank[0][:, k * P:k * P + P], xn[:, k, :], m.ident[:])
                        last.then_inc(p_xn, 1)
                    if b5 is not None:
                        pe.wait_ge(v_cm, b5.i + 1)
                        pe.matmul(m.bank[7][:, 128:256], m.ones[:], cmw[:].rearrange("p c h -> p (c h)"), start=True, stop=True).then_inc(p_gt, 1)

                pipelined(pe, step, B, 5)

            @block.scalar
            def _(act):
                def gelu(b, k):
                    act.wait_ge(p_h, FB * b.i + k + 1)
                    nc.scalar.activation(hid[:, k, :], m.bank[4 + k % 2][:], ACT.Gelu, bias=m.cols[:, V_B1 + k:V_B1 + k + 1],
                                         scale=m.alpha1[:, k:k + 1]).then_inc(c_h, 1)

                def step(b1, b2, b3, b4, b5):
                    if b3 is not None:
                        act.wait_ge(p_f, b3.i + 1)
                        act.wait_ge(v_z, b3.i)
                        nc.scalar.activation(z[:], m.bank[6][:], ACT.Identity, bias=m.cols[:, V_B2:V_B2 + 1], scale=m.alpha2[:])
                        nc.scalar.activation(thg[:], m.bank[6][:], ACT.Tanh, bias=m.half_b[:, 3:4], scale=m.alpha2h[:]).then_inc(c_thg, 1)
                    if b2 is not None:
                        act.wait_ge(v_rec, b2.i)
                        for k in range(3):
                            act.wait_ge(p_qkv, 3 * b2.i + k + 1)
                            if k == 1:
                                nc.scalar.activation(th[1][:], m.bank[2][:], ACT.Tanh, bias=m.cols[:, V_BB:V_BB + 1]).then_inc(c_th, 1)
                            else:
                                nc.scalar.activation(th[k][:], m.bank[1 + k][:], ACT.Tanh, bias=m.half_b[:, k:k + 1], scale=0.5).then_inc(c_th, 1)
                    if b5 is not None:
                        act.wait_ge(p_y, b5.i + 1)
                        act.wait_ge(g_split, b5.i)
                        nc.scalar.copy(m.y_f[b5.par][:, 0:S], m.bank[7][:]).then_inc(c_yf, 1)
                    if b2 is not None:
                        act.wait_ge(p_f, b2.i)
                        gelu(b2, 0)
                        gelu(b2, 1)
                    if b1 is not None:
                        act.wait_ge(s_x0[b1.par], 16 * (b1.half + 1))
                        act.wait_ge(v_nm, b1.i + 1)
                        act.wait_ge(p_xn, b1.i)
                        for k in range(T):
                            last = nc.scalar.activation(xn[:, k, :], x0[b1.par][:, k, :], ACT.Identity, bias=nm[:, k:k + 1], scale=r0[:, k:k + 1])
                        last.then_inc(c_xn, 1)
                    if b2 is not None:
                        gelu(b2, 2)
                        gelu(b2, 3)
                    if b1 is not None:
                        act.wait_ge(p_xn, b1.i + 1)
                        nc.scalar.copy(xnf[0][b1.par][:], m.bank[0][:]).then_inc(c_xnf, 1)
                    if b5 is not None:
                        act.wait_ge(p_gt, b5.i + 1)
                        sm = m.bank[7][:, 0:96].rearrange("p (k j) -> p k j", j=24)
                        nc.scalar.copy(m.aff[:, bass.ts(b5.i, T), :], sm[:, :, 0:8])
                        nc.scalar.activation(m.lr_th[:, bass.ts(b5.i, T), :], sm[:, :, 8:16], ACT.Tanh, scale=0.5)
                        nc.scalar.activation(m.gate_th[:, bass.ts(b5.i, T), :], sm[:, :, 16:24], ACT.Tanh, scale=0.5)
                        nc.scalar.activation(m.md_th[:, bass.ts(b5.i, NC), :], m.bank[7][:, 128:256].rearrange("p (c h) -> p c h", h=2 * H),
                                             ACT.Tanh, scale=0.5).then_inc(c_sm, 1)
                    if b4 is not None:
                        q = b4.par
                        act.wait_ge(g_r2, b4.i + 1)
                        for k in range(T):
                            nc.scalar.mul(yt[:, k, :], xn1[q][:, k, :], r2[:, 0, k:k + 1])
                        nc.scalar.copy(m.ry[:, bass.ts(b4.i, T)], r2[:, 0, :]).then_inc(c_yt, 1)

                pipelined(act, step, B, 5)

            @block.vector
            def _(dve):
                def stats(link, src, mv):
                    for k in range(T):
                        last = nc.vector.bn_stats(bn[:, k, :], src[:, k, :])
                    link(last)
                    dve.sem_inc(v_held, 1)
                    for k in range(T):
                        last = nc.vector.bn_aggr(mv[:, k, :], bn[:, k, :])
                    link(last)

                def step(b1, b2, b3, b4, b5):
                    if b1 is not None:
                        q = b1.par
                        link = Chain(dve, c1, 2 * b1.i)
                        dve.wait_ge(s_x0[q], 16 * (b1.half + 1))
                        stats(link, x0[q], mv0)
                        nc.vector.tensor_scalar(ve0[:], mv0[:, :, 1], LN_EPS, None, ALU.add).then_inc(v_var0, 1)
                    if b4 is not None:
                        q = b4.par
                        link = Chain(dve, c4, 4 * b4.i)
                        dve.wait_ge(g_r1, b4.i + 1)
                        dve.wait_ge(s_xn1o[q], 16 * b4.half)
                        for k in range(T):
                            last = nc.vector.tensor_scalar(xn1[q][:, k, :], x1[q][:, k, :], mv1[:, k, 0:1], r1[:, k:k + 1], ALU.subtract, ALU.mult)
                        link(last)
                        nc.vector.nop().then_inc(v_xn1, 1)
                    if b1 is not None:
                        dve.wait_ge(g_r0, b1.i + 1)
                        nc.vector.scalar_tensor_tensor(nm[:], mv0[:, :, 0], -1.0, r0[:], ALU.mult, ALU.mult).then_inc(v_nm, 1)
                    if b4 is not None:
                        dve.wait_ge(g_xl, b4.i)
                        stats(link, xn1[q], mv2)
                        link(nc.vector.tensor_tensor(ve2[:, 0, :], mv2[:, :, 0], mv2[:, :, 0], ALU.mult))
                        nc.vector.scalar_tensor_tensor(ve2[:, 0, :], ve2[:, 0, :], RMS_EPS, mv2[:, :, 1], ALU.add, ALU.add)
                        nc.vector.tensor_scalar(ve2[:, 1, :], mv2[:, :, 1], LN_EPS, None, ALU.add).then_inc(v_var2, 1)
                    if b3 is not None:
                        q = b3.par
                        dve.wait_ge(c_thg, b3.i + 1)
                        nc.vector.scalar_tensor_tensor(z[:], thg[:], 1.0, z[:], ALU.add, ALU.mult).then_inc(v_z, 1)
                        dve.wait_ge(v_z, b3.i + 1)
                        dve.wait_ge(v_rec, b3.i + 1)
                        dve.wait_ge(p_pr, b3.i)
                        nc.vector.tensor_tensor(pr[:], st[:], z[:], ALU.mult).then_inc(v_pr, 1)
                        link = Chain(dve, c3, 3 * b3.i)
                        dve.wait_ge(p_pr, b3.i + 1)
                        dve.wait_ge(s_x1[q], 16 * (b3.half + 1))
                        x1_flat = x1[q][:].rearrange("p k d -> p (k d)")
                        link(nc.vector.scalar_tensor_tensor(x1_flat, m.bank[0][:], -0.125, x1_flat, ALU.mult, ALU.add))
                        stats(link, x1[q], mv1)
                        nc.vector.tensor_scalar(ve1[:], mv1[:, :, 1], LN_EPS, None, ALU.add).then_inc(v_var1, 1)
                        nc.vector.nop().then_inc(v_x1, 1)
                    if b5 is not None:
                        y = m.y_f[b5.par]
                        link = Chain(dve, c5, b5.i)
                        dve.wait_ge(c_yf, b5.i + 1)
                        link(nc.vector.tensor_reduce(cm[:], y[:, 0:S].rearrange("p (c n) -> p c n", n=C), AX.X, ALU.add))
                        dve.wait_ge(c_sm, b5.i)
                        nc.vector.scalar_tensor_tensor(cmw[:], cm[:].unsqueeze(2).broadcast_to([P, NC, 2 * H]), 1.0 / C,
                                                       m.w_md[:].unsqueeze(1).broadcast_to([P, NC, 2 * H]), ALU.mult, ALU.mult).then_inc(v_cm, 1)
                    if b2 is not None:
                        link = Chain(dve, c2, 3 * b2.i)
                        dve.wait_ge(c_th, 3 * b2.i + 3)
                        link(nc.vector.scalar_tensor_tensor(th[1][:], th[0][:], -1.0, th[1][:], ALU.add, ALU.mult))
                        link(nc.vector.tensor_scalar(th[0][:], th[0][:], 0.5, 0.5, ALU.mult, ALU.add))
                        link(nc.vector.tensor_tensor_scan(st[:], th[0][:], th[1][:], 0.0, ALU.mult, ALU.add))
                        nc.vector.scalar_tensor_tensor(st[:], th[2][:], 1.0, st[:], ALU.add, ALU.mult).then_inc(v_rec, 1)
                    if b1 is not None:
                        q = b1.par
                        dve.wait_ge(c_xnf, b1.i + 1)
                        nc.vector.tensor_tensor(xnf[1][q][:], m.bank[0][:], xnf[0][q][:], ALU.subtract).then_inc(v_xnf, 1)

                pipelined(dve, step, B, 5)


def routing(nc, m):
    with ExitStack() as ctx:
        sb = lambda n, s, d=F32: ctx.enter_context(nc.sbuf_tensor(n, s, d))
        sem = lambda n: ctx.enter_context(nc.semaphore(n))
        start = sb("start", [P, B, H, T * NC])
        mom = sb("mom", [P, B, H, T * NC])
        gates = sb("gates", [P, 2, B * H, NC])
        gates_x = [sb(f"gates_x{g}", [P, B * H, T, NC]) for g in range(2)]
        lr = sb("lr", [P, NT, H])
        top = sb("top", [P, NT])
        oh = sb("oh", [P, NT, E])
        t1 = sb("t1", [P, NT, E])
        best = sb("best", [P, NT])
        cnt = sb("cnt", [P, E, NT])
        run = sb("run", [P, E, NT])
        nblk = sb("nblk", [P, E])
        nblk_i = sb("nblk_i", [P, E], I32)
        endb = sb("endb", [P, E])
        cmp = sb("cmp", [P, NB, E])
        be = sb("be", [P, NB])
        pos = sb("pos", [P, NT])
        d_c, v_oh, p_cnt, v_z = sem("d_c"), sem("v_oh"), sem("p_cnt"), sem("v_zz")
        a_th, v_lr, g_start, a_gates = sem("a_th"), sem("v_lr"), sem("g_start"), sem("a_gates")

        with nc.Block() as block:

            @block.tensor
            def _(pe):
                pe.wait_ge(v_oh, 1)
                flat = oh[:].rearrange("p n e -> p (n e)")
                pe.matmul(m.bank[0][:, 0:NT * E], m.upper[:], flat, start=True, stop=True)
                pe.matmul(m.bank[1][:, 0:NT * E], m.ones[:], flat, start=True, stop=True).then_inc(p_cnt, 1)

            @block.scalar
            def _(act):
                act.wait_ge(v_lr, 1)
                for g in range(2):
                    nc.scalar.copy(gates_x[g][:], gates[:, g].unsqueeze(2).broadcast_to([P, B * H, T, NC])).then_inc(a_gates, 1)
                act.wait_ge(v_z, 1)
                nc.scalar.activation(best[:], top[:], ACT.Tanh, scale=0.5).then_inc(a_th, 1)

            @block.vector
            def _(dve):
                def route(link):
                    bc = lambda ap: ap.unsqueeze(2).broadcast_to([P, NT, E])
                    link(nc.vector.tensor_reduce(top[:], m.aff[:], AX.X, ALU.max))
                    link(nc.vector.tensor_tensor(oh[:], m.aff[:], bc(top[:]), ALU.is_equal))
                    link(nc.vector.tensor_tensor(oh[:], oh[:], m.rank_f[:], ALU.mult))
                    link(nc.vector.tensor_reduce(best[:], oh[:], AX.X, ALU.max))
                    link(nc.vector.tensor_tensor(oh[:], m.rank_f[:], bc(best[:]), ALU.is_equal))
                    nc.vector.nop().then_inc(v_oh, 1)
                    link(nc.vector.reciprocal(pos[:], m.ry[:]))
                    link(nc.vector.tensor_tensor(top[:], top[:], pos[:], ALU.mult))
                    nc.vector.nop().then_inc(v_z, 1)
                    dve.wait_ge(p_cnt, 1)
                    link(nc.vector.tensor_copy(cnt[:], m.bank[1][:, 0:NT * E].rearrange("p (n e) -> p e n", e=E)))
                    link(nc.vector.tensor_tensor_scan(run[:].rearrange("p e n -> p (e n)"), m.restart[:].rearrange("p e n -> p (e n)"),
                                                      cnt[:].rearrange("p e n -> p (e n)"), 0.0, ALU.mult, ALU.add))
                    link(nc.vector.tensor_scalar(nblk_i[:], run[:, :, NT - 1], float(P - 1), None, ALU.add))
                    link(nc.vector.tensor_scalar(nblk_i[:], nblk_i[:], 7, None, ALU.arith_shift_right))
                    link(nc.vector.tensor_copy(nblk[:], nblk_i[:]))
                    link(nc.vector.tensor_tensor_scan(endb[:], m.ones[:, 0:E], nblk[:], 0.0, ALU.mult, ALU.add))
                    link(nc.vector.tensor_tensor(cmp[:], m.block_f[:], endb[:].unsqueeze(1).broadcast_to([P, NB, E]), ALU.is_ge))
                    link(nc.vector.tensor_reduce(be[:], cmp[:], AX.X, ALU.add))
                    link(nc.vector.tensor_scalar(m.blk_e[:], be[:], float(E - 1), None, ALU.min))
                    link(nc.vector.tensor_tensor(nblk[:], endb[:], nblk[:], ALU.subtract))
                    link(nc.vector.tensor_tensor(run[:], run[:], cnt[:], ALU.subtract))
                    link(nc.vector.scalar_tensor_tensor(run[:], nblk[:].unsqueeze(2).broadcast_to([P, E, NT]), float(P), run[:], ALU.mult, ALU.add))
                    link(nc.vector.tensor_tensor(t1[:], m.bank[0][:, 0:NT * E].rearrange("p (n e) -> p n e", e=E),
                                                 run[:].rearrange("p e n -> p n e"), ALU.add))
                    link(nc.vector.tensor_tensor(t1[:], t1[:], oh[:], ALU.mult))
                    link(nc.vector.tensor_reduce(pos[:], t1[:], AX.X, ALU.add))
                    link(nc.vector.tensor_copy(m.place[:], pos[:]))
                    dve.wait_ge(a_th, 1)
                    link(nc.vector.tensor_scalar(m.alpha_e[:], best[:], 0.5, 0.5, ALU.mult, ALU.add))
                    link(nc.vector.tensor_copy(m.xl_all[:, :, D].bitcast(I32), m.token_i[:]))

                link = Chain(dve, d_c)
                for g, sign in ((0, 0.5), (1, -0.5)):
                    link(nc.vector.tensor_scalar(gates[:, g].rearrange("p (b h) c -> p b h c", b=B),
                                                 m.md_th[:, :, g * H:g * H + H].rearrange("p (b c) h -> p b h c", b=B), sign, 0.5, ALU.mult, ALU.add))
                link(nc.vector.memset(gates[:, :, :, 0:1], 0.0))
                link(nc.vector.tensor_scalar(m.gate_th[:], m.gate_th[:], 0.5, 0.5, ALU.mult, ALU.add))
                k = -MAX_LR / D
                link(nc.vector.tensor_scalar(lr[:], m.lr_th[:], k, k, ALU.mult, ALU.add))
                nc.vector.nop().then_inc(v_lr, 1)

                route(link)
                dve.wait_ge(g_start, B)
                flat = lambda t: t[:].rearrange("p b h n -> p (b h n)")
                for g, src, dst in ((0, start, mom), (1, mom, m.coef)):
                    dve.wait_ge(a_gates, g + 1)
                    link(nc.vector.tensor_tensor_scan(flat(dst), gates_x[g][:].rearrange("p a i c -> p (a i c)"), flat(src), 0.0, ALU.mult, ALU.add))

            @block.gpsimd
            def _(pool):
                pool.wait_ge(v_lr, 1)
                for b in range(B):
                    nc.gpsimd.tensor_tensor(start[:, b].rearrange("p h (i c) -> p h i c", c=NC),
                                            lr[:, b * T:b * T + T, :].rearrange("p i h -> p h i").unsqueeze(3).broadcast_to([P, H, T, NC]),
                                            m.starts[:].rearrange("p c i -> p i c").unsqueeze(1).broadcast_to([P, H, T, NC]), ALU.mult).then_inc(g_start, 1)


def memory_attention(nc, m, a):
    with ExitStack() as ctx:
        sb = lambda n, s, d=F32: ctx.enter_context(nc.sbuf_tensor(n, s, d))
        sem = lambda n: ctx.enter_context(nc.semaphore(n))
        pair = lambda n, s: [sb(f"{n}_{k}", s, F32R) for k in ("high", "low")]
        w1 = pair("w1n", [P, D])
        yb = sb("yb", [P, S - 2 * P])
        yk = pair("yk", [P, 2 * P])
        cf = sb("cf", [P, H, T * NC])
        s_sb = [sb(f"s_sb{k}", [P, S]) for k in range(2)]
        s_2 = [pair(f"s{k}", [P, S]) for k in range(2)]
        th = sb("thu", [P, S])
        q_sb = sb("q_sb", [P, S])
        qa, qa_2 = sb("qa", [P, QW]), pair("qa2", [P, QW])
        err, err_2 = sb("err", [P, S]), pair("err2", [P, S])
        err_t = sb("err_t", [P, T, D])
        du = sb("du", [P, S])
        du_t = sb("du_t", [P, T, D])
        p_sb = sb("p_sb", [P, P_COLS])
        xs, xs_2 = sb("xs", [P, QW]), pair("xs2", [P, QW])
        vals = sb("vals", [P, QW])
        sq = sb("sq", [P, QW])
        sq_rest = sb("sq_rest", [P, QW])
        sq_3 = [sb(f"sq_{k}", [P, QW], BF16) for k in ("high", "mid", "low")]
        ones = sb("ones16", [P, 1], BF16)
        zeros = sb("zeros", [P, D])
        ms = sb("ms", [P, T])
        rs = sb("rs", [P, T])
        rg = sb("rg", [P, T])
        acc = sb("acc", [P, T, D])
        U, QA, EB, XB, VB = m.bank[0], m.bank[1], m.bank[2], m.bank[3], m.bank[7]

        p_u, p_qa, p_e, p_d, p_et, p_dt = (sem(f"p_{k}") for k in ("u", "qa", "e", "d", "et", "dt"))
        p_s0, p_x, p_s1, p_v, p_o = (sem(f"p_{k}") for k in ("s0", "x", "s1", "v", "o"))
        a_s, a_th, a_qa, a_err, a_et, a_xs, a_v, a_sq, a_dt = (sem(f"a_{k}") for k in ("s", "tu", "qa", "err", "et", "xs", "v", "sq", "dt"))
        a_sh, a_qh, a_eh, a_xh, a_hi, a_mid = (sem(f"a_{k}") for k in ("sh", "qh", "eh", "xh", "hi", "mid"))
        v_q, v_g, v_du, v_p0, v_p1, v_ms, v_acc, v_y, v_cf, v_xl, v_el = (
            sem(f"v_{k}") for k in ("q", "g", "du", "p0", "p1", "ms", "acc", "yb", "cf", "xl", "el"))
        g_rs, g_rg, g_sl, g_ql, g_rest, g_lo = (sem(f"g_{k}") for k in ("rs", "rg", "sl", "ql", "rest", "lo"))
        s_out, s_zero, s_ew = sem("s_out"), sem("s_zero"), sem("s_ew")
        a_made, v_made, v_zero = sem("a_made"), sem("v_made"), sem("v_zero")

        def heads(eng, step):
            step((0, 0), None, None)
            for h in range(H):
                step((0, h + 1) if h + 1 < H else (1, 0), (0, h), (0, h - 1) if h else None)
            with eng.Fori(1, B - 1) as b:
                for h in range(H):
                    step((b, h + 1) if h + 1 < H else (b + 1, 0), (b, h), (b, h - 1) if h else (b - 1, H - 1))
            for h in range(H):
                step((B - 1, h + 1) if h + 1 < H else None, (B - 1, h), (B - 1, h - 1) if h else (B - 2, H - 1))
            step(None, None, (B - 1, H - 1))

        n_of = lambda at: at[0] * H + at[1]
        Q_ROWS = [P] * (T - 1) + [Q_LAST]

        with nc.Block() as block:

            @block.tensor
            def _(pe):
                def product(out, left, right, start=True, stop=True):
                    for j, (u, v) in enumerate(((0, 0), (0, 1), (1, 0))):
                        last = pe.matmul(out, left[u], right[v], start=start and j == 0, stop=stop and j == 2)
                    return last

                def project(out, w, at, first, stop=True):
                    width = S if first == 0 else QW
                    y = [part[:, bass.ds(at[0], 1), first:first + width].rearrange("p a n -> p (a n)") for part in m.y_all]
                    return product(out[:, 0:width], [part[:, at[1], :] for part in w], y, stop=stop)

                def scores(left_2, right_2, left, right, done, tiles=SC_ORDER):
                    for i in tiles:
                        out = m.bank[SC_BANK[i]][:, SC_COL[i]:SC_COL[i] + QW - P * i]
                        if i < 2:
                            last = product(out, [part[:, i * P:i * P + P] for part in left_2], [part[:, P * i:] for part in right_2])
                        else:
                            last = pe.matmul(out, left[:, (i - 2) * P:(i - 1) * P], right[:, P * i:], start=True, stop=True)
                        if i != 1:
                            last.then_inc(done, 1)

                def apply(out, rows, made, n):
                    for i in SC_ORDER:
                        if i != 3:
                            pe.wait_ge(made, SC_BANKS * n + {0: 1, 1: 2, 2: 3}[i])
                        last = pe.matmul(out[:, P * i:QW], rows[:, i, :], p_sb[:, P_COL[i]:P_COL[i] + QW - P * i],
                                         start=False, stop=True, skip_group_check=True)
                    return last

                def step(f, s, z):
                    if f is not None:
                        h, n = f[1], n_of(f)
                        pe.wait_ge(v_du, n)
                        project(U, m.w_u, f, 0).then_inc(p_u, 1)
                        pe.wait_ge(a_dt, n)
                        project(EB, m.w_v, f, 0, stop=False)
                    if s is not None:
                        k = n_of(s)
                        pe.wait_ge(v_xl, k + 1)
                        pe.wait_ge(v_p0, SC_BANKS * (k + 1))
                        scores(s_2[s[1] % 2], xs_2, s_sb[s[1] % 2][:, 2 * P:], xs, p_s1)
                    if f is not None:
                        if isinstance(n, int) and n < 2:
                            pass
                        else:
                            pe.wait_ge(v_acc, n - 1)
                        project(QA, m.w_qk, f, SHIFT).then_inc(p_qa, 1)
                        pe.wait_ge(g_sl, n + 1)
                        product(EB[:], [w[:] for w in w1], [part[:] for part in s_2[h % 2]], start=False).then_inc(p_e, 1)
                    if s is not None:
                        pe.wait_ge(v_ms, k)
                        pe.wait_ge(a_et, k + 1)
                        product(VB[:, 0:QW], [w[:] for w in w1], [part[:] for part in xs_2])
                        apply(VB, err_t, v_p1, k).then_inc(p_v, 1)
                    if f is not None:
                        pe.wait_ge(a_err, n + 1)
                        pe.wait_ge(a_xs, n)
                        for t in range(T):
                            last = pe.transpose(XB[:, t * P:t * P + P], err[:, t * P:t * P + P], m.ident[:])
                        last.then_inc(p_et, 1)
                        pe.wait_ge(v_el, n + 1)
                        pe.wait_ge(v_q, n + 1)
                        product(U[:], [w[:, 3, :] for w in m.w4t], [part[:] for part in err_2]).then_inc(p_d, 1)
                        if h == 0:
                            pe.wait_ge(v_y, 3 * (f[0] + 1))
                        pe.wait_ge(g_ql, n + 1)
                        pe.wait_ge(v_p1, SC_BANKS * n)
                        scores(yk, qa_2, yb, qa, p_s0, SC_ORDER[:-1])
                        pe.wait_ge(v_du, n + 1)
                        for t in range(T):
                            last = pe.transpose(EB[:, t * P:t * P + P], du[:, t * P:t * P + P], m.ident[:])
                        last.then_inc(p_dt, 1)
                        scores(yk, qa_2, yb, qa, p_s0, SC_ORDER[-1:])
                        pe.wait_ge(a_et, n + 1)
                        project(XB, m.w_x, f, SHIFT)
                        pe.wait_ge(a_dt, n + 1)
                        apply(XB, du_t, v_p0, n).then_inc(p_x, 1)
                    if s is not None:
                        pe.wait_ge(a_v, k + 1)
                        for t, r in enumerate(Q_ROWS):
                            pe.matmul(QA[0:r, t * P:t * P + P], vals[:, t * P:t * P + r], m.w_out[:, s[1], :], start=True, stop=True)
                        pe.wait_ge(g_lo, k + 1)
                        for t, r in enumerate(Q_ROWS):
                            for j, part in enumerate(sq_3):
                                last = pe.matmul(VB[0:r, t:t + 1], part[:, t * P:t * P + r], ones[:], start=(j == 0), stop=(j == 2))
                        last.then_inc(p_o, 1)

                pe.wait_ge(v_made, 3)
                heads(pe, step)

            @block.scalar
            def _(act):
                def step(f, s, z):
                    if s is not None:
                        k = n_of(s)
                        act.wait_ge(p_x, k + 1)
                        nc.scalar.activation(xs[:], XB[:, 0:QW], ACT.Silu).then_inc(a_xs, 1)
                        act.wait_ge(a_xs, k + 1)
                        nc.scalar.copy(xs_2[0][:], xs[:]).then_inc(a_xh, 1)
                    if f is not None:
                        h, n = f[1], n_of(f)
                        act.wait_ge(p_u, n + 1)
                        nc.scalar.activation(s_sb[h % 2][:], U[:], ACT.Silu).then_inc(a_s, 1)
                        act.wait_ge(a_s, n + 1)
                        nc.scalar.copy(s_2[h % 2][0][:], s_sb[h % 2][:]).then_inc(a_sh, 1)
                        act.wait_ge(v_g, n)
                        nc.scalar.activation(th[:], U[:], ACT.Tanh, scale=0.5).then_inc(a_th, 1)
                        act.wait_ge(p_qa, n + 1)
                        act.wait_ge(p_s0, SC_BANKS * n)
                        nc.scalar.copy(qa[:], QA[:, 0:QW]).then_inc(a_qa, 1)
                        act.wait_ge(a_qa, n + 1)
                        nc.scalar.copy(qa_2[0][:], qa[:]).then_inc(a_qh, 1)
                        act.wait_ge(p_e, n + 1)
                        act.wait_ge(p_d, n)
                        nc.scalar.copy(err[:], EB[:]).then_inc(a_err, 1)
                        act.wait_ge(a_err, n + 1)
                        nc.scalar.copy(err_2[0][:], err[:]).then_inc(a_eh, 1)
                    if s is not None:
                        act.wait_ge(p_v, k + 1)
                        act.wait_ge(p_o, k)
                        nc.scalar.copy(vals[:], VB[:, 0:QW]).then_inc(a_v, 1)
                        act.wait_ge(a_v, k + 1)
                        nc.scalar.activation(sq[:], vals[:], ACT.Square).then_inc(a_sq, 1)
                        act.wait_ge(a_sq, k + 1)
                        nc.scalar.copy(sq_3[0][:], sq[:]).then_inc(a_hi, 1)
                    if f is not None:
                        act.wait_ge(p_et, n + 1)
                        nc.scalar.copy(err_t[:].rearrange("p t d -> p (t d)"), XB[:]).then_inc(a_et, 1)
                        act.wait_ge(p_dt, n + 1)
                        nc.scalar.copy(du_t[:].rearrange("p t d -> p (t d)"), EB[:]).then_inc(a_dt, 1)
                    if s is not None:
                        act.wait_ge(g_rest, k + 1)
                        nc.scalar.copy(sq_3[1][:], sq_rest[:]).then_inc(a_mid, 1)

                nc.scalar.copy(w1[0][:], m.w1n[:]).then_inc(a_made, 1)
                heads(act, step)

            @block.vector
            def _(dve):
                def weigh(h, made, done, n):
                    for i in SC_ORDER:
                        ch = NC - 2 * i
                        src = m.bank[SC_BANK[i]][:, SC_COL[i]:SC_COL[i] + C * ch].rearrange("p (c n) -> p c n", n=C)
                        dst = p_sb[:, P_COL[i]:P_COL[i] + C * ch].rearrange("p (c n) -> p c n", n=C)
                        w = cf[:, h, i * NC + 2 * i:i * NC + NC].unsqueeze(2).broadcast_to([P, ch, C])
                        if i != 3:
                            dve.wait_ge(made, SC_BANKS * n + {0: 1, 1: 2, 2: 3}[i])
                        last = nc.vector.tensor_tensor(dst, src, w, ALU.mult)
                        if i != 1:
                            last.then_inc(done, 1)

                def step(f, s, z):
                    if z is not None:
                        l = n_of(z)
                        dve.wait_ge(p_o, l + 1)
                        dve.wait_ge(g_rs, l)
                        nc.vector.tensor_scalar(ms[:, 0:T - 1], VB[:, 0:T - 1], 1.0 / D, RMS_EPS, ALU.mult, ALU.add)
                        nc.vector.tensor_scalar(ms[0:Q_LAST, T - 1:T], VB[0:Q_LAST, T - 1:T], 1.0 / D, RMS_EPS, ALU.mult, ALU.add).then_inc(v_ms, 1)
                    if f is not None:
                        h, n = f[1], n_of(f)
                    if s is not None:
                        k = n_of(s)
                        dve.wait_ge(a_xh, k + 1)
                        nc.vector.tensor_tensor(xs_2[1][:], xs[:], xs_2[0][:], ALU.subtract).then_inc(v_xl, 1)
                    if z is not None:
                        dve.wait_ge(g_rg, l + 1)
                        if z[1] == 0:
                            dve.wait_ge(s_out, 32 * z[0])
                        else:
                            dve.wait_ge(v_acc, l)
                        for t, r in enumerate(Q_ROWS):
                            o, g, sums = QA[0:r, t * P:t * P + P], rg[0:r, t:t + 1], acc[0:r, t, :]
                            if z[1] == 0:
                                last = nc.vector.tensor_scalar(sums, o, g, None, ALU.mult)
                            else:
                                last = nc.vector.scalar_tensor_tensor(sums, o, g, sums, ALU.mult, ALU.add)
                        last.then_inc(v_acc, 1)
                    if s is not None:
                        dve.wait_ge(p_x, k + 1)
                        weigh(s[1], p_s1, v_p1, k)
                    if f is not None:
                        if h == 0:
                            dve.wait_ge(p_s0, SC_BANKS * H * f[0])
                            high, low = (part[:, bass.ds(f[0], 1), 0:S].rearrange("p a n -> p (a n)") for part in m.y_all)
                            nc.vector.tensor_copy(yk[0][:], high[:, 0:2 * P]).then_inc(v_y, 1)
                            nc.vector.tensor_copy(yk[1][:], low[:, 0:2 * P]).then_inc(v_y, 1)
                            nc.vector.tensor_tensor(yb[:], high[:, 2 * P:], low[:, 2 * P:], ALU.add).then_inc(v_y, 1)
                        if h == 0:
                            if s is not None:
                                dve.wait_ge(v_p1, SC_BANKS * (k + 1))
                            nc.vector.tensor_copy(cf[:], m.coef[:, bass.ts(f[0], 1), :, :].rearrange("p a h c -> p (a h) c")).then_inc(v_cf, 1)
                        dve.wait_ge(a_th, n + 1)
                        dve.wait_ge(a_s, n + 1)
                        nc.vector.scalar_tensor_tensor(q_sb[:], U[:], 1.0, s_sb[h % 2][:], ALU.add, ALU.subtract).then_inc(v_q, 1)
                        dve.wait_ge(v_q, n + 1)
                        nc.vector.scalar_tensor_tensor(q_sb[:], th[:], 1.0, q_sb[:], ALU.add, ALU.mult).then_inc(v_g, 1)
                        dve.wait_ge(a_eh, n + 1)
                        nc.vector.tensor_tensor(err_2[1][:], err[:], err_2[0][:], ALU.subtract).then_inc(v_el, 1)
                        dve.wait_ge(v_g, n + 1)
                        dve.wait_ge(p_d, n + 1)
                        nc.vector.scalar_tensor_tensor(du[:], q_sb[:], 0.5, U[:], ALU.mult, ALU.mult).then_inc(v_du, 1)
                        if h == 0:
                            dve.wait_ge(v_cf, f[0] + 1)
                        if s is not None:
                            dve.wait_ge(p_v, k + 1)
                        weigh(h, p_s0, v_p0, n)

                nc.vector.memset(zeros[:], 0.0).then_inc(v_zero, 1)
                nc.vector.memset(ms[:], 1.0).then_inc(v_made, 1)
                nc.vector.memset(ones[:], 1.0).then_inc(v_made, 1)
                dve.wait_ge(a_made, 1)
                nc.vector.tensor_tensor(w1[1][:], m.w1n[:], w1[0][:], ALU.subtract).then_inc(v_made, 1)
                dve.wait_ge(v_made, 3)
                heads(dve, step)

            @block.gpsimd
            def _(pool):
                def scatter(s, part):
                    if s is None or not isinstance(s[0], int) or s[0] > 0:
                        return
                    t = T * s[1] + part
                    nc.gpsimd.indirect_dma_start(m.sorted_rows, bass.IndirectOffsetOnAxis(m.place[:, t:t + 1], axis=0),
                                                 m.xl_all[:, t, :], None).then_inc(m.s_scatter, 16)

                def lacks(whole, parts, done):
                    nc.gpsimd.tensor_tensor(parts[1][:], whole[:], parts[0][:], ALU.subtract).then_inc(done, 1)

                def step(f, s, z):
                    if s is not None:
                        k = n_of(s)
                    if z is not None:
                        l = n_of(z)
                        pool.wait_ge(v_ms, l + 1)
                        nc.gpsimd.tensor_tensor(rs[:], ms[:], m.neg_half[:, 0:T], ALU.pow).then_inc(g_rs, 1)
                        pool.wait_ge(g_rs, l + 1)
                        pool.wait_ge(v_acc, l)
                        gate = m.gate_th[:, bass.ts(z[0], T), :][:, :, z[1]]
                        nc.gpsimd.tensor_tensor(rg[:], rs[:], gate, ALU.mult).then_inc(g_rg, 1)
                    if f is not None:
                        h, n = f[1], n_of(f)
                        pool.wait_ge(a_sh, n + 1)
                        lacks(s_sb[h % 2], s_2[h % 2], g_sl)
                        scatter(s, 0)
                        pool.wait_ge(a_qh, n + 1)
                        lacks(qa, qa_2, g_ql)
                        scatter(s, 1)
                    if s is not None:
                        pool.wait_ge(a_hi, k + 1)
                        pool.wait_ge(p_o, k)
                        nc.gpsimd.tensor_tensor(sq_rest[:], sq[:], sq_3[0][:], ALU.subtract).then_inc(g_rest, 1)
                        scatter(s, 2)
                        pool.wait_ge(a_mid, k + 1)
                        pool.wait_ge(g_rest, k + 1)
                        nc.gpsimd.tensor_tensor(sq_3[2][:], sq_rest[:], sq_3[1][:], ALU.subtract).then_inc(g_lo, 1)
                        scatter(s, 3)

                heads(pool, step)
                pool.wait_ge(m.s_scatter, 16 * NT)

            @block.sync
            def _(sp):
                rows = m.attn_out.rearrange("(b s) d -> b s d", s=S)
                sp.wait_ge(v_zero, 1)
                sp.dma_start(rows[:, 0:SHIFT, :].rearrange("b p d -> p b d"), zeros[0:SHIFT].unsqueeze(1).broadcast_to([SHIFT, B, D])).then_inc(s_zero, 16)
                rest = S - SHIFT - (T - 1) * P
                for e in range(E):
                    sp.dma_start(m.ew1[:, e, 0:HF], a["L1_ffn_w1"][e]).then_inc(s_ew, 16)
                sp.dma_start(m.ew2[:], a["L1_ffn_w2"].rearrange("e (k f) d -> f e k d", f=P)).then_inc(s_ew, 16)
                with sp.Fori(0, B) as b:
                    sp.wait_ge(v_acc, (b + 1) * H)
                    sp.dma_start(rows[b, SHIFT:SHIFT + (T - 1) * P, :].rearrange("(t p) d -> p t d", p=P), acc[:, 0:T - 1, :]).then_inc(s_out, 16)
                    sp.dma_start(rows[b, S - rest:S, :], acc[0:rest, T - 1, :]).then_inc(s_out, 16)
                sp.wait_ge(m.s_scatter, 16 * NT)
                for r in range(RING):
                    sp.dma_start(m.rows[r][:], m.sorted_rows[r * P:r * P + P, :]).then_inc(m.s_rows[r], 16)
                sp.wait_ge(s_out, 32 * B)
                sp.wait_ge(s_zero, 16)
                sp.wait_ge(s_ew, 16 * (E + 1))


def experts(nc, m):
    with ExitStack() as ctx:
        sb = lambda n, s, d=F32: ctx.enter_context(nc.sbuf_tensor(n, s, d))
        sem = lambda n: ctx.enter_context(nc.semaphore(n))
        some = lambda k, n, s, d=F32: [sb(f"{n}{i}", s, d) for i in range(k)]
        w1, w2 = m.ew1, m.ew2
        rows, s_rows = m.rows, m.s_rows
        numbers = sb("numbers", [P, NB], I32)
        w1s = some(RING, "w1s", [P, B2 + D])
        ids = some(RING, "ids", [P, 1], I32)
        xf = some(2, "xf", [P, P])
        hid = some(2, "hidx", [P, FB, P])
        y = some(RING, "yx", [P, D])
        s_y = [sem(f"s_y{k}") for k in range(RING)]
        p_t, p_h, p_y = sem("p_t"), sem("p_hh"), sem("p_yy")
        v_w, v_xf, v_y = sem("v_w"), sem("v_xf"), sem("v_yy")
        a_h = sem("a_h")
        g_held, v_held = sem("g_held"), sem("v_held_x")
        s_last = sem("s_last")

        with nc.Block() as block:

            @block.sync
            def _(sp):
                src = m.sorted_rows.rearrange("(n p) r -> n p r", p=P)
                def load(j):
                    for r in range(RING):
                        sp.wait_ge(p_t, RING * j + r - (RING - 1))
                        sp.wait_ge(v_xf, RING * j + r - (RING - 1))
                        sp.dma_start(rows[r][:], src[RING * j + r]).then_inc(s_rows[r], 16)

                with sp.Fori(1, B + 1) as j:
                    load(j)
                    for kept, rows_of in ((m.xn1_all, m.xn1_rows), (m.at_all, m.attn_out), (m.x1_all, m.x1_rows)):
                        sp.dma_start(kept[:, bass.ts(j - 1, T), :], rows_of.rearrange("(b t p) d -> b p t d", t=T, p=P)[j - 1]).then_inc(s_last, 16)
                for j in range(B + 1, NB // RING):
                    load(j)
                sp.wait_ge(s_last, 3 * 16 * B)

            @block.scalar
            def _(act):
                def step(t1, t2, t3, t4):
                    if t2 is not None:
                        r = t2.par
                        act.wait_ge(p_h, t2.i + 1)
                        act.wait_ge(p_y, less(t2.i, 1))
                        for k in range(FB):
                            last = nc.scalar.activation(hid[r % 2][:, k, :], m.bank[2 + r % 2][:, k * P:k * P + P], ACT.Relu,
                                                        bias=w1s[r][:, PAR + 2 + k:PAR + 3 + k])
                        last.then_inc(a_h, 1)

                pipelined(act, step, NB, 4, RING)

            @block.tensor
            def _(pe):
                def step(t1, t2, t3, t4):
                    if t3 is not None:
                        e = pe.value_load(m.blk_e[0:1, bass.ds(t3.i, 1)], min_val=0, max_val=E - 1)
                    if t1 is not None:
                        r = t1.par
                        pe.wait_ge(s_rows[r], 16 * (t1.half + 1))
                        pe.wait_ge(v_xf, less(t1.i, 1))
                        pe.transpose(m.bank[r % 2][:, 0:P], rows[r][:, 0:D], m.ident[:]).then_inc(p_t, 1)
                    if t2 is not None:
                        r = t2.par
                        pe.wait_ge(v_xf, t2.i + 1)
                        pe.wait_ge(a_h, less(t2.i, 1))
                        for k in range(FB):
                            last = pe.matmul(m.bank[2 + r % 2][:, k * P:k * P + P], w1s[r][:, k * P:k * P + P], xf[r % 2][:], start=True, stop=True)
                        last.then_inc(p_h, 1)
                    if t3 is not None:
                        r = t3.par % 2
                        pe.wait_ge(a_h, t3.i + 1)
                        pe.wait_ge(v_y, less(t3.i, 1))
                        for k in range(FB):
                            last = pe.matmul(m.bank[4 + r][:, 0:D], hid[r][:, k, :], w2[:, bass.ds(e, 1), k, :].rearrange("p a d -> p (a d)"),
                                             start=(k == 0), stop=(k == FB - 1))
                        last.then_inc(p_y, 1)

                pipelined(pe, step, NB, 4, RING)

            @block.vector
            def _(dve):
                def step(t1, t2, t3, t4):
                    if t1 is not None:
                        r = t1.par
                        e = dve.value_load(m.blk_e[0:1, bass.ds(t1.i, 1)], min_val=0, max_val=E - 1)
                        dve.wait_ge(v_y, less(t1.i, 3))
                        dve.wait_ge(p_h, less(t1.i, 1))
                        dve.sem_inc(v_held, 1)
                        nc.vector.tensor_copy(w1s[r][:], w1[:, bass.ds(e, 1), :].rearrange("p a d -> p (a d)")).then_inc(v_w, 1)
                        dve.wait_ge(s_rows[r], 16 * (t1.half + 1))
                        dve.sem_inc(v_held, 1)
                        nc.vector.tensor_copy(numbers[:, bass.ds(t1.i, 1)], rows[r][:, D:ROW].bitcast(I32))
                        dve.wait_ge(v_w, t1.i + 1)
                        dve.wait_ge(p_t, t1.i + 1)
                        nc.vector.tensor_scalar(xf[r % 2][:], m.bank[r % 2][:, 0:P], w1s[r][:, PAR:PAR + 1], w1s[r][:, PAR + 1:PAR + 2],
                                                ALU.mult, ALU.add).then_inc(v_xf, 1)
                    if t4 is not None:
                        r = t4.par
                        dve.wait_ge(p_y, t4.i + 1)
                        dve.wait_ge(s_y[r], 16 * t4.half)
                        dve.sem_inc(v_held, 1)
                        nc.vector.tensor_copy(ids[r][:], numbers[:, bass.ds(t4.i, 1)])
                        nc.vector.tensor_tensor(y[r][:], m.bank[4 + r % 2][:, 0:D], w1s[r][:, B2:], ALU.add).then_inc(v_y, 1)

                pipelined(dve, step, NB, 4, RING)

            @block.gpsimd
            def _(pool):
                with pool.Fori(0, NB // RING) as j:
                    for r in range(RING):
                        pool.wait_ge(v_y, RING * j + r + 1)
                        pool.sem_inc(g_held, 1)
                        nc.gpsimd.indirect_dma_start(m.ffn_rows, bass.IndirectOffsetOnAxis(ids[r][:, 0:1], axis=0),
                                                     y[r][:], None).then_inc(s_y[r], 16)
                for r in range(RING):
                    pool.wait_ge(s_y[r], 16 * (NB // RING))


def combine(nc, m, out):
    with ExitStack() as ctx:
        sb = lambda n, s, d=F32: ctx.enter_context(nc.sbuf_tensor(n, s, d))
        sem = lambda n: ctx.enter_context(nc.semaphore(n))
        f = [sb(f"fin_f{k}", [P, T * D]) for k in range(B)]
        g = [sb(f"fin_g{k}", [P, T * D]) for k in range(RING)]
        o = [sb(f"fin_o{k}", [P, T * D]) for k in range(RING)]
        s_in = [sem(f"fin_in{k}") for k in range(B)]
        s_o = [sem(f"fin_out{k}") for k in range(RING)]
        v_f, a_g, v_o, g_prod = sem("fin_vf"), sem("fin_ag"), sem("fin_vo"), sem("fin_gp")
        flat = lambda t, b: t[:, b * T:b * T + T, :].rearrange("p t d -> p (t d)")

        with nc.Block() as block:

            @block.sync
            def _(sp):
                rows = m.ffn_rows[0:B * S].rearrange("(b t p) d -> b p t d", t=T, p=P)
                for b in range(B):
                    sp.dma_start(f[b][:].rearrange("p (t d) -> p t d", d=D), rows[b]).then_inc(s_in[b], 16)

            @block.scalar
            def _(act):
                dst = out.rearrange("b (t p) d -> b p t d", p=P)
                for b in range(B + 1):
                    if b < B:
                        act.wait_ge(v_f, b + 1)
                        if b >= RING:
                            act.wait_ge(g_prod, b - RING + 1)
                        nc.scalar.activation(g[b % RING][:], f[b][:], ACT.Silu).then_inc(a_g, 1)
                    if b >= 1:
                        act.wait_ge(v_o, b)
                        act.dma_start(dst[b - 1], o[(b - 1) % RING][:].rearrange("p (t d) -> p t d", d=D)).then_inc(s_o[(b - 1) % RING], 16)
                for q in range(RING):
                    act.wait_ge(s_o[q], 16 * B // RING)

            @block.vector
            def _(dve):
                for b in range(B + 1):
                    if b < B:
                        dve.wait_ge(s_in[b], 16)
                        for t in range(T):
                            part = f[b][:, t * D:t * D + D]
                            last = nc.vector.scalar_tensor_tensor(part, part, m.alpha_e[:, b * T + t:b * T + t + 1],
                                                                  m.xn1_all[:, b * T + t, :], ALU.mult, ALU.add)
                        last.then_inc(v_f, 1)
                    if b >= 1:
                        q = (b - 1) % RING
                        dve.wait_ge(g_prod, b)
                        nc.vector.tensor_tensor(o[q][:], o[q][:], flat(m.x1_all, b - 1), ALU.add).then_inc(v_o, 1)

            @block.gpsimd
            def _(pool):
                for b in range(B):
                    q = b % RING
                    pool.wait_ge(a_g, b + 1)
                    if b >= RING:
                        pool.wait_ge(s_o[q], 16 * (b // RING))
                    nc.gpsimd.tensor_tensor(o[q][:], flat(m.at_all, b), g[q][:], ALU.mult).then_inc(g_prod, 1)


def program(nc, a, out):
    with ExitStack() as ctx:
        sb = lambda n, s, d=F32: ctx.enter_context(nc.sbuf_tensor(n, s, d))
        m = Mem()
        m.bank = [ctx.enter_context(nc.psum_tensor(f"bank{k}", [P, 512], F32)) for k in range(8)]
        m.sorted_rows = nc.dram_tensor("sorted_rows", (NB * P, ROW), F32, kind="Internal").ap()
        m.attn_out = nc.dram_tensor("attn_out", (B * S, D), F32, kind="Internal").ap()
        m.xn1_rows = nc.dram_tensor("xn1_rows", (B * S, D), F32, kind="Internal").ap()
        m.x1_rows = nc.dram_tensor("x1_rows", (B * S, D), F32, kind="Internal").ap()
        m.ffn_rows = nc.dram_tensor("ffn_rows", (B * S + NB * P, D), F32, kind="Internal").ap()
        m.s_scatter = ctx.enter_context(nc.semaphore("s_scatter"))
        m.s_rows = [ctx.enter_context(nc.semaphore(f"s_rows{k}")) for k in range(RING)]
        m.s_x0 = [ctx.enter_context(nc.semaphore(f"s_x0_{k}")) for k in range(2)]
        m.ident, m.ones, m.upper = sb("ident", [P, P]), sb("ones", [P, P]), sb("upper", [P, P])
        m.neg_half = sb("neg_half", [P, 2 * T])
        m.starts = sb("starts", [P, NC, T])
        m.rank_f = sb("rank_f", [P, NT, E])
        m.block_f = sb("block_f", [P, NB, E])
        m.token_i = sb("token_i", [P, NT], I32)
        m.restart = sb("restart", [P, E, NT])
        m.rows = [sb(f"rows{k}", [P, ROW]) for k in range(RING)]
        m.cols = sb("cols", [P, V_ROWS])
        m.w4t = [sb(f"w4t_{k}", [P, 4, D], F32R) for k in ("high", "low")]
        m.w1n = sb("w1n", [P, D])
        m.ew1, m.ew2 = sb("ew1", [P, E, B2 + D]), sb("ew2", [P, E, FB, D])
        m.aff, m.lr_th, m.gate_th = (sb(n, [P, NT, E]) for n in ("aff", "lr_th", "gate_th"))
        m.md_th = sb("md_th", [P, B * NC, 2 * H])
        m.ry = sb("ry", [P, NT])
        m.coef = sb("coef", [P, B, H, T * NC])
        m.place = sb("place", [P, NT], U32)
        m.alpha_e = sb("alpha_e", [P, NT])
        m.blk_e = sb("blk_e", [P, NB], I32)
        with ExitStack() as front:
            sb1 = lambda n, s, d=F32: front.enter_context(nc.sbuf_tensor(n, s, d))
            m.w_u, m.w_v, m.w_qk, m.w_x = ([sb1(f"{n}_{k}", [P, H, D], F32R) for k in ("high", "low")]
                                           for n in ("w_u", "w_v", "w_qk", "w_x"))
            m.w_out = sb1("w_out", [P, H, D])
            m.y_all = [sb1(f"y_{k}", [P, B, SHIFT + QW], F32R) for k in ("high", "low")]
            m.xl_all = sb1("xl_all", [P, NT, ROW])
            with ExitStack() as first:
                sb0 = lambda n, s, d=F32: first.enter_context(nc.sbuf_tensor(n, s, d))
                m.s1t, m.s2t = sb0("s1t", [P, FB, P], F32R), sb0("s2t", [P, FB, P])
                m.alpha1, m.alpha2, m.alpha2h = sb0("alpha1", [P, FB]), sb0("alpha2", [P, 1]), sb0("alpha2h", [P, 1])
                m.half_b = sb0("half_b", [P, 4])
                m.w_sm, m.w_md = sb0("w_sm", [P, E + 2 * H]), sb0("w_md", [P, 2 * H])
                m.x0 = [sb0(f"x0{k}", [P, T, D]) for k in range(2)]
                m.y_f = [sb0(f"y_f{k}", [P, S + SHIFT]) for k in range(2)]
                prepare(nc, m, a)
                layer0(nc, m, a)
            routing(nc, m)
            memory_attention(nc, m, a)
        m.xn1_all, m.at_all, m.x1_all = (sb(n, [P, NT, D]) for n in ("xn1_all", "at_all", "x1_all"))
        experts(nc, m)
        combine(nc, m, out)


_INS = ["L0_attn_inputs", "L0_attn_Wa", "L0_attn_ba", "L0_attn_Wb", "L0_attn_bb", "L0_attn_Wc", "L0_attn_bc",
        "L0_ffn_w1", "L0_ffn_b1", "L0_ffn_w2", "L0_ffn_b2", "L1_attn_store_norm_g", "L1_attn_retrieve_norm_g",
        "L1_attn_w_kv", "L1_attn_w_q", "L1_attn_w_step", "L1_attn_w_mom", "L1_attn_w_decay", "L1_attn_w_gate",
        "L1_attn_w_combine", "L1_attn_mh_gamma", "L1_attn_mem_w0", "L1_attn_mem_w1", "L1_ffn_centroids",
        "L1_ffn_ln_g", "L1_ffn_ln_b", "L1_ffn_w1", "L1_ffn_b1", "L1_ffn_w2", "L1_ffn_b2"]


def kernel(**inputs):
    import numpy as np
    import concourse.bacc as bacc
    from concourse.bass_utils import run_bass_kernel_spmd

    nc = bacc.Bacc("TRN2", target_bir_lowering=False, num_devices=1)
    arrays, args = {}, {}
    for name in _INS:
        x = np.ascontiguousarray(inputs[name])
        arrays[f"in_{name}"] = x
        args[name] = nc.dram_tensor(f"in_{name}", x.shape, mybir.dt.from_np(x.dtype), kind="ExternalInput").ap()
    out = nc.dram_tensor("out", (B, S, D), F32, kind="ExternalOutput").ap()
    program(nc, args, out)
    r = run_bass_kernel_spmd(nc, [arrays], core_ids=[0])
    return r.results[0]["out"]
```
